# Optimizing a Trainium2 kernel written in Bass

```python
import numpy as np
import jax
import jax.numpy as jnp

def _softmax(x, axis=-1):
    return jax.nn.softmax(x, axis=axis)

def _gelu(x):
    return jax.nn.gelu(x, approximate=True)

def _silu(x):
    return jax.nn.silu(x)

def _sigmoid(x):
    return jax.nn.sigmoid(x)

def _layernorm(x, axis=-1, eps=1e-05):
    m = jnp.mean(x, axis=axis, keepdims=True)
    v = jnp.var(x, axis=axis, keepdims=True)
    return (x - m) / jnp.sqrt(v + eps)

def _scatter_add(tgt, idx, src, axis=0):
    return tgt.at[idx].add(src)

def _segment_sum(src, seg, n):
    return jax.ops.segment_sum(src, seg, n)
kernel_name = 'mk_gnn_ffn_d1_gnn_r8_7c9049'

def setup_inputs(seed: int=0):
    np.random.seed(seed)
    _w = jnp.asarray

    def _rec_inputs():
        import jax
        import jax.numpy as jnp
        _gk = jax.random.key(seed)
        x = -8.776e-05 + 1 * jax.random.normal(jax.random.fold_in(_gk, 1), (1250, 512), jnp.float32)
        src = jax.random.randint(jax.random.fold_in(_gk, 2), (20000,), 0, 1250, jnp.int32)
        dst = jnp.minimum((1250 * jax.random.uniform(jax.random.fold_in(_gk, 3), (20000,)) ** 2.0).astype(jnp.int32), 9999)
        _o = jnp.argsort(dst, stable=True)
        src = src[_o]
        dst = dst[_o]
        return (x, src, dst)
    x, src, dst = _rec_inputs()

    def _L0_gnn_setup():
        import jax, jax.numpy as jnp
        import numpy as np
        N_NODES = 1250
        N_EDGES = 20000
        IN_DIM = 512
        OUT_DIM = 512
        LN_EPS = 1e-05
        key = jax.random.key(seed)
        k_x, k_src, k_ws, k_wn = jax.random.split(key, 4)
        x = jax.random.normal(k_x, (N_NODES, IN_DIM), dtype=jnp.float32)
        edge_src = jax.random.randint(k_src, (N_EDGES,), 0, N_NODES, dtype=jnp.int32)
        edge_dst = jnp.repeat(jnp.arange(N_NODES, dtype=jnp.int32), N_EDGES // N_NODES)
        deg = jnp.full((N_NODES,), float(N_EDGES // N_NODES), dtype=jnp.float32)
        scale = 1.0 / np.sqrt(IN_DIM)
        W_self = jax.random.normal(k_ws, (OUT_DIM, IN_DIM), dtype=jnp.float32) * scale
        W_neigh = jax.random.normal(k_wn, (OUT_DIM, IN_DIM), dtype=jnp.float32) * scale
        bias = jnp.zeros((OUT_DIM,), dtype=jnp.float32)
        gamma = jnp.ones((OUT_DIM,), dtype=jnp.float32)
        beta = jnp.zeros((OUT_DIM,), dtype=jnp.float32)
        return {'x': x, 'edge_src': edge_src, 'edge_dst': edge_dst, 'deg': deg, 'W_self': W_self, 'W_neigh': W_neigh, 'bias': bias, 'gamma': gamma, 'beta': beta}
    _L0_gnn_all = _L0_gnn_setup()
    _L0_gnn_in = {k: v for k, v in _L0_gnn_all.items() if k in ('W_self', 'W_neigh', 'bias', 'gamma', 'beta')}
    del _L0_gnn_all

    def _L0_ffn_setup():
        import jax, jax.numpy as jnp
        import numpy as np
        TOP_K = 6
        CAP_FACTOR = 2.0
        key = jax.random.key(seed)
        ks = jax.random.split(key, 9)
        B, S, D, F, E, SH = (4, 256, 512, 256, 64, 2)
        return {'x': jax.random.normal(ks[0], (B, S, D), jnp.float32), 'router_w': jax.random.normal(ks[1], (E, D), jnp.float32) * 0.02, 'bias': jnp.zeros((E,), jnp.float32), 'shared_w_gate': jax.random.normal(ks[2], (SH, F, D), jnp.float32) * 0.02, 'shared_w_up': jax.random.normal(ks[3], (SH, F, D), jnp.float32) * 0.02, 'shared_w_down': jax.random.normal(ks[4], (SH, D, F), jnp.float32) * 0.02, 'w_gate': jax.random.normal(ks[5], (E, F, D), jnp.float32) * 0.02, 'w_up': jax.random.normal(ks[6], (E, F, D), jnp.float32) * 0.02, 'w_down': jax.random.normal(ks[7], (E, D, F), jnp.float32) * 0.02}
    _L0_ffn_all = _L0_ffn_setup()
    _L0_ffn_in = {k: v for k, v in _L0_ffn_all.items() if k in ('router_w', 'bias', 'shared_w_gate', 'shared_w_up', 'shared_w_down', 'w_gate', 'w_up', 'w_down')}
    del _L0_ffn_all
    return {'x': x, 'src': src, 'dst': dst, 'L0_gnn_W_self': _L0_gnn_in['W_self'], 'L0_gnn_W_neigh': _L0_gnn_in['W_neigh'], 'L0_gnn_bias': _L0_gnn_in['bias'], 'L0_gnn_gamma': _L0_gnn_in['gamma'], 'L0_gnn_beta': _L0_gnn_in['beta'], 'L0_ffn_router_w': _L0_ffn_in['router_w'], 'L0_ffn_bias': _L0_ffn_in['bias'], 'L0_ffn_shared_w_gate': _L0_ffn_in['shared_w_gate'], 'L0_ffn_shared_w_up': _L0_ffn_in['shared_w_up'], 'L0_ffn_shared_w_down': _L0_ffn_in['shared_w_down'], 'L0_ffn_w_gate': _L0_ffn_in['w_gate'], 'L0_ffn_w_up': _L0_ffn_in['w_up'], 'L0_ffn_w_down': _L0_ffn_in['w_down']}

def reference(x, src, dst, L0_gnn_W_self, L0_gnn_W_neigh, L0_gnn_bias, L0_gnn_gamma, L0_gnn_beta, L0_ffn_router_w, L0_ffn_bias, L0_ffn_shared_w_gate, L0_ffn_shared_w_up, L0_ffn_shared_w_down, L0_ffn_w_gate, L0_ffn_w_up, L0_ffn_w_down):
    import jax
    import jax.numpy as jnp

    def _L0_gnn_ref(x, edge_src, edge_dst, deg, W_self, W_neigh, bias, gamma, beta):
        import jax, jax.numpy as jnp
        import numpy as np
        N_NODES = 1250
        N_EDGES = 20000
        IN_DIM = 512
        OUT_DIM = 512
        LN_EPS = 1e-05
        n = x.shape[0]
        h_self = jnp.einsum('nd,od->no', x, W_self)
        neigh_sum = jax.ops.segment_sum(x[edge_src], edge_dst, num_segments=n)
        neigh_mean = neigh_sum / jnp.maximum(deg, 1.0)[:, None]
        h_neigh = jnp.einsum('nd,od->no', neigh_mean, W_neigh)
        h = h_self + h_neigh + bias
        mu = jnp.mean(h, axis=-1, keepdims=True)
        var = jnp.mean(jnp.square(h - mu), axis=-1, keepdims=True)
        h = (h - mu) * jax.lax.rsqrt(var + LN_EPS)
        return h * gamma + beta

    def _L0_ffn_ref(x, router_w, bias, shared_w_gate, shared_w_up, shared_w_down, w_gate, w_up, w_down):
        import jax, jax.numpy as jnp
        import numpy as np
        TOP_K = 6
        CAP_FACTOR = 2.0
        B, S, D = x.shape
        E = router_w.shape[0]
        K = TOP_K
        N = B * S
        C = max(1, int(N * K * CAP_FACTOR / E))
        router_logits = jnp.einsum('bsd,ed->bse', x, router_w) + bias
        hg = jnp.einsum('bsd,efd->bsef', x, shared_w_gate)
        hu = jnp.einsum('bsd,efd->bsef', x, shared_w_up)
        shared_out = jnp.einsum('bsef,edf->bsd', jax.nn.silu(hg) * hu, shared_w_down)
        shared_out = shared_out / shared_w_gate.shape[0]
        router_probs = jax.nn.softmax(router_logits, axis=-1)
        topk_p, topk_i = jax.lax.top_k(router_probs, K)
        topk_p = topk_p / (jnp.sum(topk_p, axis=-1, keepdims=True) + 1e-09)
        x_flat = x.reshape(N, D)
        flat_e = topk_i.reshape(-1)
        flat_g = topk_p.reshape(-1)
        token_ids = jnp.repeat(jnp.arange(N), K)
        order = jnp.argsort(flat_e)
        se = flat_e[order]
        st = token_ids[order]
        sg = flat_g[order]
        M = se.shape[0]
        pos = jnp.arange(M)
        is_first = jnp.concatenate([jnp.ones((1,), bool), se[1:] != se[:-1]])
        group_starts = jax.lax.cummax(pos * is_first.astype(pos.dtype))
        slot = pos - group_starts
        valid = slot < C
        safe_slot = jnp.where(valid, slot, C)
        expert_in = jnp.zeros((E, C + 1, D), x.dtype).at[se, safe_slot].set(x_flat[st])
        expert_gate = jnp.zeros((E, C + 1), x.dtype).at[se, safe_slot].set(sg)
        expert_tok = jnp.full((E, C + 1), N, jnp.int32).at[se, safe_slot].set(st.astype(jnp.int32))
        expert_mask = jnp.zeros((E, C + 1), bool).at[se, safe_slot].set(valid)
        expert_in = expert_in[:, :C]
        expert_gate = expert_gate[:, :C]
        expert_tok = expert_tok[:, :C]
        expert_mask = expert_mask[:, :C]
        hg = jnp.einsum('ecd,efd->ecf', expert_in, w_gate)
        hu = jnp.einsum('ecd,efd->ecf', expert_in, w_up)
        expert_out = jnp.einsum('ecf,edf->ecd', jax.nn.silu(hg) * hu, w_down)
        fm = expert_mask.reshape(-1)
        dst = jnp.where(fm, expert_tok.reshape(-1), N)
        fg = jnp.where(fm, expert_gate.reshape(-1), jnp.zeros((), x.dtype))
        sparse = jax.ops.segment_sum(fg[:, None] * expert_out.reshape(-1, D), dst, num_segments=N + 1)[:N]
        return shared_out + sparse.reshape(B, S, D)
    deg = jnp.maximum(jax.ops.segment_sum(jnp.ones(dst.shape, jnp.float32), dst, num_segments=1250), 1.0)
    x = x + _L0_gnn_ref(_layernorm(x, axis=-1), src, dst, deg, L0_gnn_W_self, L0_gnn_W_neigh, L0_gnn_bias, L0_gnn_gamma, L0_gnn_beta)
    x = x + _L0_ffn_ref(_layernorm(x, axis=-1)[None], L0_ffn_router_w, L0_ffn_bias, L0_ffn_shared_w_gate, L0_ffn_shared_w_up, L0_ffn_shared_w_down, L0_ffn_w_gate, L0_ffn_w_up, L0_ffn_w_down)[0]
    return x

_drawn_inputs = setup_inputs


def setup_inputs(seed=0):
    import zlib

    import numpy as np

    out = dict(_drawn_inputs(seed))
    spreads = {'L0_gnn_bias': (0.0, 0.1),
     'L0_gnn_gamma': (1.0, 0.2),
     'L0_gnn_beta': (0.0, 0.1),
     'L0_ffn_bias': (0.0, 0.8)}
    factors = {'L0_ffn_router_w': 5.568,
     'L0_ffn_shared_w_gate': 3.354,
     'L0_ffn_shared_w_up': 3.281,
     'L0_ffn_shared_w_down': 3.28,
     'L0_ffn_w_gate': 5.136,
     'L0_ffn_w_up': 5.04,
     'L0_ffn_w_down': 5.062}
    for name, (base, spread) in spreads.items():
        noise = np.random.default_rng([zlib.crc32(name.encode()), seed]).standard_normal(out[name].shape)
        drawn = base * np.exp(spread * noise) if base else spread * noise
        out[name] = jnp.asarray(drawn.astype(out[name].dtype))
    for name, factor in factors.items():
        out[name] = (out[name] * factor).astype(out[name].dtype)
    return out
```

```python
from contextlib import ExitStack

import concourse.bass as bass
from concourse import mybir

F32 = mybir.dt.float32
BF16 = mybir.dt.bfloat16
F16 = mybir.dt.float16
I32 = mybir.dt.int32
U32 = mybir.dt.uint32
ALU = mybir.AluOpType
ACT = mybir.ActivationFunctionType
AX = mybir.AxisListType

P = 128
N, D, E, F = 1250, 512, 64, 256
TOPK = 6
SH = 2
CAP = N * TOPK * 2 // E
NT = -(-N // P)
NPAD = NT * P
LAST = N - (NT - 1) * P
DC, FC = D // P, F // P
EPS = 1e-5
EDGES, EP = 20000, 125
ET = EDGES // EP
EH = ET // 2
G = 4
NG = ET // G
DEG = NPAD - 1
SLOTS = 2 * P
ZROW = E * SLOTS
U = 4
WCOL = DC * 2 * F + FC * D


class Steps:

    def __init__(self, eng, sem):
        self.eng, self.sem, self.n = eng, sem, 0

    def mark(self, ins):
        ins.then_inc(self.sem, 1)
        self.n += 1

    def wait(self):
        self.eng.wait_ge(self.sem, self.n)

    def restart(self):
        if self.n:
            self.wait()
            self.eng.sem_inc(self.sem, -self.n)
            self.n = 0


def gnn_moe(nc, x, src, dst, w_self, w_neigh, bias, gamma, beta, router_w, router_b,
            shared_gu, shared_down, expert_w, out):
    ctx = ExitStack()
    with ctx:
        def sb(name, shape, dt):
            return ctx.enter_context(nc.sbuf_tensor(name, shape, dt))

        def sem(name):
            return ctx.enter_context(nc.semaphore(name))

        t_dram = nc.dram_tensor("t_rows", [NPAD, D], F32).ap()
        y_dram = nc.dram_tensor("y_rows", [ZROW + P, D], F32).ap()

        ps = ctx.enter_context(nc.psum_tensor("ps", [P, 8, 512], F32))
        acc = [ps[:, 3 * b:3 * b + 3, :].rearrange("p b n -> p (b n)") for b in range(2)]

        iota_h = sb("iota_h", [P, NPAD], F16)
        iota_e = sb("iota_e", [P, E], F32)
        ident = sb("ident", [P, P], F32)
        before = sb("before", [P, P], BF16)
        ones = sb("ones", [P, P], BF16)
        zero_h = sb("zero_h", [P, P], F16)
        zrows = sb("zrows", [P, D], F32)
        tok_f = sb("tok_f", [P, NT], F32)
        valid = sb("valid", [P, NT], F32)
        src_i = sb("src_i", [EH, 2, EP], I32)
        dst_i = sb("dst_i", [EH, 2, EP], I32)
        xs = sb("xs", [P, NT, D], F32)
        ws = sb("ws", [P, DC, D], F32)
        wn = sb("wn", [P, DC, D], F32)
        rw = sb("rw", [P, DC, E], F32)
        rb = sb("rb", [P, E], F32)
        bias_b = sb("bias_b", [P, D], F32)
        gamma_b = sb("gamma_b", [P, D], F32)
        beta_b = sb("beta_b", [P, D], F32)
        src_f = sb("src_f", [EH, 2, EP], F32)
        dst_f = sb("dst_f", [EH, 2, EP], F32)
        ends = sb("ends", [EH, 4], F32)
        edge = sb("edge", [EP, 4 * EH], F32)
        wrow = sb("wrow", [1, 2, NG], F32)
        wint = sb("wint", [1, 2, NG], I32)
        wcap = sb("wcap", [1, 2, NG], F32)
        wtab_f = sb("wtab_f", [1, 3, NG], F32)
        zrow1 = sb("zrow1", [1, E], F32)
        wtab = sb("wtab", [1, 3, NG], I32)
        hot_all = sb("hot_all", [P, 2, G, NPAD], BF16)
        hot_src = [hot_all[0:EP, b, :, :] for b in range(2)]
        hot_dst = [sb(f"hot_dst{b}", [EP, G, P], BF16) for b in range(2)]
        hot_more = sb("hot_more", [EP, G, P], BF16)
        counts = sb("counts", [P, NT, NPAD], F32)
        stat = sb("stat", [P, NT, 6], F32)
        mv = sb("mv", [P, NT, 2], F32)
        ve = sb("ve", [P, NT], F32)
        sd = sb("sd", [P, NT], F32)
        rs = sb("rs", [P, NT], F32)
        rq = sb("rq", [P, NT], F32)
        xn = sb("xn", [P, NT, D], F32)
        cw = sb("cw", [P, NPAD], F32)
        xw = sb("xw", [P, D], F32)
        ct = sb("ct", [P, NT, P], F32)
        nsum = sb("nsum", [P, D], F32)
        nsum_t = sb("nsum_t", [P, DC, P], F32)
        xw_t = sb("xw_t", [P, DC, P], F32)
        rdeg = sb("rdeg", [P, NT], F32)
        hn = sb("hn", [P, D], F32)
        h0 = sb("h0", [P, D], F32)
        h1 = sb("h1", [P, D], F32)
        st1 = sb("st1", [P, 16], F32)
        st2 = sb("st2", [P, 16], F32)
        tw = sb("tw", [P, D], F32)
        tw_t = sb("tw_t", [P, DC, P], F32)
        t_t = sb("t_t", [P, NT, D], F32)
        logits = sb("logits", [P, NT, E], F32)
        wsd = ws
        tt2 = [xw_t, tw_t]
        sg, hsh, hsh_t = h0, h1, nsum_t
        v8 = sb("v8", [P, NT, 8], F32)
        lgw = sb("lgw", [P, E], F32)
        v8w = sb("v8w", [P, 8], F32)
        i8 = sb("i8", [P, 8], U32)
        i6 = sb("i6", [P, TOPK], F32)
        ctf = ct[:, :, :].rearrange("p a n -> p (a n)")
        hot_e = ctf[:, 0:TOPK * E].rearrange("p (k e) -> p k e", k=TOPK)
        hot_s = ctf[:, TOPK * E:2 * TOPK * E].rearrange("p (k e) -> p k e", k=TOPK)
        mask = sb("mask", [P, E], BF16)
        msum = sb("msum", [P, E], BF16)
        slot = sb("slot", [P, TOPK], F32)
        keep = sb("keep", [P, TOPK], F32)
        half = sb("half", [P, TOPK], F32)
        lo = sb("lo", [P, TOPK], F32)
        hi = sb("hi", [P, TOPK], F32)
        yrow = sb("yrow", [P, TOPK], F32)
        yidx = sb("yidx", [P, NT, TOPK], I32)
        vm1 = sb("vm1", [P, NT], F32)
        ex6 = sb("ex6", [P, NT, TOPK], F32)
        zsum = sb("zsum", [P, 2, NT], F32)
        rden = sb("rden", [P, NT], F32)
        gate = sb("gate", [P, NT, TOPK], F32)
        hot_w = TOPK * P // 2
        hot_lo, hot_hi = (cw[:, q * hot_w:(q + 1) * hot_w].bitcast(F16).rearrange("p (k m) -> p k m", k=TOPK)
                          for q in range(2))
        tokidx = sb("tokidx", [P, 2 * E], I32)
        cnt = sb("cnt", [1, E], F32)
        rank_f = sb("rank_f", [1, U + E], F32)
        rank = sb("rank", [1, U + E], I32)
        cflat = counts[:, :, :].rearrange("p w n -> p (w n)")
        wbuf = [cflat[:, s * WCOL:(s + 1) * WCOL] for s in range(U)]
        idxb = [[sb(f"idx{h}_{s}", [P, 1], I32) for s in range(U)] for h in range(2)]
        gx = [[xn[:, U * h + s, :] for s in range(U)] for h in range(2)]
        xt = [ct[:, DC * h:DC * h + DC, :] for h in range(2)]
        sil = [cw[:, F * h:F * h + F] for h in range(2)]
        ht = [cw[:, F * (2 + h):F * (3 + h)].rearrange("p (c m) -> p c m", c=FC) for h in range(2)]
        hh = [xw[:, F * h:F * h + F] for h in range(2)]
        yb = [[t_t[:, U * h + s, :] for s in range(U)] for h in range(2)]
        wsg = hot_all[:, :, :, :].rearrange("p b t n -> p (b t n)")[:, 0:DC * 2 * D * 2].bitcast(F32).rearrange("p (c n) -> p c n", c=DC)
        yg = [[xn[:, k, :] for k in range(TOPK)], None]
        yg[1] = [t_t[:, k, :] for k in range(TOPK)]
        cidx = [[sb(f"cidx{b}_{k}", [P, 1], I32) for k in range(TOPK)] for b in range(2)]
        oacc = [tw, nsum]

        s_src, s_dst, s_x, s_w, s_wn, s_vec, s_rw = (sem(n) for n in (
            "src_in", "dst_in", "x_in", "w_self_in", "w_neigh_in", "vectors_in", "router_in"))
        s_gu, s_dn = sem("shared_gu_in"), sem("shared_down_in")
        s_cst = sem("consts_set")
        s_idt = sem("ident_zeroed")
        s_hot0 = sem("hot_src_set")
        s_xpad = sem("x_pad_zeroed")
        dv = sem("dve_steps")
        s_past = {n: sem(f"past_{n}") for n in ("dve", "pe", "sp", "pool", "act")}
        s_ef = sem("edges_float")
        s_eT = sem("edges_transposed")
        s_win = sem("windows_known")
        s_hs = sem("hot_ready")
        s_cd = sem("group_counted")
        s_cc = sem("counts_current")
        m_hot, m_cnt, m_add = sem("more_hot_ready"), sem("more_counted"), sem("more_added")
        s_xn = sem("x_normed")
        s_cw, s_xw = sem("counts_staged"), sem("x_staged")
        s_ctT, s_ctA, s_ctV = sem("counts_T"), sem("counts_T_copied_act"), sem("counts_T_copied_dve")
        s_ns, s_nsc = sem("neigh_summed"), sem("neigh_copied")
        s_nT, s_nTc, s_xT, s_xTc = sem("neigh_T"), sem("neigh_T_copied"), sem("x_T"), sem("x_T_copied")
        s_self, s_nb = sem("self_projected"), sem("neigh_projected")
        s_rdeg, s_hn, s_h = sem("degree_known"), sem("neigh_scaled"), sem("self_added")
        s_var, s_sqrt = sem("variance_ready"), sem("sqrt_ready")
        s_t, s_tst = sem("t_ready"), sem("t_stored")
        s_tT, s_tTc, s_lg, s_lgc = sem("t_T"), sem("t_T_copied"), sem("logits_done"), sem("logits_copied")
        s_tk = sem("t_T_kept")
        s_tt2 = sem("t_T_staged")
        s_ga, s_up, s_silu, s_hm = sem("gate_done"), sem("up_done"), sem("silu_done"), sem("hidden_done")
        s_hT, s_hTc, s_dw, s_base = sem("hidden_T"), sem("hidden_T_copied"), sem("down_done"), sem("base_ready")
        s_mask, s_pre = sem("mask_ready"), sem("prefix_done")
        s_sub, s_exp = sem("logits_lowered"), sem("exps_done")
        s_z = sem("zrows_set")
        s_zf = sem("second_rows_zeroed")
        s_hl, s_tab, s_cnt = sem("table_hot"), sem("table_added"), sem("tokens_counted")
        s_rank, s_tok = sem("rank_known"), sem("tokens_listed")
        e_w = [sem(f"expert_w_in{s}") for s in range(U)]
        e_idx = sem("expert_idx_copied")
        e_gx = [sem(f"rows_in{s}") for s in range(U)]
        e_gx2 = sem("second_rows_in")
        e_xT = sem("rows_T"), sem("second_rows_T")
        e_xTc = sem("rows_T_copied"), sem("second_rows_T_copied")
        e_gu = sem("gate_up"), sem("second_gate_up")
        e_si = sem("silu"), sem("second_silu")
        e_h = sem("hidden"), sem("second_hidden")
        e_hT = sem("hid_T"), sem("second_hid_T")
        e_hTc = sem("hid_T_copied"), sem("second_hid_T_copied")
        e_y = sem("y"), sem("second_y")
        e_yc = sem("y_copied"), sem("second_y_copied")
        e_st = [sem(f"y_stored{s}") for s in range(U)]
        e_st2 = sem("zero_and_second_y_stored")
        s_out = [sem(f"out_stored{b}") for b in range(2)]
        c_idx = sem("combine_idx_copied")
        c_y = [[sem(f"y_in{b}_{k}") for k in range(TOPK)] for b in range(2)]
        c_acc = sem("combined")

        block = ctx.enter_context(nc.Block())

        @block.sync
        def _(sp):
            sp.dma_start(dst_i[:, :, :], dst.rearrange("(h t p) -> t h p", h=2, p=EP)).then_inc(s_dst, 16)
            sp.dma_start(src_i[:, :, :], src.rearrange("(h t p) -> t h p", h=2, p=EP)).then_inc(s_src, 16)
            sp.dma_start(xs[:, 0:NT - 1, :], x[0:(NT - 1) * P, :].rearrange("(t p) d -> p t d", p=P)).then_inc(s_x, 16)
            sp.wait_ge(s_xpad, 1)
            sp.dma_start(xs[0:LAST, NT - 1, :], x[(NT - 1) * P:N, :]).then_inc(s_x, 16)
            sp.dma_start(ws[:, :, :], w_self).then_inc(s_w, 16)
            sp.dma_start(wn[:, :, :], w_neigh).then_inc(s_wn, 16)
            sp.dma_start(rw[:, :, :], router_w).then_inc(s_rw, 16)
            for buf, vec in ((bias_b, bias), (gamma_b, gamma), (beta_b, beta), (rb, router_b)):
                v = vec.rearrange("(a n) -> a n", a=1)
                sp.dma_start(buf[:, :], v.broadcast_to([P, v.shape[1]])).then_inc(s_vec, 16)
            sp.wait_ge(s_z, 1)
            sp.dma_start(y_dram[ZROW:ZROW + P, :], zrows[:, :]).then_inc(e_st2, 16)
            halves = y_dram[0:ZROW, :].rearrange("(e h p) d -> p h e d", h=2, p=P)
            for q in range(4):
                sp.dma_start(halves[:, 1, q * E // 4:(q + 1) * E // 4, :],
                             zrows[:, :].rearrange("p (a d) -> p a d", a=1).broadcast_to([P, E // 4, D])).then_inc(s_zf, 16)
            sp.wait_ge(s_cc, NG + 1)
            sp.dma_start(wsg[:, :, :], shared_gu).then_inc(s_gu, 16)
            with sp.Fori(0, NT) as w:
                sp.wait_ge(s_t, w + 1)
                sp.dma_start(t_dram[bass.ds(w * P, P), :], tw[:, :]).then_inc(s_tst, 16)
            sp.wait_ge(s_self, NT)
            sp.dma_start(wsd[:, :, :], shared_down).then_inc(s_dn, 16)
            sp.wait_ge(s_cw, NT)
            for s in range(U):
                sp.dma_start(wbuf[s], expert_w[s]).then_inc(e_w[s], 16)

            def expert_io(i, load):
                for s in range(U):
                    e = i * U + s
                    r0 = sp.value_load(rank[0:1, bass.ds(e + U - 1, 1)], min_val=0, max_val=E)
                    r1 = sp.value_load(rank[0:1, bass.ds(e + U, 1)], min_val=0, max_val=E)
                    sp.wait_ge(e_yc[0], e + 2)
                    sp.dma_start(y_dram[bass.ds(e * SLOTS, P), :], yb[0][s]).then_inc(e_st[s], 16)
                    with sp.If(r1 > r0):
                        sp.wait_ge(e_yc[1], r1 + 1)
                        sp.dma_start(y_dram[bass.ds(e * SLOTS + P, P), :], yb[1][s]).then_inc(e_st2, 16)
                    if load:
                        sp.dma_start(wbuf[s], expert_w[bass.ds(e + U, 1), :, :].rearrange("a p n -> (a p) n")
                                     ).then_inc(e_w[s], 16)
                    with sp.If(r1 > r0):
                        sp.wait_ge(e_st2, r1 * 16 + 16)
                        sp.sem_inc(s_past["sp"], 1)

            sp.wait_ge(s_rank, 1)
            sp.wait_ge(s_zf, 64)
            with sp.Fori(0, E // U - 1) as i:
                expert_io(i, True)
            expert_io(E // U - 1, False)
            for w in range(NT):
                sp.wait_ge(c_acc, (w + 1))
                rows = P if w < NT - 1 else LAST
                sp.dma_start(out[w * P:w * P + rows, :], oacc[w % 2][0:rows, :]).then_inc(s_out[w % 2], 16)
            for b in range(2):
                sp.wait_ge(s_out[b], 16 * (NT // 2))

        @block.gpsimd
        def _(pool):
            g = nc.gpsimd
            g.memset(xs[96:P, NT - 1, :], 0.0).then_inc(s_xpad, 1)
            pool.wait_ge(s_xpad, 1)
            g.memset(ident[:, :], 0.0).then_inc(s_idt, 1)
            g.memset(before[:, :], 1.0).then_inc(s_idt, 1)
            pool.wait_ge(s_idt, 2)
            g.affine_select(out=ident[:, :], in_=ident[:, :], compare_op=ALU.not_equal, fill=1.0, base=0,
                            pattern=[[-1, P]], channel_multiplier=1).then_inc(s_cst, 1)
            g.affine_select(out=before[:, :], in_=before[:, :], compare_op=ALU.is_gt, fill=0.0, base=0,
                            pattern=[[1, P]], channel_multiplier=-1).then_inc(s_cst, 1)
            g.iota(iota_h[:, :], [[1, NPAD]], base=0, channel_multiplier=0,
                   allow_small_or_imprecise_dtypes=True).then_inc(s_cst, 1)
            for b in range(2):
                g.memset(hot_src[b][:, :, N:NPAD], 0.0).then_inc(s_idt, 1)
            pool.wait_ge(s_idt, 4)
            for b in range(2):
                g.memset(hot_src[b][:, :, DEG:NPAD], 1.0).then_inc(s_hot0, 1)
            g.memset(counts[:, :, :], 0.0).then_inc(s_cc, 1)
            g.iota(iota_e[:, :], [[1, E]], base=0, channel_multiplier=0,
                   allow_small_or_imprecise_dtypes=True).then_inc(s_cst, 1)
            g.iota(tok_f[:, :], [[P, NT]], base=0, channel_multiplier=1,
                   allow_small_or_imprecise_dtypes=True).then_inc(s_cst, 1)
            g.memset(ones[:, :], 1.0).then_inc(s_cst, 1)
            g.memset(zero_h[:, :], 0.0).then_inc(s_cst, 1)
            g.memset(msum[:, :], 0.0).then_inc(s_cst, 1)
            g.memset(zrow1[:, :], 0.0).then_inc(s_cst, 1)
            g.memset(rank_f[:, :], 0.0).then_inc(s_cst, 1)
            g.memset(zrows[:, :], 0.0).then_inc(s_z, 1)

            pool.wait_ge(s_xn, 1)
            pool.wait_ge(s_cc, NG + 1)
            g.tensor_copy(cw[:, :], counts[:, 0, :]).then_inc(s_cw, 1)
            g.tensor_copy(xw[:, :], xn[:, 0, :]).then_inc(s_xw, 1)

            def stage_counts(w):
                pool.wait_ge(s_ctT, w * 3)
                pool.wait_ge(s_rdeg, w)
                g.tensor_copy(cw[:, :], counts[:, bass.ds(w, 1), :].rearrange("p a n -> p (a n)")).then_inc(s_cw, 1)

            def stage_tile(w, last=False):
                pool.wait_ge(s_xT, w)
                g.tensor_copy(xw[:, :], xn[:, bass.ds(w, 1), :].rearrange("p a n -> p (a n)")).then_inc(s_xw, 1)
                if not last:
                    stage_counts(w + 1)
                pool.wait_ge(s_tTc, w)
                g.tensor_copy(t_t[:, bass.ds(w - 1, 1), :].rearrange("p a n -> p (a n)"),
                              tw_t[:, :, :].rearrange("p c m -> p (c m)")).then_inc(s_tk, 1)

            stage_counts(1)
            with pool.Fori(1, NT - 1) as w:
                stage_tile(w)
            stage_tile(NT - 1, last=True)
            pool.wait_ge(s_tTc, NT)
            g.tensor_copy(t_t[:, NT - 1, :], tw_t[:, :, :].rearrange("p c m -> p (c m)")).then_inc(s_tk, 1)

            pool.wait_ge(s_tst, 16 * NT)
            pool.wait_ge(s_tok, 1)
            pool.wait_ge(s_rank, 1)

            def gather(e, s, h, done):
                g.tensor_copy(idxb[h][s][:, :], tokidx[:, bass.ds(2 * e + h, 1)]).then_inc(e_idx, 1)
                pool.wait_ge(e_idx, 1)
                pool.sem_inc(e_idx, -1)
                g.indirect_dma_start(gx[h][s], None, t_dram, bass.IndirectOffsetOnAxis(ap=idxb[h][s][:, :], axis=0)
                                     ).then_inc(done, 16)

            with pool.Fori(0, E // U) as i:
                for s in range(U):
                    e = i * U + s
                    pool.wait_ge(e_xT[0], e + 1)
                    gather(e, s, 0, e_gx[s])
                    ro = pool.value_load(rank[0:1, bass.ds(e, 1)], min_val=0, max_val=E)
                    r0 = pool.value_load(rank[0:1, bass.ds(e + U - 1, 1)], min_val=0, max_val=E)
                    r1 = pool.value_load(rank[0:1, bass.ds(e + U, 1)], min_val=0, max_val=E)
                    with pool.If(r1 > r0):
                        pool.wait_ge(e_xT[1], ro + 1)
                        gather(e, s, 1, e_gx2)
                        pool.wait_ge(e_gx2, r1 * 16)
                        pool.sem_inc(s_past["pool"], 1)

            for s in range(U):
                pool.wait_ge(e_st[s], 16 * (E // U))
            second = pool.value_load(rank[0:1, U + E - 1:U + E], min_val=0, max_val=E)
            pool.wait_ge(e_st2, second * 16 + 16)
            pool.sem_inc(s_past["pool"], 1)
            for w in range(NT):
                b = w % 2
                for k in range(TOPK):
                    if w >= 2:
                        pool.wait_ge(c_acc, w - 1)
                    g.tensor_copy(cidx[b][k][:, :], yidx[:, w, k:k + 1]).then_inc(c_idx, 1)
                    pool.wait_ge(c_idx, w * TOPK + k + 1)
                    g.indirect_dma_start(yg[b][k], None, y_dram, bass.IndirectOffsetOnAxis(ap=cidx[b][k][:, :], axis=0)
                                         ).then_inc(c_y[b][k], 16)

        @block.tensor
        def _(pe):
            T = nc.tensor
            pe.wait_ge(s_cst, 1)
            pe.wait_ge(s_ef, 2)
            for q, a in enumerate((src_f, src_f, dst_f, dst_f)):
                m = T.transpose(ps[0:EP, 6, q * EH:(q + 1) * EH], a[:, q % 2, :], ident[0:EH, 0:EH])
            m.then_inc(s_eT, 1)
            pe.wait_ge(s_ef, 4)
            for q in range(4):
                m = T.transpose(ps[0:1, 7, q * EH:(q + 1) * EH], ends[:, q:q + 1], ident[0:EH, 0:EH])
            m.then_inc(s_eT, 1)

            def count(par, hot):
                for t in range(G):
                    for n0 in range(0, NPAD, 512):
                        n1 = min(n0 + 512, NPAD)
                        m = T.matmul(acc[par][:, n0:n1], hot[:, t, :], hot_src[par][:, t, n0:n1],
                                     start=(t == 0), stop=(t == G - 1))
                return m

            def group(g, par):
                pe.wait_ge(s_hs, g + 1)
                if not isinstance(g, int) or g >= 2:
                    pe.wait_ge(s_cc, g)
                count(par, hot_dst[par]).then_inc(s_cd, 1)
                more = pe.value_load(wtab[0:1, 1, bass.ds(g, 1)], min_val=0, max_val=NT - 1)
                with pe.If(more > 0):
                    base = pe.value_load(wtab[0:1, 2, bass.ds(g, 1)], min_val=0, max_val=NT * NG)
                    with pe.Fori(0, NT - 1) as j:
                        with pe.If(j < more):
                            pe.wait_ge(s_cc, g + 2)
                            pe.wait_ge(m_hot, (base + j + 1) * G)
                            count(par, hot_more).then_inc(m_cnt, 1)
                            pe.wait_ge(m_add, base + j + 1)
                            pe.sem_inc(s_past["pe"], 1)

            pe.wait_ge(s_hot0, 2)
            pe.wait_ge(s_win, 1)
            for g in range(2):
                group(g, g)
            with pe.Fori(1, NG // 2) as i:
                for par in range(2):
                    group(i * 2 + par, par)

            def counts_T(w):
                pe.wait_ge(s_cw, w + 1)
                for b in range(3):
                    for q in range(4 * b, min(4 * b + 4, NT)):
                        m = T.transpose(ps[:, b, (q % 4) * P:(q % 4 + 1) * P], cw[:, q * P:(q + 1) * P], ident[:, :])
                    m.then_inc(s_ctT, 1)

            def neigh(w):
                pe.wait_ge(s_ctA, 2 * w + 2)
                pe.wait_ge(s_ctV, w + 1)
                for q in range(NT):
                    m = T.matmul(ps[:, 5, :], ct[:, q, :], xn[:, q, :], start=(q == 0), stop=(q == NT - 1))
                m.then_inc(s_ns, 1)

            def turn(bank, a, done):
                for c in range(DC):
                    m = T.transpose(ps[:, bank, c * P:(c + 1) * P], a[:, c * P:(c + 1) * P], ident[:, :])
                m.then_inc(done, 1)

            def project(bank, a, wt, done, n=D):
                for c in range(DC):
                    m = T.matmul(ps[:, bank, 0:n], a[:, c, :], wt[:, c, :], start=(c == 0), stop=(c == DC - 1))
                m.then_inc(done, 1)

            def tile_a(w):
                pe.wait_ge(s_nsc, w + 1)
                if not isinstance(w, int) or w:
                    pe.wait_ge(s_tTc, w)
                turn(3, nsum, s_nT)
                pe.wait_ge(s_xw, w + 1)
                if not isinstance(w, int) or w:
                    pe.wait_ge(s_lgc, w)
                turn(4, xw, s_xT)
                pe.wait_ge(s_xTc, w + 1)
                if not isinstance(w, int) or w:
                    pe.wait_ge(s_h, w)
                project(6, xw_t, ws, s_self)
                pe.wait_ge(s_nTc, w + 1)
                if not isinstance(w, int) or w:
                    pe.wait_ge(s_hn, w)
                project(7, nsum_t, wn, s_nb)

            def tile_b(w):
                pe.wait_ge(s_t, w + 1)
                turn(3, tw, s_tT)
                pe.wait_ge(s_tTc, w + 1)
                project(4, tw_t, rw, s_lg, E)

            pe.wait_ge(s_xn, 1)
            pe.wait_ge(s_cc, NG + 1)
            pe.wait_ge(s_w, 16)
            pe.wait_ge(s_wn, 16)
            pe.wait_ge(s_rw, 16)
            counts_T(0)
            neigh(0)
            with pe.Fori(1, NT) as k:
                counts_T(k)
                tile_a(k - 1)
                neigh(k)
                tile_b(k - 1)
            tile_a(NT - 1)
            tile_b(NT - 1)

            def down(w):
                pe.wait_ge(s_hTc, w + 1)
                if not isinstance(w, int) or w:
                    pe.wait_ge(s_base, w)
                project(3, hsh_t, wsd, s_dw)

            def hidden_T(w):
                pe.wait_ge(s_hm, w + 1)
                turn(2, hsh, s_hT)

            def prefix(w):
                pe.wait_ge(s_mask, w + 1)
                T.matmul(ps[:, 4, 0:E], before[:, :], mask[:, :], start=True, stop=False)
                T.matmul(ps[:, 4, 0:E], ones[:, :], msum[:, :], start=False, stop=True).then_inc(s_pre, 1)

            def table(w):
                pe.wait_ge(s_hl, w + 1)
                for k in range(TOPK):
                    m = T.matmul(ps[:, 5, 0:P], hot_lo[:, k, :], hot_hi[:, k, :], start=False, stop=False,
                                 skip_group_check=True)
                m.then_inc(s_tab, 1)

            def gate_(w, par):
                pe.wait_ge(s_tt2, w + 1)
                if not isinstance(w, int) or w:
                    pe.wait_ge(s_silu, w)
                project(0, tt2[par], wsg[:, :, 0:D], s_ga)

            def up_(w, par):
                if not isinstance(w, int) or w:
                    pe.wait_ge(s_hm, w)
                project(1, tt2[par], wsg[:, :, D:2 * D], s_up)

            pe.wait_ge(s_gu, 16)
            pe.wait_ge(s_dn, 16)
            pe.wait_ge(s_cst, 10)
            pe.wait_ge(s_lgc, NT)
            pe.wait_ge(s_nsc, NT)
            T.matmul(ps[:, 5, 0:P], zero_h[:, :], zero_h[:, :], start=True, stop=False, skip_group_check=True)

            def shared(w, par, first=False):
                gate_(w, par)
                if not first:
                    hidden_T(w - 1)
                prefix(w)
                up_(w, par)
                if not first:
                    down(w - 1)
                    table(w - 1)

            shared(0, 0, True)
            shared(1, 1)
            with pe.Fori(1, NT // 2) as i:
                shared(i * 2, 0)
                shared(i * 2 + 1, 1)
            table(NT - 1)
            T.matmul(ps[:, 5, 0:P], zero_h[:, :], zero_h[:, :], start=False, stop=True,
                     skip_group_check=True).then_inc(s_tab, 1)
            pe.wait_ge(s_mask, NT + 1)
            T.matmul(ps[0:1, 6, 0:E], ones[:, 0:1], msum[:, :], start=True, stop=True).then_inc(s_cnt, 1)
            hidden_T(NT - 1)
            down(NT - 1)

            pe.wait_ge(s_base, NT)
            pe.wait_ge(s_tok, 1)
            pe.wait_ge(s_rank, 1)
            pe.sem_inc(e_xT[0], U)
            pe.sem_inc(e_xT[1], 1)

            def rows_T(h, s, n):
                pe.wait_ge(e_xTc[h], n)
                for c in range(DC):
                    m = T.transpose(ps[:, 4 * h, c * P:(c + 1) * P], gx[h][s][:, c * P:(c + 1) * P], ident[:, :])
                m.then_inc(e_xT[h], 1)

            def gate_up(h, s, n):
                pe.wait_ge(e_xTc[h], n + 1)
                pe.wait_ge(e_h[h], n)
                for c in range(DC):
                    m = T.matmul(ps[:, 4 * h + 1, :], xt[h][:, c, :], wbuf[s][:, c * 2 * F:(c + 1) * 2 * F],
                                 start=(c == 0), stop=(c == DC - 1))
                m.then_inc(e_gu[h], 1)

            def hid_T(h, n):
                pe.wait_ge(e_h[h], n + 1)
                pe.wait_ge(e_hTc[h], n)
                for c in range(FC):
                    m = T.transpose(ps[:, 4 * h + 2, c * P:(c + 1) * P], hh[h][:, c * P:(c + 1) * P], ident[:, :])
                m.then_inc(e_hT[h], 1)

            def down_y(h, s, n):
                pe.wait_ge(e_hTc[h], n + 1)
                pe.wait_ge(e_yc[h], n)
                o = DC * 2 * F
                for c in range(FC):
                    m = T.matmul(ps[:, 4 * h + 3, :], ht[h][:, c, :], wbuf[s][:, o + c * D:o + (c + 1) * D],
                                 start=(c == 0), stop=(c == FC - 1))
                m.then_inc(e_y[h], 1)

            def rows_T_both(e, s, turn_no, r0, r1):
                pe.wait_ge(e_gx[s], turn_no * 16)
                rows_T(0, s, e + 1)
                with pe.If(r1 > r0):
                    pe.wait_ge(e_gx2, r1 * 16)
                    rows_T(1, s, r1)

            def expert_body(i, first=False, last=False):
                r = [pe.value_load(rank[0:1, bass.ds(i * U + j, 1)], min_val=0, max_val=E)
                     for j in range(2, U + (U if last else U + 1))]
                r = [None, None] + r
                if first:
                    rows_T_both(0, 0, 1, r[U - 1], r[U])
                for s in range(U):
                    e = i * U + s
                    pe.wait_ge(e_w[s], (i + 1) * 16)
                    gate_up(0, s, e + 1)
                    with pe.If(r[U + s] > r[U + s - 1]):
                        gate_up(1, s, r[U + s])
                    if not (first and s == 0):
                        hid_T(0, e)
                        with pe.If(r[U + s - 1] > r[U + s - 2]):
                            hid_T(1, r[U + s - 1])
                    if not (last and s == U - 1):
                        rows_T_both(e + 1, (s + 1) % U, i + 1 + (s + 1) // U, r[U + s], r[U + s + 1])
                    if not (first and s == 0):
                        down_y(0, (s - 1) % U, e)
                        with pe.If(r[U + s - 1] > r[U + s - 2]):
                            down_y(1, (s - 1) % U, r[U + s - 1])
                if last:
                    hid_T(0, E)
                    with pe.If(r[2 * U - 1] > r[2 * U - 2]):
                        hid_T(1, r[2 * U - 1])
                    down_y(0, U - 1, E)
                    with pe.If(r[2 * U - 1] > r[2 * U - 2]):
                        down_y(1, U - 1, r[2 * U - 1])

            expert_body(0, first=True)
            with pe.Fori(1, E // U - 1) as i:
                expert_body(i)
            expert_body(E // U - 1, last=True)

        @block.scalar
        def _(act):
            A = nc.scalar

            def later(w):
                return not isinstance(w, int) or w > 0

            def flat(a):
                return a.rearrange("p a n -> p (a n)")

            act.wait_ge(s_var, 1)
            A.activation(sd[:, :], ve[:, :], ACT.Sqrt).then_inc(s_sqrt, 1)

            def counts_T(w):
                if later(w):
                    act.wait_ge(s_ns, w)
                for b in range(2):
                    act.wait_ge(s_ctT, 3 * w + b + 1)
                    A.activation(flat(ct[:, 4 * b:4 * b + 4, :]), ps[:, b, :], ACT.Copy).then_inc(s_ctA, 1)

            def neigh(w):
                act.wait_ge(s_ns, w + 1)
                if later(w):
                    act.wait_ge(s_nT, w)
                A.activation(nsum[:, :], ps[:, 5, :], ACT.Copy).then_inc(s_nsc, 1)

            def tile(w):
                act.wait_ge(s_nT, w + 1)
                if later(w):
                    act.wait_ge(s_nb, w)
                A.activation(flat(nsum_t[:, :, :]), ps[:, 3, :], ACT.Copy).then_inc(s_nTc, 1)
                act.wait_ge(s_nb, w + 1)
                act.wait_ge(s_rdeg, w + 1)
                if later(w):
                    act.wait_ge(s_h, w)
                A.activation(hn[:, :], ps[:, 7, :], ACT.Copy, scale=rdeg[:, bass.ds(w, 1)]).then_inc(s_hn, 1)
                for j, st in enumerate((st1, st2)):
                    act.wait_ge(s_var, 2 * w + j + 2)
                    A.activation(st[:, 9:10], st[:, 8:9], ACT.Sqrt).then_inc(s_sqrt, 1)

            counts_T(0)
            neigh(0)
            with act.Fori(1, NT) as k:
                counts_T(k)
                tile(k - 1)
                neigh(k)
            tile(NT - 1)

            def stage(w, par):
                act.wait_ge(s_tk, w + 1)
                if not isinstance(w, int) or w >= 2:
                    act.wait_ge(s_up, w - 1)
                A.activation(flat(tt2[par][:, :, :]), flat(t_t[:, bass.ds(w, 1), :]), ACT.Copy).then_inc(s_tt2, 1)

            def silu(w):
                act.wait_ge(s_ga, w + 1)
                if later(w):
                    act.wait_ge(s_hm, w)
                A.activation(sg[:, :], ps[:, 0, :], ACT.Silu).then_inc(s_silu, 1)

            def hidden_T(w):
                act.wait_ge(s_hT, w + 1)
                if later(w):
                    act.wait_ge(s_dw, w)
                A.activation(flat(hsh_t[:, :, :]), ps[:, 2, :], ACT.Copy).then_inc(s_hTc, 1)

            act.wait_ge(s_self, NT)
            act.wait_ge(s_lg, NT)
            act.wait_ge(s_tk, NT)
            act.wait_ge(s_t, NT)
            stage(0, 0)
            stage(1, 1)
            silu(0)
            silu(1)
            hidden_T(0)
            with act.Fori(1, NT // 2) as i:
                for par in range(2):
                    stage(2 * i + par, par)
                    silu(2 * i + par)
                    hidden_T(2 * i + par - 1)
            hidden_T(NT - 1)
            act.wait_ge(s_sub, 1)
            A.activation(flat(logits[:, :, :]), flat(logits[:, :, :]), ACT.Exp).then_inc(s_exp, 1)
            A.activation(flat(ex6[:, :, :]), flat(ex6[:, :, :]), ACT.Exp).then_inc(s_exp, 1)
            act.wait_ge(s_rank, 1)
            act.sem_inc(e_yc[0], 1)
            act.sem_inc(e_yc[1], 1)

            def e_silu(h, n):
                act.wait_ge(e_gu[h], n)
                act.wait_ge(e_h[h], n)
                A.activation(sil[h], ps[:, 4 * h + 1, 0:F], ACT.Silu).then_inc(e_si[h], 1)

            def y_copy(h, s, n):
                act.wait_ge(e_y[h], n)
                A.activation(yb[h][s], ps[:, 4 * h + 3, :], ACT.Copy).then_inc(e_yc[h], 1)

            def y_both(e, s, turn_no, r):
                if later(turn_no):
                    act.wait_ge(e_st[s], turn_no * 16)
                y_copy(0, s, e + 1)
                with act.If(r[2] > r[1]):
                    act.wait_ge(e_st2, r[0] * 16 + 16)
                    y_copy(1, s, r[2])

            def expert_body(i, first=False, last=False):
                r = [act.value_load(rank[0:1, bass.ds(i * U + j, 1)], min_val=0, max_val=E) for j in range(2 * U)]
                if first:
                    before_first = None
                else:
                    before_first = act.value_load(rank[0:1, bass.ds(i * U - 1, 1)], min_val=0, max_val=E)
                r = [before_first] + r
                for s in range(U):
                    e = i * U + s
                    e_silu(0, e + 1)
                    with act.If(r[U + s + 1] > r[U + s]):
                        e_silu(1, r[U + s + 1])
                    if not (first and s == 0):
                        y_both(e - 1, (s - 1) % U, (i if s else i - 1), (r[s], r[U + s - 1], r[U + s]))
                if last:
                    y_both(E - 1, U - 1, i, (r[U], r[2 * U - 1], r[2 * U]))

            expert_body(0, first=True)
            expert_body(1)
            with act.Fori(2, E // U - 1) as i:
                expert_body(i)
            expert_body(E // U - 1, last=True)

        @block.vector
        def _(dve):
            V = nc.vector
            own = Steps(dve, dv)

            def later(w):
                return not isinstance(w, int) or w > 0

            def flat(a):
                return a.rearrange("p a n -> p (a n)")


            dve.wait_ge(s_dst, 16)
            V.tensor_copy(dst_f[:, :, :], dst_i[:, :, :]).then_inc(s_ef, 1)
            dve.wait_ge(s_src, 16)
            V.tensor_copy(src_f[:, :, :], src_i[:, :, :]).then_inc(s_ef, 1)
            dve.wait_ge(s_ef, 2)
            V.tensor_reduce(ends[:, 0:2], dst_f[:, :, :], AX.X, ALU.min).then_inc(s_ef, 1)
            V.tensor_reduce(ends[:, 2:4], dst_f[:, :, :], AX.X, ALU.max).then_inc(s_ef, 1)
            dve.wait_ge(s_eT, 1)
            own.mark(V.tensor_copy(edge[:, :], ps[0:EP, 6, 0:4 * EH]))
            dve.wait_ge(s_eT, 2)
            for j, op in enumerate((ALU.min, ALU.max)):
                own.mark(V.tensor_reduce(wrow[0:1, j, :], ps[0:1, 7, j * ET:(j + 1) * ET].rearrange("p (g t) -> p g t", t=G),
                                         AX.X, op))
            own.wait()
            own.mark(V.tensor_copy(wint[:, :, :], wrow[:, :, :]))
            own.wait()
            own.mark(V.tensor_single_scalar(wint[:, :, :], wint[:, :, :], 7, ALU.arith_shift_right))
            own.wait()
            own.mark(V.tensor_scalar(wcap[:, :, :], wint[:, :, :], float(NT - 1), None, ALU.min))
            own.wait()
            own.mark(V.tensor_copy(wtab_f[:, 0, :], wcap[:, 0, :]))
            own.mark(V.tensor_tensor(wtab_f[:, 1, :], wcap[:, 1, :], wcap[:, 0, :], ALU.subtract))
            own.wait()
            dve.wait_ge(s_cst, 10)
            own.mark(V.tensor_tensor_scan(wtab_f[:, 2, :], zrow1[:, 0:NG], wtab_f[:, 1, :], 0.0, ALU.add, ALU.add))
            own.wait()
            own.mark(V.tensor_tensor(wtab_f[:, 2, :], wtab_f[:, 2, :], wtab_f[:, 1, :], ALU.subtract))
            own.wait()
            V.tensor_copy(wtab[:, :, :], wtab_f[:, :, :]).then_inc(s_win, 1)
            dve.wait_ge(s_win, 1)
            dve.wait_ge(s_hot0, 2)

            dve.wait_ge(s_x, 32)
            for w in range(NT):
                own.mark(V.bn_stats(stat[:, w, :], xs[:, w, :]))
            own.wait()
            for w in range(NT):
                own.mark(V.bn_aggr(mv[:, w, :], stat[:, w, :]))
            own.wait()
            V.tensor_scalar(ve[:, :], mv[:, :, 1], EPS, None, ALU.add).then_inc(s_var, 1)
            dve.wait_ge(s_sqrt, 1)

            def inv_sqrt(r, q, root, v):
                own.mark(V.reciprocal(r, root))
                own.wait()
                own.mark(V.tensor_tensor(q, r, r, ALU.mult))
                own.wait()
                own.mark(V.tensor_tensor(q, q, v, ALU.mult))
                own.wait()
                own.mark(V.tensor_scalar(q, q, -0.5, 1.5, ALU.mult, ALU.add))
                own.wait()
                own.mark(V.tensor_tensor(r, r, q, ALU.mult))
                own.wait()

            inv_sqrt(rs[:, :], rq[:, :], sd[:, :], ve[:, :])
            for w in range(NT):
                m = V.tensor_scalar(xn[:, w, :], xs[:, w, :], mv[:, w, 0:1], rs[:, w:w + 1], ALU.subtract, ALU.mult)
                if w < NT - 1:
                    own.mark(m)
            m.then_inc(s_xn, 1)
            own.mark(V.tensor_scalar(valid[:, :], tok_f[:, :], float(N), None, ALU.is_lt))
            own.wait()
            own.mark(V.tensor_scalar(vm1[:, :], valid[:, :], 1.0, None, ALU.subtract))

            def hot_window(hot, g, w, t):
                return V.tensor_scalar(hot[:, t, :], iota_h[0:EP, bass.ds(w * P, P)],
                                       edge[:, bass.ds(ET + g * G + t, 1)], None, ALU.is_equal)

            def hot_rows(g, par):
                w = dve.value_load(wtab[0:1, 0, bass.ds(g, 1)], min_val=0, max_val=NT - 1)
                if not isinstance(g, int) or g >= 2:
                    dve.wait_ge(s_cd, g - 1)
                for t in range(G):
                    own.mark(V.tensor_scalar(hot_src[par][:, t, 0:N], iota_h[0:EP, 0:N],
                                             edge[:, bass.ds(g * G + t, 1)], None, ALU.is_equal))
                    m = hot_window(hot_dst[par], g, w, t)
                    if t < G - 1:
                        own.mark(m)
                own.wait()
                m.then_inc(s_hs, 1)

            def add_counts(w, par):
                rows = flat(counts[:, bass.ds(w, 1), :])
                return V.tensor_tensor(rows, acc[par][:, 0:NPAD], rows, ALU.add)

            def add_group(g, par):
                w = dve.value_load(wtab[0:1, 0, bass.ds(g, 1)], min_val=0, max_val=NT - 1)
                dve.wait_ge(s_cd, g + 1)
                dve.wait_ge(s_cc, g + 1)
                add_counts(w, par).then_inc(s_cc, 1)
                more = dve.value_load(wtab[0:1, 1, bass.ds(g, 1)], min_val=0, max_val=NT - 1)
                with dve.If(more > 0):
                    base = dve.value_load(wtab[0:1, 2, bass.ds(g, 1)], min_val=0, max_val=NT * NG)
                    with dve.Fori(0, NT - 1) as j:
                        with dve.If(j < more):
                            dve.wait_ge(s_cc, g + 2)
                            v = nc.s_assert_within(w + j + 1, 0, NT - 1, skip_runtime_bounds_check_because="the last window of a group is at most NT - 1")
                            for t in range(G):
                                m = hot_window(hot_more, g, v, t)
                                m.then_inc(m_hot, 1)
                            dve.wait_ge(m_cnt, base + j + 1)
                            add_counts(v, par).then_inc(m_add, 1)
                            dve.wait_ge(m_add, base + j + 1)
                            dve.sem_inc(s_past["dve"], 1)

            hot_rows(0, 0)
            hot_rows(1, 1)
            add_group(0, 0)
            own.restart()
            with dve.Fori(1, NG // 2) as i:
                hot_rows(2 * i, 0)
                add_group(2 * i - 1, 1)
                hot_rows(2 * i + 1, 1)
                add_group(2 * i, 0)
                own.restart()
            add_group(NG - 1, 1)
            dve.wait_ge(s_cc, NG + 1)

            def degree(w):
                dve.wait_ge(s_cw, w + 1)
                own.mark(V.tensor_scalar(rdeg[:, bass.ds(w, 1)], cw[:, DEG:NPAD], 1.0, None, ALU.max))
                own.wait()
                V.reciprocal(rdeg[:, bass.ds(w, 1)], rdeg[:, bass.ds(w, 1)]).then_inc(s_rdeg, 1)

            def counts_T(w):
                dve.wait_ge(s_ctT, 3 * w + 3)
                if later(w):
                    dve.wait_ge(s_ns, w)
                V.tensor_copy(flat(ct[:, 8:NT, :]), ps[:, 2, 0:(NT - 8) * P]).then_inc(s_ctV, 1)

            def norm(st, a, at):
                own.mark(V.bn_stats(st[:, 0:6], a))
                own.wait()
                own.mark(V.bn_aggr(st[:, 6:8], st[:, 0:6]))
                own.wait()
                V.tensor_scalar(st[:, 8:9], st[:, 7:8], EPS, None, ALU.add).then_inc(s_var, 1)
                dve.wait_ge(s_sqrt, at)
                inv_sqrt(st[:, 10:11], st[:, 11:12], st[:, 9:10], st[:, 8:9])

            def tile(w):
                xrow = flat(xs[:, bass.ds(w, 1), :])
                dve.wait_ge(s_xT, w + 1)
                if later(w):
                    dve.wait_ge(s_self, w)
                V.tensor_copy(flat(xw_t[:, :, :]), ps[:, 4, :]).then_inc(s_xTc, 1)
                dve.wait_ge(s_self, w + 1)
                dve.wait_ge(s_hn, w + 1)
                V.tensor_tensor(h0[:, :], ps[:, 6, :], hn[:, :], ALU.add).then_inc(s_h, 1)
                dve.wait_ge(s_h, w + 1)
                own.mark(V.tensor_tensor(h0[:, :], h0[:, :], bias_b[:, :], ALU.add))
                own.wait()
                norm(st1, h0[:, :], 2 * w + 2)
                own.mark(V.scalar_tensor_tensor(out=h1[:, :], in0=h0[:, :], scalar=st1[:, 6:7], in1=gamma_b[:, :],
                                                op0=ALU.subtract, op1=ALU.mult))
                own.wait()
                own.mark(V.scalar_tensor_tensor(out=h0[:, :], in0=h1[:, :], scalar=st1[:, 10:11], in1=beta_b[:, :],
                                                op0=ALU.mult, op1=ALU.add))
                own.wait()
                own.mark(V.tensor_tensor(xrow, xrow, h0[:, :], ALU.add))
                own.wait()
                norm(st2, xrow, 2 * w + 3)
                if later(w):
                    dve.wait_ge(s_tst, w * 16)
                V.tensor_scalar(tw[:, :], xrow, st2[:, 6:7], st2[:, 10:11], ALU.subtract, ALU.mult).then_inc(s_t, 1)

            def router(w):
                dve.wait_ge(s_tT, w + 1)
                if later(w):
                    dve.wait_ge(s_tk, w)
                V.tensor_copy(flat(tw_t[:, :, :]), ps[:, 3, :]).then_inc(s_tTc, 1)
                dve.wait_ge(s_lg, w + 1)
                V.tensor_tensor(flat(logits[:, bass.ds(w, 1), :]), ps[:, 4, 0:E], rb[:, :], ALU.add).then_inc(s_lgc, 1)

            dve.wait_ge(s_vec, 64)
            degree(0)
            counts_T(0)
            own.restart()
            with dve.Fori(1, NT) as k:
                degree(k)
                counts_T(k)
                tile(k - 1)
                router(k - 1)
                own.restart()
            tile(NT - 1)
            router(NT - 1)

            def choose(w):
                lg = flat(logits[:, bass.ds(w, 1), :])
                v = flat(v8[:, bass.ds(w, 1), :])
                ok, okm = valid[:, bass.ds(w, 1)], vm1[:, bass.ds(w, 1)]
                dve.wait_ge(s_lgc, w + 1)
                own.mark(V.tensor_copy(lgw[:, :], lg))
                own.wait()
                own.mark(V.max(v8w[:, :], lgw[:, :]))
                own.wait()
                own.mark(V.max_index(i8[:, :], v8w[:, :], lgw[:, :]))
                own.mark(V.tensor_copy(v, v8w[:, :]))
                own.wait()
                own.mark(V.tensor_copy(i6[:, :], i8[:, 0:TOPK]))
                own.wait()
                own.mark(V.tensor_scalar(i6[:, :], i6[:, :], ok, okm, ALU.mult, ALU.add))
                own.wait()
                own.mark(V.tensor_tensor(hot_e[:, :, :], iota_e[:, :].rearrange("p (a e) -> p a e", a=1).broadcast_to([P, TOPK, E]),
                                         i6[:, :].rearrange("p (k a) -> p k a", a=1).broadcast_to([P, TOPK, E]), ALU.is_equal))
                own.wait()
                if later(w):
                    dve.wait_ge(s_pre, w)
                    own.mark(V.tensor_tensor(msum[:, :], msum[:, :], mask[:, :], ALU.add))
                    own.wait()
                with nc.allow_low_precision("0 or 1"):
                    V.tensor_reduce(mask[:, :], hot_e[:, :, :].rearrange("p k e -> p e k"), AX.X, ALU.add).then_inc(s_mask, 1)

            def place(w):
                ok = valid[:, bass.ds(w, 1)]
                dve.wait_ge(s_pre, w + 1)
                own.mark(V.tensor_tensor(hot_s[:, :, :], ps[:, 4, 0:E].rearrange("p (a e) -> p a e", a=1).broadcast_to([P, TOPK, E]),
                                         hot_e[:, :, :], ALU.mult))
                own.wait()
                own.mark(V.tensor_reduce(slot[:, :], hot_s[:, :, :], AX.X, ALU.add))
                own.wait()
                own.mark(V.tensor_scalar(keep[:, :], slot[:, :], float(CAP), ok, ALU.is_lt, ALU.mult))
                own.mark(V.tensor_scalar(half[:, :], slot[:, :], float(P), None, ALU.is_ge))
                own.wait()
                own.mark(V.scalar_tensor_tensor(out=lo[:, :], in0=half[:, :], scalar=float(-P), in1=slot[:, :],
                                                op0=ALU.mult, op1=ALU.add))
                own.mark(V.scalar_tensor_tensor(out=hi[:, :], in0=i6[:, :], scalar=2.0, in1=half[:, :],
                                                op0=ALU.mult, op1=ALU.add))
                own.wait()
                own.mark(V.scalar_tensor_tensor(out=yrow[:, :], in0=hi[:, :], scalar=float(P), in1=lo[:, :],
                                                op0=ALU.mult, op1=ALU.add))
                own.wait()
                own.mark(V.scalar_tensor_tensor(out=yrow[:, :], in0=yrow[:, :], scalar=float(-ZROW), in1=keep[:, :],
                                                op0=ALU.add, op1=ALU.mult))
                own.mark(V.scalar_tensor_tensor(out=hi[:, :], in0=hi[:, :], scalar=1.0, in1=keep[:, :],
                                                op0=ALU.add, op1=ALU.mult))
                own.wait()
                own.mark(V.tensor_scalar(flat(yidx[:, bass.ds(w, 1), :]), yrow[:, :], float(ZROW), None, ALU.add))
                own.mark(V.tensor_scalar(hi[:, :], hi[:, :], -1.0, None, ALU.add))
                own.wait()
                if later(w):
                    dve.wait_ge(s_tab, w)
                for k in range(TOPK):
                    own.mark(V.tensor_scalar(hot_lo[:, k, :], iota_h[:, 0:P], lo[:, k:k + 1], tok_f[:, bass.ds(w, 1)],
                                             ALU.is_equal, ALU.mult))
                    m = V.tensor_scalar(hot_hi[:, k, :], iota_h[:, 0:P], hi[:, k:k + 1], None, ALU.is_equal)
                    if k < TOPK - 1:
                        own.mark(m)
                own.wait()
                m.then_inc(s_hl, 1)

            def hidden(w):
                dve.wait_ge(s_silu, w + 1)
                dve.wait_ge(s_up, w + 1)
                if later(w):
                    dve.wait_ge(s_hT, w)
                V.tensor_tensor(hsh[:, :], ps[:, 1, :], sg[:, :], ALU.mult).then_inc(s_hm, 1)

            def base_row(w):
                xrow = flat(xs[:, bass.ds(w, 1), :])
                dve.wait_ge(s_dw, w + 1)
                V.scalar_tensor_tensor(out=xrow, in0=ps[:, 3, :], scalar=1.0 / SH, in1=xrow,
                                       op0=ALU.mult, op1=ALU.add).then_inc(s_base, 1)

            choose(0)
            place(0)
            hidden(0)
            own.restart()
            with dve.Fori(1, NT) as w:
                choose(w)
                place(w)
                hidden(w)
                base_row(w - 1)
                own.restart()
            dve.wait_ge(s_pre, NT)
            own.mark(V.tensor_tensor(msum[:, :], msum[:, :], mask[:, :], ALU.add))
            own.wait()
            dve.sem_inc(s_mask, 1)
            dve.wait_ge(s_tab, NT + 1)
            V.tensor_copy(tokidx[:, :], ps[:, 5, 0:2 * E]).then_inc(s_tok, 1)
            dve.wait_ge(s_cnt, 1)
            own.mark(V.tensor_scalar(cnt[:, :], ps[0:1, 6, 0:E], float(P), None, ALU.is_gt))
            own.wait()
            own.mark(V.tensor_tensor_scan(rank_f[:, U:U + E], zrow1[:, :], cnt[:, :], 0.0, ALU.add, ALU.add))
            own.wait()
            V.tensor_copy(rank[:, :], rank_f[:, :]).then_inc(s_rank, 1)
            base_row(NT - 1)
            for q in (e_xTc, e_h, e_hTc):
                for h in range(2):
                    dve.sem_inc(q[h], 1)

            top = v8[:, :, 0:1]
            own.mark(V.tensor_tensor(logits[:, :, :], logits[:, :, :], top.broadcast_to([P, NT, E]), ALU.subtract))
            V.tensor_tensor(ex6[:, :, :], v8[:, :, 0:TOPK], top.broadcast_to([P, NT, TOPK]), ALU.subtract).then_inc(s_sub, 1)
            dve.wait_ge(s_exp, 2)
            own.mark(V.tensor_reduce(zsum[:, 0, :], logits[:, :, :], AX.X, ALU.add))
            own.mark(V.tensor_reduce(zsum[:, 1, :], ex6[:, :, :], AX.X, ALU.add))
            own.wait()
            own.mark(V.scalar_tensor_tensor(out=rden[:, :], in0=zsum[:, 0, :], scalar=1e-9, in1=zsum[:, 1, :],
                                            op0=ALU.mult, op1=ALU.add))
            own.wait()
            own.mark(V.reciprocal(rden[:, :], rden[:, :]))
            own.wait()
            own.mark(V.tensor_tensor(gate[:, :, :], ex6[:, :, :],
                                     rden[:, :].rearrange("p (w a) -> p w a", a=1).broadcast_to([P, NT, TOPK]), ALU.mult))
            own.wait()

            def rows_T(h, n):
                dve.wait_ge(e_xT[h], n + (U if h == 0 else 1))
                if h == 1 or later(n - 1):
                    dve.wait_ge(e_h[h], n)
                V.tensor_copy(flat(xt[h][:, :, :]), ps[:, 4 * h, :]).then_inc(e_xTc[h], 1)

            def hid(h, n):
                dve.wait_ge(e_si[h], n)
                dve.wait_ge(e_hTc[h], n)
                V.tensor_tensor(hh[h], ps[:, 4 * h + 1, F:2 * F], sil[h], ALU.mult).then_inc(e_h[h], 1)

            def hid_T(h, n):
                dve.wait_ge(e_hT[h], n)
                dve.wait_ge(e_yc[h], n)
                V.tensor_copy(flat(ht[h][:, :, :]), ps[:, 4 * h + 2, 0:F]).then_inc(e_hTc[h], 1)

            def expert_body(i, first=False, last=False):
                r = [dve.value_load(rank[0:1, bass.ds(i * U + j, 1)], min_val=0, max_val=E)
                     for j in range(2, U + (U if last else U + 1))]
                r = [None, None] + r
                if first:
                    rows_T(0, 1)
                    with dve.If(r[U] > r[U - 1]):
                        rows_T(1, r[U])
                for s in range(U):
                    e = i * U + s
                    if not (first and s == 0):
                        hid_T(0, e)
                        with dve.If(r[U + s - 1] > r[U + s - 2]):
                            hid_T(1, r[U + s - 1])
                    hid(0, e + 1)
                    with dve.If(r[U + s] > r[U + s - 1]):
                        hid(1, r[U + s])
                    if not (last and s == U - 1):
                        rows_T(0, e + 2)
                        with dve.If(r[U + s + 1] > r[U + s]):
                            rows_T(1, r[U + s + 1])
                if last:
                    hid_T(0, E)
                    with dve.If(r[2 * U - 1] > r[2 * U - 2]):
                        hid_T(1, r[2 * U - 1])

            expert_body(0, first=True)
            with dve.Fori(1, E // U - 1) as i:
                expert_body(i)
            expert_body(E // U - 1, last=True)

            for w in range(NT):
                b = w % 2
                if w >= 2:
                    dve.wait_ge(s_out[b], 16 * (w // 2))
                for k in range(TOPK):
                    dve.wait_ge(c_y[b][k], 16 * (w // 2 + 1))
                    m = V.scalar_tensor_tensor(out=oacc[b][:, :], in0=yg[b][k], scalar=gate[:, w, k:k + 1],
                                               in1=xs[:, w, :] if k == 0 else oacc[b][:, :], op0=ALU.mult, op1=ALU.add)
                    if k < TOPK - 1:
                        own.mark(m)
                        own.wait()
                m.then_inc(c_acc, 1)


_OUT = ((N, D), "float32")


def kernel(x, src, dst, L0_gnn_W_self, L0_gnn_W_neigh, L0_gnn_bias, L0_gnn_gamma, L0_gnn_beta, L0_ffn_router_w,
           L0_ffn_bias, L0_ffn_shared_w_gate, L0_ffn_shared_w_up, L0_ffn_shared_w_down, L0_ffn_w_gate, L0_ffn_w_up,
           L0_ffn_w_down):
    import numpy as np
    import concourse.bacc as bacc
    from concourse.bass_utils import run_bass_kernel_spmd

    def chunks(a):
        return a.reshape(a.shape[0] // P, P, a.shape[1]).transpose(1, 0, 2)

    def t(a):
        return np.asarray(a).T

    def rows(a):
        a = np.asarray(a)
        return a.reshape(-1, a.shape[-1]).T

    gu = np.concatenate([np.asarray(L0_ffn_w_gate), np.asarray(L0_ffn_w_up)], axis=1)
    gu = gu.transpose(0, 2, 1).reshape(E, DC, P, 2 * F).transpose(0, 2, 1, 3).reshape(E, P, DC * 2 * F)
    dn = np.asarray(L0_ffn_w_down).transpose(0, 2, 1).reshape(E, FC, P, D).transpose(0, 2, 1, 3).reshape(E, P, FC * D)
    sdn = np.asarray(L0_ffn_shared_w_down).transpose(0, 2, 1).reshape(SH * F, D)
    arrays = {
        "x": x, "src": src, "dst": dst,
        "w_self": chunks(t(L0_gnn_W_self)), "w_neigh": chunks(t(L0_gnn_W_neigh)),
        "bias": L0_gnn_bias, "gamma": L0_gnn_gamma, "beta": L0_gnn_beta,
        "router_w": chunks(t(L0_ffn_router_w)), "router_b": L0_ffn_bias,
        "shared_gu": chunks(np.concatenate([rows(L0_ffn_shared_w_gate), rows(L0_ffn_shared_w_up)], axis=1)),
        "shared_down": chunks(sdn),
        "expert_w": np.concatenate([gu, dn], axis=2),
    }
    nc = bacc.Bacc("TRN2", target_bir_lowering=False, num_devices=1)
    args = []
    for name in arrays:
        arrays[name] = np.ascontiguousarray(arrays[name])
        a = arrays[name]
        args.append(nc.dram_tensor(name, a.shape, mybir.dt.from_np(a.dtype), kind="ExternalInput").ap())
    args.append(nc.dram_tensor("out", _OUT[0], F32, kind="ExternalOutput").ap())
    gnn_moe(nc, *args)
    return run_bass_kernel_spmd(nc, [arrays], core_ids=[0]).results[0]["out"]
```

```python
from contextlib import ExitStack

import concourse.bass as bass
from concourse import mybir

F32 = mybir.dt.float32
F32R = mybir.dt.float32r
BF16 = mybir.dt.bfloat16
F16 = mybir.dt.float16
I32 = mybir.dt.int32
U32 = mybir.dt.uint32
ALU = mybir.AluOpType
ACT = mybir.ActivationFunctionType
AX = mybir.AxisListType

P = 128
N, D, E, F = 1250, 512, 64, 256
TOPK = 6
SH = 2
CAP = N * TOPK * 2 // E
NT = -(-N // P)
NPAD = NT * P
LAST = N - (NT - 1) * P
DC, FC = D // P, F // P
EPS = 1e-5
EDGES, EP = 20000, 125
ET = EDGES // EP
EH = ET // 2
G = 8
NG = ET // G
DEG = NPAD - 1
CW = -(-(N + P) // 4) * 4
NP = NT // 2
assert NG == 2 * NT
TW = D + E
ROWS = N + P
U = 4
WG = DC * 2 * F
WCOL = WG + FC * D
WPART = D * 2
assert WG == 2 * WPART and WCOL == 3 * WPART
EARLY_REST = (G * NPAD + 2 * DC * D + NT * D) - (4 * WCOL + 8 * DC * P + 4 * FC * P + 4 * F)


class Steps:

    def __init__(self, eng, sem):
        self.eng, self.sem, self.n = eng, sem, 0

    def mark(self, ins):
        ins.then_inc(self.sem, 1)
        self.n += 1

    def wait(self):
        self.eng.wait_ge(self.sem, self.n)

    def restart(self):
        if self.n:
            self.wait()
            self.eng.sem_inc(self.sem, -self.n)
            self.n = 0


class Ranks:

    def __init__(self, eng, rank, low, high):
        self.eng, self.rank, self.low, self.high = eng, rank, low, high
        self.kept = [eng.alloc_register(name=f"rank_{j}") for j in range(high - low + 1)]

    def read(self, j):
        at = self.i * U + j
        if not isinstance(at, int) or at < U + E:
            self.r[j] = self.eng.value_load(self.rank[0:1, bass.ds(at, 1)], min_val=0, max_val=E)

    def begin(self, i, first):
        self.i, self.r = i, {}
        for j, reg in zip(range(self.low, self.high + 1), self.kept):
            if first:
                self.read(j)
            else:
                self.r[j] = self.eng.snap(reg, min_val=0, max_val=E)
        return self.r

    def next(self, s):
        self.read(self.high + 1 + s)

    def hand_over(self):
        for j, reg in zip(range(self.low, self.high + 1), self.kept):
            self.eng.reg_mov(reg, self.r[j + U])


def gnn_moe(nc, x, src, dst, w_self, w_neigh, bias, gamma, beta, router_w, router_b,
            shared_gu, shared_down, expert_w, out):
    ctx = ExitStack()
    with ctx:
        def sb(name, shape, dt):
            return ctx.enter_context(nc.sbuf_tensor(name, shape, dt))

        def sem(name):
            return ctx.enter_context(nc.semaphore(name))

        t_dram = nc.dram_tensor("t_rows", [ROWS, TW], F32).ap()

        ps = ctx.enter_context(nc.psum_tensor("ps", [P, 8, 512], F32))
        acc = [ps[:, 3 * b:3 * b + 3, :].rearrange("p b n -> p (b n)") for b in range(2)]

        with ExitStack() as early:
            def sb_early(name, shape, dt):
                return early.enter_context(nc.sbuf_tensor(name, shape, dt))

            hot_all = sb_early("hot_all", [P, 2, G, NPAD], BF16)
            ws = sb_early("ws", [P, DC, D], F32)
            wn = sb_early("wn", [P, DC, D], F32)
            xs = sb_early("xs", [P, NT, D], F32)
        hot_src = [hot_all[0:EP, b, :, :] for b in range(2)]
        w_hi = [sb(f"w_hi{b}", [P, WCOL], F32R) for b in range(2)]
        w_lo = [sb(f"w_lo{b}", [P, WCOL], F32R) for b in range(2)]
        xt = [[[sb(f"xt_{part}{h}_{b}", [P, DC, P], F32R) for b in range(2)] for h in range(2)] for part in ("hi", "lo")]
        ht = [[sb(f"ht_{part}{h}", [P, FC, P], F32R) for h in range(2)] for part in ("hi", "lo")]
        sil = [sb(f"sil{h}", [P, F], F32) for h in range(2)]
        hh = [sb(f"hh{h}", [P, F], F32) for h in range(2)]
        sb("early_rest", [P, EARLY_REST], F32)

        iota_h = sb("iota_h", [P, CW], F16)
        iota_e = sb("iota_e", [P, E], F32)
        ident = sb("ident", [P, P], F32)
        before = sb("before", [P, P], BF16)
        ones = sb("ones", [P, P], BF16)
        zero_h = sb("zero_h", [P, P], F16)
        zrows = sb("zrows", [P, TW], F32)
        tok_f = sb("tok_f", [P, NT], F32)
        tok1_f = sb("tok1_f", [P, NT], F32)
        dump_f = sb("dump_f", [P, 1], F32)
        valid = sb("valid", [P, NT], F32)
        rw = sb("rw", [P, DC, E], F32)
        rb = sb("rb", [P, E], F32)
        bias_b = sb("bias_b", [P, D], F32)
        gamma_b = sb("gamma_b", [P, D], F32)
        beta_b = sb("beta_b", [P, D], F32)
        xn = sb("xn", [P, NT, D], F32)
        src_i, dst_i = (xn[0:EH, q, 0:2 * EP].bitcast(I32).rearrange("t (h p) -> t h p", h=2) for q in range(2))
        src_f, dst_f = (xn[0:EH, q, 0:2 * EP].rearrange("t (h p) -> t h p", h=2) for q in range(2, 4))
        ends = sb("ends", [EH, 4], F32)
        edge = sb("edge", [EP, 4 * EH], F32)
        wrow = sb("wrow", [1, 2, NG], F32)
        wint = sb("wint", [1, 2, NG], I32)
        wtab_f = sb("wtab_f", [1, 3, NG], F32)
        zrow1 = sb("zrow1", [1, E], F32)
        wtab = sb("wtab", [1, 3, NG], I32)
        hot_dst = [sb(f"hot_dst{b}", [EP, G, P], BF16) for b in range(2)]
        hot_more = sb("hot_more", [EP, G, P], BF16)
        dist = sb("dist", [EP, G, P], BF16)
        counts = sb("counts", [P, NT, CW], F32)
        stat = sb("stat", [P, NT, 6], F32)
        mv = sb("mv", [P, NT, 2], F32)
        ve = sb("ve", [P, NT], F32)
        sd = sb("sd", [P, NT], F32)
        rs = sb("rs", [P, NT], F32)
        rq = sb("rq", [P, NT], F32)
        xw = sb("xw", [P, D], F32)
        xw_t = sb("xw_t", [P, DC, P], F32)
        deg = sb("deg", [P, NT], F32)
        rdeg = sb("rdeg", [P, NT], F32)
        over = hot_all[:, :, :, :].rearrange("p b t n -> p (b t n)").bitcast(F32)
        taken = [0]

        def place_over(words):
            taken[0] += words
            assert taken[0] <= G * NPAD
            return over[:, taken[0] - words:taken[0]]

        wsg = place_over(DC * 2 * D).rearrange("p (c n) -> p c n", c=DC)
        nsum_t = place_over(DC * 2 * P).rearrange("p (c m) -> p c m", c=DC)
        empty = place_over(2 * E)
        h0 = place_over(D)
        h1 = place_over(D)
        tw = place_over(D)
        tw_t = place_over(D).rearrange("p (c m) -> p c m", c=DC)
        ct = place_over(NT * P).rearrange("p (q m) -> p q m", q=NT)
        cw = place_over(NPAD)
        st1 = sb("st1", [P, 16], F32)
        st2 = sb("st2", [P, 16], F32)
        t_t = sb("t_t", [P, NT, D], F32)
        logits = sb("logits", [P, NT, E], F32)
        wsd = ws
        tt2 = [xw_t, tw_t]
        sg, hsh = h0, h1
        hsh_t = nsum_t.rearrange("p c m -> p (c m)")[:, 0:D].rearrange("p (c m) -> p c m", c=DC)
        v8 = sb("v8", [P, NT, 8], F32)
        lgw = sb("lgw", [P, E], F32)
        v8w = sb("v8w", [P, 8], F32)
        i8 = sb("i8", [P, 8], U32)
        i6 = sb("i6", [P, TOPK], F32)
        i6_all = sb("i6_all", [P, NT, TOPK], F32)
        ctf = ct[:, :, :].rearrange("p a n -> p (a n)")
        hot_e = ctf[:, 0:TOPK * E].rearrange("p (k e) -> p k e", k=TOPK)
        hot_s = ctf[:, TOPK * E:2 * TOPK * E].rearrange("p (k e) -> p k e", k=TOPK)
        mask = sb("mask", [P, E], BF16)
        msum = sb("msum", [P, E], BF16)
        slot = sb("slot", [P, TOPK], F32)
        keep = sb("keep", [P, TOPK], F32)
        half = sb("half", [P, TOPK], F32)
        lo = sb("lo", [P, TOPK], F32)
        hi = sb("hi", [P, TOPK], F32)
        vm1 = sb("vm1", [P, NT], F32)
        ex6 = sb("ex6", [P, NT, TOPK], F32)
        zsum = sb("zsum", [P, 2, NT], F32)
        rden = sb("rden", [P, NT], F32)
        gates = sb("gates", [P, NT, E], F32)
        hot_w = TOPK * P // 2
        hot_lo, hot_hi = (cw[:, q * hot_w:(q + 1) * hot_w].bitcast(F16).rearrange("p (k m) -> p k m", k=TOPK)
                          for q in range(2))
        tokidx = sb("tokidx", [P, 2 * E], I32)
        cnt = sb("cnt", [1, E], F32)
        rank_f = sb("rank_f", [1, U + E + U], F32)
        rank = sb("rank", [1, U + E + U], I32)
        cflat = counts[:, :, :].rearrange("p w n -> p (w n)")
        wbuf = [cflat[:, s * WCOL:(s + 1) * WCOL] for s in range(U)]
        idxb = [[sb(f"idx{h}_{s}", [P, 1], I32) for s in range(U)] for h in range(2)]
        idxa = [sb(f"idx_add{h}", [P, 1], I32) for h in range(2)]
        kept = [[sb(f"kept{h}_{s}", [P, 1], F32) for s in range(U)] for h in range(2)]
        xflat = xn[:, :, :].rearrange("p w n -> p (w n)")
        gx = [[xflat[:, (U * h + s) * TW:(U * h + s + 1) * TW] for s in range(U)] for h in range(2)]
        yb = [[t_t[:, 2 * h + b, :] for b in range(2)] for h in range(2)]

        s_src, s_dst, s_x, s_w, s_wn, s_vec, s_rw = (sem(n) for n in (
            "src_in", "dst_in", "x_in", "w_self_in", "w_neigh_in", "vectors_in", "router_in"))
        s_gu, s_dn = sem("shared_gu_in"), sem("shared_down_in")
        s_cst = sem("consts_set")
        s_idt = sem("ident_zeroed")
        s_hot0 = sem("hot_src_set")
        s_xpad = sem("x_pad_zeroed")
        dv = sem("dve_steps")
        s_past = {n: sem(f"past_{n}") for n in ("dve", "pe", "sp", "pool", "act")}
        s_ef = sem("edges_float")
        s_eT = sem("edges_transposed")
        s_win = sem("windows_known")
        s_hs, s_hd = sem("hot_src_ready"), sem("hot_dst_ready")
        s_dist = sem("distances_ready")
        s_cd = sem("group_counted")
        s_cc = sem("counts_current")
        m_hot, m_cnt, m_add = sem("more_hot_ready"), sem("more_counted"), sem("more_added")
        s_xn = sem("x_normed")
        s_xw, s_xT, s_xTc = sem("x_staged"), sem("x_T"), sem("x_T_copied")
        s_self, s_selfc = sem("self_projected"), sem("self_copied")
        s_deg, s_rdeg = sem("degrees_turned"), sem("degrees_known")
        s_ns, s_nsc = sem("neigh_summed"), sem("neigh_copied")
        s_nb, s_h = sem("neigh_projected"), sem("neigh_added")
        s_var, s_sqrt = sem("variance_ready"), sem("sqrt_ready")
        s_t, s_tst = sem("t_ready"), sem("t_stored")
        s_tT, s_tTc, s_lg, s_lgc = sem("t_T"), sem("t_T_copied"), sem("logits_done"), sem("logits_copied")
        s_tk = sem("t_T_kept")
        s_tt2 = sem("t_T_staged")
        s_ga, s_up, s_silu, s_hm = sem("gate_done"), sem("up_done"), sem("silu_done"), sem("hidden_done")
        s_hT, s_hTc, s_dw, s_base = sem("hidden_T"), sem("hidden_T_copied"), sem("down_done"), sem("base_ready")
        s_mask, s_pre = sem("mask_ready"), sem("prefix_done")
        s_exp, s_gate, s_gst = sem("exps_done"), sem("gates_ready"), sem("gates_stored")
        s_z = sem("zrows_set")
        s_rest = sem("spare_rows_zeroed")
        s_bst = sem("base_stored")
        s_hl, s_tab, s_cnt = sem("table_hot"), sem("table_added"), sem("tokens_counted")
        s_rank, s_tok = sem("rank_known"), sem("tokens_listed")
        e_w = [sem(f"expert_w_in{s}") for s in range(U)]
        e_wh, e_wl = sem("weights_high"), sem("weights_low")
        e_idx = sem("expert_idx_copied")
        e_gx = [sem(f"rows_in{s}") for s in range(U)]
        e_gx2 = sem("second_rows_in")
        e_xT = sem("rows_T"), sem("second_rows_T")
        e_xh = sem("rows_T_high"), sem("second_rows_T_high")
        e_xl = sem("rows_T_low"), sem("second_rows_T_low")
        e_g = sem("gates_kept"), sem("second_gates_kept")
        e_gu = sem("gate_up"), sem("second_gate_up")
        e_si = sem("silu"), sem("second_silu")
        e_h = sem("hidden"), sem("second_hidden")
        e_hT = sem("hid_T"), sem("second_hid_T")
        e_hh = sem("hid_T_high"), sem("second_hid_T_high")
        e_hl = sem("hid_T_low"), sem("second_hid_T_low")
        e_y = sem("y"), sem("second_y")
        e_yc = sem("y_scaled"), sem("second_y_scaled")
        e_sc = sem("y_added")

        block = ctx.enter_context(nc.Block())

        @block.sync
        def _(sp):
            sp.dma_start(dst_i[:, :, :], dst.rearrange("(h t p) -> t h p", h=2, p=EP)).then_inc(s_dst, 16)
            sp.dma_start(src_i[:, :, :], src.rearrange("(h t p) -> t h p", h=2, p=EP)).then_inc(s_src, 16)
            sp.dma_start(xs[:, 0:NT - 1, :], x[0:(NT - 1) * P, :].rearrange("(t p) d -> p t d", p=P)).then_inc(s_x, 16)
            sp.wait_ge(s_xpad, 1)
            sp.dma_start(xs[0:LAST, NT - 1, :], x[(NT - 1) * P:N, :]).then_inc(s_x, 16)
            sp.dma_start(ws[:, :, :], w_self).then_inc(s_w, 16)
            sp.dma_start(wn[:, :, :], w_neigh).then_inc(s_wn, 16)
            sp.dma_start(rw[:, :, :], router_w).then_inc(s_rw, 16)
            for buf, vec in ((bias_b, bias), (gamma_b, gamma), (beta_b, beta), (rb, router_b)):
                v = vec.rearrange("(a n) -> a n", a=1)
                sp.dma_start(buf[:, :], v.broadcast_to([P, v.shape[1]])).then_inc(s_vec, 16)
            sp.wait_ge(s_z, 1)
            sp.dma_start(t_dram[NPAD:ROWS, :], zrows[0:ROWS - NPAD, :]).then_inc(s_rest, 16)
            sp.dma_start(out[NPAD:ROWS, :], zrows[0:ROWS - NPAD, 0:D]).then_inc(s_rest, 16)
            sp.wait_ge(s_cc, NG + 1)
            sp.dma_start(wsg[:, :, :], shared_gu).then_inc(s_gu, 16)
            sp.wait_ge(s_self, NT)
            sp.dma_start(wsd[:, :, :], shared_down).then_inc(s_dn, 16)
            with sp.Fori(0, NT) as w:
                sp.wait_ge(s_t, w + 1)
                sp.dma_start(t_dram[bass.ds(w * P, P), 0:D], tw).then_inc(s_tst, 16)
            sp.wait_ge(s_ns, 2 * NP)
            for s in range(U):
                sp.dma_start(wbuf[s], expert_w[s]).then_inc(e_w[s], 16)

            sp.wait_ge(s_gate, 1)
            sp.dma_start(t_dram[0:NPAD, D:TW].rearrange("(w p) e -> p w e", p=P), gates[:, :, :]).then_inc(s_gst, 16)
            with sp.Fori(0, NT) as w:
                sp.wait_ge(s_base, w + 1)
                sp.dma_start(out[bass.ds(w * P, P), :], xs[:, bass.ds(w, 1), :].rearrange("p a n -> p (a n)")).then_inc(s_bst, 16)
            with sp.Fori(0, E // U - 1) as i:
                for s in range(U):
                    sp.wait_ge(e_wl, 3 * (i * U + s) + 3)
                    sp.dma_start(wbuf[s], expert_w[bass.ds((i + 1) * U + s, 1), :, :].rearrange("a p n -> (a p) n")
                                 ).then_inc(e_w[s], 16)
            second = sp.value_load(rank[0:1, U + E - 1:U + E], min_val=0, max_val=E)
            sp.wait_ge(e_sc, 16 * E + second * 16)
            sp.sem_inc(s_past["sp"], 1)

        @block.gpsimd
        def _(pool):
            g = nc.gpsimd
            g.memset(xs[96:P, NT - 1, :], 0.0).then_inc(s_xpad, 1)
            pool.wait_ge(s_xpad, 1)
            g.memset(ident[:, :], 0.0).then_inc(s_idt, 1)
            g.memset(before[:, :], 1.0).then_inc(s_idt, 1)
            pool.wait_ge(s_idt, 2)
            g.affine_select(out=ident[:, :], in_=ident[:, :], compare_op=ALU.not_equal, fill=1.0, base=0,
                            pattern=[[-1, P]], channel_multiplier=1).then_inc(s_cst, 1)
            g.affine_select(out=before[:, :], in_=before[:, :], compare_op=ALU.is_gt, fill=0.0, base=0,
                            pattern=[[1, P]], channel_multiplier=-1).then_inc(s_cst, 1)
            g.iota(iota_h[:, :], [[1, CW]], base=0, channel_multiplier=0,
                   allow_small_or_imprecise_dtypes=True).then_inc(s_cst, 1)
            for b in range(2):
                g.memset(hot_src[b][:, :, N:NPAD], 0.0).then_inc(s_idt, 1)
            pool.wait_ge(s_idt, 4)
            for b in range(2):
                g.memset(hot_src[b][:, :, DEG:NPAD], 1.0).then_inc(s_hot0, 1)
            g.memset(counts[:, :, :], 0.0).then_inc(s_cc, 1)
            g.iota(iota_e[:, :], [[1, E]], base=0, channel_multiplier=0,
                   allow_small_or_imprecise_dtypes=True).then_inc(s_cst, 1)
            g.iota(tok_f[:, :], [[P, NT]], base=0, channel_multiplier=1,
                   allow_small_or_imprecise_dtypes=True).then_inc(s_cst, 1)
            g.iota(tok1_f[:, :], [[P, NT]], base=1, channel_multiplier=1,
                   allow_small_or_imprecise_dtypes=True).then_inc(s_cst, 1)
            g.iota(dump_f[:, :], [[1, 1]], base=N + 1, channel_multiplier=1,
                   allow_small_or_imprecise_dtypes=True).then_inc(s_cst, 1)
            g.memset(ones[:, :], 1.0).then_inc(s_cst, 1)
            g.memset(zero_h[:, :], 0.0).then_inc(s_cst, 1)
            g.memset(msum[:, :], 0.0).then_inc(s_cst, 1)
            g.memset(zrow1[:, :], 0.0).then_inc(s_cst, 1)
            g.memset(rank_f[:, :], 0.0).then_inc(s_cst, 1)
            g.memset(zrows[:, :], 0.0).then_inc(s_z, 1)

            pool.wait_ge(s_xn, 1)
            g.tensor_copy(xw[:, :], xn[:, 0, :]).then_inc(s_xw, 1)
            with pool.Fori(1, NT) as w:
                pool.wait_ge(s_xT, w)
                g.tensor_copy(xw[:, :], xn[:, bass.ds(w, 1), :].rearrange("p a n -> p (a n)")).then_inc(s_xw, 1)
            with pool.Fori(0, NT) as w:
                pool.wait_ge(s_tTc, w + 1)
                g.tensor_copy(t_t[:, bass.ds(w, 1), :].rearrange("p a n -> p (a n)"),
                              tw_t.rearrange("p c m -> p (c m)")).then_inc(s_tk, 1)

            pool.wait_ge(s_tst, 16 * NT)
            pool.wait_ge(s_gst, 16)
            pool.wait_ge(s_rest, 32)
            pool.wait_ge(s_tok, 1)
            pool.wait_ge(s_rank, 1)

            def gather(e, s, h, done):
                g.tensor_copy(idxb[h][s][:, :], tokidx[:, bass.ds(2 * e + h, 1)]).then_inc(e_idx, 1)
                pool.wait_ge(e_idx, 1)
                pool.sem_inc(e_idx, -1)
                g.indirect_dma_start(gx[h][s], None, t_dram, bass.IndirectOffsetOnAxis(ap=idxb[h][s][:, :], axis=0)
                                     ).then_inc(done, 16)

            def gather_both(e, s, r0, r1):
                gather(e, s, 0, e_gx[s])
                with pool.If(r1 > r0):
                    with pool.If(r0 > 0):
                        pool.wait_ge(e_gx2, r0 * 16)
                        pool.sem_inc(s_past["pool"], 1)
                    gather(e, s, 1, e_gx2)

            def add(e, s, h):
                g.tensor_copy(idxa[h][:, :], tokidx[:, bass.ds(2 * e + h, 1)]).then_inc(e_idx, 1)
                pool.wait_ge(e_idx, 1)
                pool.sem_inc(e_idx, -1)
                g.indirect_dma_start(out, bass.IndirectOffsetOnAxis(ap=idxa[h][:, :], axis=0), yb[h][s % 2], None,
                                     compute_op=ALU.add).then_inc(e_sc, 16)

            def y_there(e, r0, r1):
                pool.wait_ge(e_yc[0], e + 2)
                pool.sem_inc(s_past["pool"], 1)
                with pool.If(r1 > r0):
                    pool.wait_ge(e_yc[1], r1 + 1)
                    pool.sem_inc(s_past["pool"], 1)

            def add_both(e, s, r0, r1):
                if not (isinstance(e, int) and e == 0):
                    pool.wait_ge(e_sc, (e + r0) * 16)
                pool.sem_inc(s_past["pool"], 1)
                add(e, s, 0)
                with pool.If(r1 > r0):
                    add(e, s, 1)

            for s in range(U):
                r0, r1 = (pool.value_load(rank[0:1, U + s - 1 + j:U + s + j], min_val=0, max_val=E) for j in range(2))
                gather_both(s, s, r0, r1)
            pool.wait_ge(s_bst, 16 * NT)

            def step(e, s, r, i):
                if i is not None:
                    pool.wait_ge(e_xT[0], e + 1 - U)
                    pool.wait_ge(e_g[0], e + 1 - U)
                    pool.sem_inc(s_past["pool"], 1)
                    with pool.If(r[2] > r[1]):
                        pool.wait_ge(e_g[1], r[2])
                        pool.sem_inc(s_past["pool"], 1)
                    gather_both(e, s, r[U + 1], r[U + 2])
                if not (isinstance(e, int) and e == U):
                    y_there(e - U - 1, r[0], r[1])
                    add_both(e - U - 1, (s - 1) % U, r[0], r[1])

            ranks = Ranks(pool, rank, -2, U)

            def expert_body(i, first=False):
                r = ranks.begin(i, first)
                for s in range(U):
                    step(i * U + s, s, [r.get(j) for j in range(s - 2, U + s + 1)], i)
                    ranks.next(s)
                ranks.hand_over()

            expert_body(1, first=True)
            with pool.Fori(2, E // U) as i:
                expert_body(i)
            r = [pool.value_load(rank[0:1, E + j:E + j + 1], min_val=0, max_val=E) for j in range(-2, U)]
            for s in range(U + 1):
                step(E + s, s, r[s:s + 2], None)

        @block.tensor
        def _(pe):
            T = nc.tensor
            pe.wait_ge(s_cst, 1)
            pe.wait_ge(s_ef, 2)
            for q, a in enumerate((src_f, src_f, dst_f, dst_f)):
                m = T.transpose(ps[0:EP, 6, q * EH:(q + 1) * EH], a[:, q % 2, :], ident[0:EH, 0:EH])
            m.then_inc(s_eT, 1)
            pe.wait_ge(s_ef, 4)
            for q in range(4):
                m = T.transpose(ps[0:1, 7, q * EH:(q + 1) * EH], ends[:, q:q + 1], ident[0:EH, 0:EH])
            m.then_inc(s_eT, 1)

            def count(par, hot):
                for q in range(NT):
                    for t in range(G):
                        m = T.matmul(acc[par][:, q * P:(q + 1) * P], hot_src[par][:, t, q * P:(q + 1) * P], hot[:, t, :],
                                     start=(t == 0), stop=(t == G - 1))
                return m

            def group(g, par):
                pe.wait_ge(s_hs, g + 1)
                pe.wait_ge(s_hd, g + 1)
                if not isinstance(g, int) or g >= 2:
                    pe.wait_ge(s_cc, g)
                count(par, hot_dst[par]).then_inc(s_cd, 1)
                more = pe.value_load(wtab[0:1, 1, bass.ds(g, 1)], min_val=0, max_val=NT - 1)
                with pe.If(more > 0):
                    base = pe.value_load(wtab[0:1, 2, bass.ds(g, 1)], min_val=0, max_val=NT * NG)
                    with pe.Fori(0, NT - 1) as j:
                        with pe.If(j < more):
                            pe.wait_ge(s_cc, g + 2)
                            pe.wait_ge(m_hot, (base + j + 1) * G)
                            count(par, hot_more).then_inc(m_cnt, 1)
                            pe.wait_ge(m_add, base + j + 1)
                            pe.sem_inc(s_past["pe"], 1)

            def turn(bank, a, done):
                for c in range(DC):
                    m = T.transpose(ps[:, bank, c * P:(c + 1) * P], a[:, c * P:(c + 1) * P], ident[:, :])
                m.then_inc(done, 1)

            def project(bank, a, wt, done, n=D):
                for c in range(DC):
                    m = T.matmul(ps[:, bank, 0:n], a[:, c, :], wt[:, c, :], start=(c == 0), stop=(c == DC - 1))
                m.then_inc(done, 1)

            def x_turn(w):
                pe.wait_ge(s_xw, w + 1)
                if not isinstance(w, int) or w:
                    pe.wait_ge(s_xTc, w)
                turn(6, xw, s_xT)

            def self_project(w):
                pe.wait_ge(s_xTc, w + 1)
                if not isinstance(w, int) or w:
                    pe.wait_ge(s_selfc, w)
                project(7, xw_t, ws, s_self)

            pe.wait_ge(s_hot0, 2)
            pe.wait_ge(s_win, 1)
            for g in range(2):
                group(g, g)
            pe.wait_ge(s_w, 16)
            with pe.Fori(1, NT) as i:
                x_turn(i - 1)
                group(i * 2, 0)
                self_project(i - 1)
                group(i * 2 + 1, 1)
            x_turn(NT - 1)
            self_project(NT - 1)

            pe.wait_ge(s_cc, NG + 1)
            pe.wait_ge(s_selfc, NT)
            for w in range(NT):
                m = T.matmul(ps[:, 3, w:w + 1], counts[:, NT - 1, w * P:(w + 1) * P], ident[:, P - 1:P], start=True, stop=True)
            m.then_inc(s_deg, 1)

            def neigh(k, half):
                if not isinstance(k, int) or k:
                    pe.wait_ge(s_nsc, 2 * k + half - 1)
                for c in (2 * half, 2 * half + 1):
                    for q in range(NT):
                        m = T.matmul(ps[:, 5 + half, (c % 2) * 2 * P:(c % 2 + 1) * 2 * P], xn[:, q, c * P:(c + 1) * P],
                                     counts[:, q, bass.ds(k * 2 * P, 2 * P)], start=(q == 0), stop=(q == NT - 1))
                m.then_inc(s_ns, 1)

            def neigh_project(w, side):
                if side == 0:
                    pe.wait_ge(s_nsc, w + 2)
                if not isinstance(w, int) or w:
                    pe.wait_ge(s_h, w)
                project(7, nsum_t[:, :, side * P:(side + 1) * P], wn, s_nb)

            def t_route(w):
                pe.wait_ge(s_t, w + 1)
                turn(3, tw, s_tT)
                pe.wait_ge(s_tTc, w + 1)
                project(4, tw_t, rw, s_lg, E)

            pe.wait_ge(s_wn, 16)
            pe.wait_ge(s_rw, 16)
            neigh(0, 0)
            neigh(0, 1)
            pe.wait_ge(s_rdeg, 1)
            with pe.Fori(1, NP) as k:
                for side in range(2):
                    neigh_project(2 * k - 2 + side, side)
                    neigh(k, side)
                    t_route(2 * k - 2 + side)
            for side in range(2):
                neigh_project(NT - 2 + side, side)
                t_route(NT - 2 + side)

            def down(w):
                pe.wait_ge(s_hTc, w + 1)
                if not isinstance(w, int) or w:
                    pe.wait_ge(s_base, w)
                project(3, hsh_t, wsd, s_dw)

            def hidden_T(w):
                pe.wait_ge(s_hm, w + 1)
                turn(2, hsh, s_hT)

            def prefix(w):
                pe.wait_ge(s_mask, w + 1)
                T.matmul(ps[:, 4, 0:E], before[:, :], mask[:, :], start=True, stop=False)
                T.matmul(ps[:, 4, 0:E], ones[:, :], msum[:, :], start=False, stop=True).then_inc(s_pre, 1)

            def table(w):
                pe.wait_ge(s_hl, w + 1)
                for k in range(TOPK):
                    m = T.matmul(ps[:, 5, 0:P], hot_lo[:, k, :], hot_hi[:, k, :], start=False, stop=False,
                                 skip_group_check=True)
                m.then_inc(s_tab, 1)

            def gate_(w, par):
                pe.wait_ge(s_tt2, w + 1)
                if not isinstance(w, int) or w:
                    pe.wait_ge(s_silu, w)
                project(0, tt2[par], wsg[:, :, 0:D], s_ga)

            def up_(w, par):
                if not isinstance(w, int) or w:
                    pe.wait_ge(s_hm, w)
                project(1, tt2[par], wsg[:, :, D:2 * D], s_up)

            pe.wait_ge(s_gu, 16)
            pe.wait_ge(s_dn, 16)
            pe.wait_ge(s_cst, 12)
            pe.wait_ge(s_lgc, NT)
            T.matmul(ps[:, 5, 0:P], zero_h[:, :], zero_h[:, :], start=True, stop=False, skip_group_check=True)

            def shared(w, par, first=False):
                gate_(w, par)
                if not first:
                    hidden_T(w - 1)
                prefix(w)
                up_(w, par)
                if not first:
                    down(w - 1)
                    table(w - 1)

            shared(0, 0, True)
            shared(1, 1)
            with pe.Fori(1, NT // 2) as i:
                shared(i * 2, 0)
                shared(i * 2 + 1, 1)
            table(NT - 1)
            T.matmul(ps[:, 5, 0:P], zero_h[:, :], zero_h[:, :], start=False, stop=True,
                     skip_group_check=True).then_inc(s_tab, 1)
            pe.wait_ge(s_mask, NT + 1)
            T.matmul(ps[0:1, 6, 0:E], ones[:, 0:1], msum[:, :], start=True, stop=True).then_inc(s_cnt, 1)
            hidden_T(NT - 1)
            down(NT - 1)

            pe.wait_ge(s_base, NT)
            pe.wait_ge(s_tok, 1)
            pe.wait_ge(s_rank, 1)
            for h in range(2):
                for q in (e_gu, e_hT, e_y):
                    pe.sem_inc(q[h], 1)

            def rows_T(h, s, n):
                pe.wait_ge(e_xl[h], n)
                for c in range(DC):
                    m = T.transpose(ps[:, 4 * h, c * P:(c + 1) * P], gx[h][s][:, c * P:(c + 1) * P], ident[:, :])
                m.then_inc(e_xT[h], 1)

            def three_passes(bank, a, b, chunks, column):
                for c in range(chunks):
                    for p, (i, j) in enumerate(((0, 0), (0, 1), (1, 0))):
                        m = T.matmul(ps[:, bank, :], a[i][:, c, :], b[j][:, column + c * D:column + (c + 1) * D],
                                     start=(c == 0 and p == 0), stop=(c == chunks - 1 and p == 2))
                return m

            def gate_up(h, s, n):
                pe.wait_ge(e_xl[h], n + 1)
                pe.wait_ge(e_h[h], n)
                three_passes(4 * h + 1, [x[h][s % 2] for x in xt], [w_hi[s % 2], w_lo[s % 2]], DC, 0).then_inc(e_gu[h], 1)

            def hid_T(h, n):
                pe.wait_ge(e_h[h], n + 1)
                pe.wait_ge(e_hl[h], n)
                for c in range(FC):
                    m = T.transpose(ps[:, 4 * h + 2, c * P:(c + 1) * P], hh[h][:, c * P:(c + 1) * P], ident[:, :])
                m.then_inc(e_hT[h], 1)

            def down_y(h, s, n):
                pe.wait_ge(e_hl[h], n + 1)
                pe.wait_ge(e_yc[h], n)
                three_passes(4 * h + 3, [x[h] for x in ht], [w_hi[s % 2], w_lo[s % 2]], FC, WG).then_inc(e_y[h], 1)

            def rows_T_both(e, s, turn_no, r0, r1):
                pe.wait_ge(e_gx[s], turn_no * 16)
                rows_T(0, s, e + 1)
                with pe.If(r1 > r0):
                    pe.wait_ge(e_gx2, r1 * 16)
                    rows_T(1, s, r1)

            def down_both(e, s, r0, r1):
                pe.wait_ge(e_wl, 3 * e + 3)
                down_y(0, s, e + 1)
                with pe.If(r1 > r0):
                    down_y(1, s, r1)

            ranks = Ranks(pe, rank, U - 2, U + 1)

            def expert_body(i, first=False, last=False):
                r = ranks.begin(i, first)
                if first:
                    rows_T_both(0, 0, 1, r[U - 1], r[U])
                for s in range(U):
                    e = i * U + s
                    if not (last and s == U - 1):
                        rows_T_both(e + 1, (s + 1) % U, i + 1 + (s + 1) // U, r[U + s], r[U + s + 1])
                    pe.wait_ge(e_wl, 3 * e + 2)
                    gate_up(0, s, e + 1)
                    ranks.next(s)
                    with pe.If(r[U + s] > r[U + s - 1]):
                        gate_up(1, s, r[U + s])
                    if not (first and s == 0):
                        down_both(e - 1, (s - 1) % U, r[U + s - 2], r[U + s - 1])
                    hid_T(0, e + 1)
                    with pe.If(r[U + s] > r[U + s - 1]):
                        hid_T(1, r[U + s])
                if last:
                    down_both(E - 1, U - 1, r[2 * U - 2], r[2 * U - 1])
                else:
                    ranks.hand_over()

            expert_body(0, first=True)
            with pe.Fori(1, E // U - 1) as i:
                expert_body(i)
            expert_body(E // U - 1, last=True)

        @block.scalar
        def _(act):
            A = nc.scalar

            def later(w):
                return not isinstance(w, int) or w > 0

            def flat(a):
                return a.rearrange("p a n -> p (a n)")

            def hot_window(g, par):
                w = act.value_load(wtab[0:1, 0, bass.ds(g, 1)], min_val=0, max_val=N - 1)
                if g is not None and (not isinstance(g, int) or g >= 1):
                    act.wait_ge(s_hd, g)
                for t in range(G):
                    m = A.activation(dist[:, t, :], iota_h[0:EP, bass.ds(w, P)], ACT.Abs, scale=-1.0,
                                     bias=edge[:, bass.ds(ET + g * G + t, 1)])
                m.then_inc(s_dist, 1)
                act.wait_ge(s_dist, g + 1)
                if not isinstance(g, int) or g >= 2:
                    act.wait_ge(s_cd, g - 1)
                A.activation(hot_dst[par][:, :, :], dist[:, :, :], ACT.Relu, scale=-1.0, bias=1.0).then_inc(s_hd, 1)

            def x_T(w):
                act.wait_ge(s_xT, w + 1)
                if later(w):
                    act.wait_ge(s_self, w)
                A.activation(flat(xw_t[:, :, :]), ps[:, 6, :], ACT.Copy).then_inc(s_xTc, 1)

            act.wait_ge(s_win, 1)
            act.wait_ge(s_cst, 3)
            hot_window(0, 0)
            hot_window(1, 1)
            act.wait_ge(s_var, 1)
            A.activation(sd[:, :], ve[:, :], ACT.Sqrt).then_inc(s_sqrt, 1)
            with act.Fori(1, NT) as i:
                hot_window(2 * i, 0)
                x_T(i - 1)
                hot_window(2 * i + 1, 1)
            x_T(NT - 1)

            def neigh(k, half):
                act.wait_ge(s_ns, 2 * k + half + 1)
                if later(k):
                    act.wait_ge(s_nb, 2 * k)
                A.activation(nsum_t[:, 2 * half:2 * half + 2, :].rearrange("p c m -> p (c m)"), ps[:, 5 + half, :], ACT.Copy
                             ).then_inc(s_nsc, 1)

            def roots(w):
                for j, st in enumerate((st1, st2)):
                    act.wait_ge(s_var, 2 * w + j + 2)
                    A.activation(st[:, 9:10], st[:, 8:9], ACT.Sqrt).then_inc(s_sqrt, 1)

            neigh(0, 0)
            neigh(0, 1)
            with act.Fori(1, NP) as k:
                roots(2 * k - 2)
                roots(2 * k - 1)
                neigh(k, 0)
                neigh(k, 1)
            roots(NT - 2)
            roots(NT - 1)
            act.wait_ge(s_lgc, NT)
            A.activation(flat(gates[:, :, :]), flat(logits[:, :, :]), ACT.Exp).then_inc(s_exp, 1)
            A.activation(flat(ex6[:, :, :]), flat(ex6[:, :, :]), ACT.Exp).then_inc(s_exp, 1)

            def stage(w, par):
                act.wait_ge(s_tk, w + 1)
                if not isinstance(w, int) or w >= 2:
                    act.wait_ge(s_up, w - 1)
                A.activation(flat(tt2[par][:, :, :]), flat(t_t[:, bass.ds(w, 1), :]), ACT.Copy).then_inc(s_tt2, 1)

            def silu(w):
                act.wait_ge(s_ga, w + 1)
                if later(w):
                    act.wait_ge(s_hm, w)
                A.activation(sg[:, :], ps[:, 0, :], ACT.Silu).then_inc(s_silu, 1)

            def hidden_T(w):
                act.wait_ge(s_hT, w + 1)
                if later(w):
                    act.wait_ge(s_dw, w)
                A.activation(flat(hsh_t[:, :, :]), ps[:, 2, :], ACT.Copy).then_inc(s_hTc, 1)

            act.wait_ge(s_self, NT)
            act.wait_ge(s_lg, NT)
            act.wait_ge(s_tk, NT)
            act.wait_ge(s_t, NT)
            stage(0, 0)
            stage(1, 1)
            silu(0)
            silu(1)
            hidden_T(0)
            with act.Fori(1, NT // 2) as i:
                for par in range(2):
                    stage(2 * i + par, par)
                    silu(2 * i + par)
                    hidden_T(2 * i + par - 1)
            hidden_T(NT - 1)
            act.wait_ge(s_dw, NT)
            act.wait_ge(s_tab, NT + 1)
            act.wait_ge(s_rank, 1)
            act.wait_ge(s_base, NT)
            for h in range(2):
                for q in (e_yc,):
                    act.sem_inc(q[h], 1)

            def w_high(e, s, n, part, r):
                if part == 0:
                    act.wait_ge(e_w[s], n * 16)
                if r is not None:
                    used = e_y if part == 2 else e_gu
                    act.wait_ge(used[0], e)
                    act.wait_ge(used[1], r + 1)
                cols = slice(part * WPART, (part + 1) * WPART)
                A.activation(w_hi[s % 2][:, cols], wbuf[s][:, cols], ACT.Copy).then_inc(e_wh, 1)

            def x_high(h, s, n, gu):
                act.wait_ge(e_xT[h], n)
                act.wait_ge(e_gu[h], gu)
                A.activation(flat(xt[0][h][s % 2][:, :, :]), ps[:, 4 * h, :], ACT.Copy).then_inc(e_xh[h], 1)

            def e_silu(h, n):
                act.wait_ge(e_gu[h], n + 1)
                act.wait_ge(e_h[h], n)
                A.activation(sil[h][:, :], ps[:, 4 * h + 1, 0:F], ACT.Silu).then_inc(e_si[h], 1)

            def h_high(h, n):
                act.wait_ge(e_hT[h], n + 1)
                act.wait_ge(e_y[h], n)
                A.activation(flat(ht[0][h][:, :, :]), ps[:, 4 * h + 2, 0:F], ACT.Copy).then_inc(e_hh[h], 1)

            def y_scaled(h, e, s, n):
                act.wait_ge(e_g[h], n)
                act.wait_ge(e_y[h], n + 1)
                A.activation(yb[h][s % 2], ps[:, 4 * h + 3, :], ACT.Copy, scale=kept[h][s][:, :]
                             ).then_inc(e_yc[h], 1)

            def y_both(e, s, added, r0, r1):
                if added is not None:
                    act.wait_ge(e_sc, (e - 1 + added) * 16)
                y_scaled(0, e, s, e + 1)
                with act.If(r1 > r0):
                    y_scaled(1, e, s, r1)

            ranks = Ranks(act, rank, U - 3, U + 1)

            def expert_body(i, first=False, last=False):
                r = ranks.begin(i, first)
                if first:
                    act.wait_ge(s_bst, 16 * NT)
                    for part in range(3):
                        w_high(0, 0, 1, part, None)
                    x_high(0, 0, 1, 1)
                    with act.If(r[U] > r[U - 1]):
                        x_high(1, 0, r[U], r[U - 1] + 1)
                for s in range(U):
                    e = i * U + s
                    s1 = (s + 1) % U
                    before = None if first and s == 0 else r[U + s - 1]
                    if not (last and s == U - 1):
                        x_high(0, s1, e + 2, e + 1)
                        with act.If(r[U + s + 1] > r[U + s]):
                            x_high(1, s1, r[U + s + 1], r[U + s - 1] + 1)
                        for part in range(2):
                            w_high(e + 1, s1, i + 1 + (s + 1) // U, part, before)
                    ranks.next(s)
                    e_silu(0, e + 1)
                    with act.If(r[U + s] > r[U + s - 1]):
                        e_silu(1, r[U + s])
                    if not (first and s == 0):
                        y_both(e - 1, (s - 1) % U, None if first and s <= 2 else r[U + s - 3],
                               r[U + s - 2], r[U + s - 1])
                    h_high(0, e + 1)
                    with act.If(r[U + s] > r[U + s - 1]):
                        h_high(1, r[U + s])
                    if not (last and s == U - 1):
                        w_high(e + 1, s1, i + 1 + (s + 1) // U, 2, before)
                if last:
                    y_both(E - 1, U - 1, r[2 * U - 3], r[2 * U - 2], r[2 * U - 1])
                else:
                    ranks.hand_over()

            expert_body(0, first=True)
            with act.Fori(1, E // U - 1) as i:
                expert_body(i)
            expert_body(E // U - 1, last=True)

        @block.vector
        def _(dve):
            V = nc.vector
            own = Steps(dve, dv)

            def later(w):
                return not isinstance(w, int) or w > 0

            def flat(a):
                return a.rearrange("p a n -> p (a n)")


            dve.wait_ge(s_dst, 16)
            V.tensor_copy(dst_f[:, :, :], dst_i[:, :, :]).then_inc(s_ef, 1)
            dve.wait_ge(s_src, 16)
            V.tensor_copy(src_f[:, :, :], src_i[:, :, :]).then_inc(s_ef, 1)
            dve.wait_ge(s_ef, 2)
            V.tensor_reduce(ends[:, 0:2], dst_f[:, :, :], AX.X, ALU.min).then_inc(s_ef, 1)
            V.tensor_reduce(ends[:, 2:4], dst_f[:, :, :], AX.X, ALU.max).then_inc(s_ef, 1)
            dve.wait_ge(s_eT, 1)
            own.mark(V.tensor_copy(edge[:, :], ps[0:EP, 6, 0:4 * EH]))
            dve.wait_ge(s_eT, 2)
            for j, op in enumerate((ALU.min, ALU.max)):
                own.mark(V.tensor_reduce(wrow[0:1, j, :], ps[0:1, 7, j * ET:(j + 1) * ET].rearrange("p (g t) -> p g t", t=G),
                                         AX.X, op))
            own.wait()
            own.mark(V.tensor_copy(wtab_f[:, 0, :], wrow[:, 0, :]))
            own.mark(V.tensor_tensor(wrow[:, 1, :], wrow[:, 1, :], wrow[:, 0, :], ALU.subtract))
            own.wait()
            own.mark(V.tensor_copy(wint[:, 0, :], wrow[:, 1, :]))
            own.wait()
            own.mark(V.tensor_single_scalar(wint[:, 0, :], wint[:, 0, :], 7, ALU.arith_shift_right))
            own.wait()
            own.mark(V.tensor_copy(wtab_f[:, 1, :], wint[:, 0, :]))
            own.wait()
            dve.wait_ge(s_cst, 12)
            own.mark(V.tensor_tensor_scan(wtab_f[:, 2, :], zrow1[:, 0:NG], wtab_f[:, 1, :], 0.0, ALU.add, ALU.add))
            own.wait()
            own.mark(V.tensor_tensor(wtab_f[:, 2, :], wtab_f[:, 2, :], wtab_f[:, 1, :], ALU.subtract))
            own.wait()
            V.tensor_copy(wtab[:, :, :], wtab_f[:, :, :]).then_inc(s_win, 1)
            dve.wait_ge(s_win, 1)
            dve.wait_ge(s_hot0, 2)

            def hot_rows(g, par):
                if not isinstance(g, int) or g >= 2:
                    dve.wait_ge(s_cd, g - 1)
                for t in range(G):
                    m = V.tensor_scalar(hot_src[par][:, t, 0:N], iota_h[0:EP, 0:N],
                                        edge[:, bass.ds(g * G + t, 1)], None, ALU.is_equal)
                    if t < G - 1:
                        own.mark(m)
                own.wait()
                m.then_inc(s_hs, 1)

            def add_counts(w, par):
                cells = counts[:, :, bass.ds(w, P)]
                return V.tensor_tensor(cells, acc[par][:, 0:NPAD].rearrange("p (q m) -> p q m", q=NT), cells, ALU.add)

            def add_group(g, par):
                w = dve.value_load(wtab[0:1, 0, bass.ds(g, 1)], min_val=0, max_val=N - 1)
                dve.wait_ge(s_cd, g + 1)
                dve.wait_ge(s_cc, g + 1)
                add_counts(w, par).then_inc(s_cc, 1)
                more = dve.value_load(wtab[0:1, 1, bass.ds(g, 1)], min_val=0, max_val=NT - 1)
                with dve.If(more > 0):
                    base = dve.value_load(wtab[0:1, 2, bass.ds(g, 1)], min_val=0, max_val=NT * NG)
                    with dve.Fori(0, NT - 1) as j:
                        with dve.If(j < more):
                            dve.wait_ge(s_cc, g + 2)
                            v = nc.s_assert_within(w + (j + 1) * P, 0, N - 1, skip_runtime_bounds_check_because="the last window of a group starts at its last node or before it")
                            for t in range(G):
                                m = V.tensor_scalar(hot_more[:, t, :], iota_h[0:EP, bass.ds(v, P)],
                                                    edge[:, bass.ds(ET + g * G + t, 1)], None, ALU.is_equal)
                                m.then_inc(m_hot, 1)
                            dve.wait_ge(m_cnt, base + j + 1)
                            add_counts(v, par).then_inc(m_add, 1)
                            dve.wait_ge(m_add, base + j + 1)
                            dve.sem_inc(s_past["dve"], 1)

            def keep_self(w):
                dve.wait_ge(s_self, w + 1)
                V.tensor_tensor(flat(t_t[:, bass.ds(w, 1), :]), ps[:, 7, :], bias_b[:, :], ALU.add).then_inc(s_selfc, 1)

            hot_rows(0, 0)
            hot_rows(1, 1)

            dve.wait_ge(s_x, 32)
            for w in range(NT):
                own.mark(V.bn_stats(stat[:, w, :], xs[:, w, :]))
            own.wait()
            for w in range(NT):
                own.mark(V.bn_aggr(mv[:, w, :], stat[:, w, :]))
            own.wait()
            V.tensor_scalar(ve[:, :], mv[:, :, 1], EPS, None, ALU.add).then_inc(s_var, 1)
            dve.wait_ge(s_sqrt, 1)

            def inv_sqrt(r, q, root, v):
                own.mark(V.reciprocal(r, root))
                own.wait()
                own.mark(V.tensor_tensor(q, r, r, ALU.mult))
                own.wait()
                own.mark(V.tensor_tensor(q, q, v, ALU.mult))
                own.wait()
                own.mark(V.tensor_scalar(q, q, -0.5, 1.5, ALU.mult, ALU.add))
                own.wait()
                own.mark(V.tensor_tensor(r, r, q, ALU.mult))
                own.wait()

            inv_sqrt(rs[:, :], rq[:, :], sd[:, :], ve[:, :])
            for w in range(NT):
                m = V.tensor_scalar(xn[:, w, :], xs[:, w, :], mv[:, w, 0:1], rs[:, w:w + 1], ALU.subtract, ALU.mult)
                if w < NT - 1:
                    own.mark(m)
            m.then_inc(s_xn, 1)
            own.mark(V.tensor_scalar(valid[:, :], tok_f[:, :], float(N), None, ALU.is_lt))
            own.wait()
            own.mark(V.tensor_scalar(vm1[:, :], valid[:, :], 1.0, None, ALU.subtract))

            dve.wait_ge(s_vec, 64)
            add_group(0, 0)
            own.restart()
            with dve.Fori(1, NT) as i:
                hot_rows(2 * i, 0)
                add_group(2 * i - 1, 1)
                hot_rows(2 * i + 1, 1)
                keep_self(i - 1)
                add_group(2 * i, 0)
                own.restart()
            add_group(NG - 1, 1)
            keep_self(NT - 1)
            dve.wait_ge(s_cc, NG + 1)

            dve.wait_ge(s_deg, 1)
            own.mark(V.tensor_scalar(deg[:, :], ps[:, 3, 0:NT], 1.0, None, ALU.max))
            own.wait()
            V.reciprocal(rdeg[:, :], deg[:, :]).then_inc(s_rdeg, 1)
            dve.wait_ge(s_rdeg, 1)

            def norm(st, a, at):
                own.mark(V.bn_stats(st[:, 0:6], a))
                own.wait()
                own.mark(V.bn_aggr(st[:, 6:8], st[:, 0:6]))
                own.wait()
                V.tensor_scalar(st[:, 8:9], st[:, 7:8], EPS, None, ALU.add).then_inc(s_var, 1)
                dve.wait_ge(s_sqrt, at)
                inv_sqrt(st[:, 10:11], st[:, 11:12], st[:, 9:10], st[:, 8:9])

            def tile(w):
                xrow = flat(xs[:, bass.ds(w, 1), :])
                dve.wait_ge(s_nb, w + 1)
                V.scalar_tensor_tensor(out=h0[:, :], in0=ps[:, 7, :], scalar=rdeg[:, bass.ds(w, 1)],
                                       in1=flat(t_t[:, bass.ds(w, 1), :]), op0=ALU.mult, op1=ALU.add).then_inc(s_h, 1)
                dve.wait_ge(s_h, w + 1)
                norm(st1, h0[:, :], 2 * w + 2)
                own.mark(V.scalar_tensor_tensor(out=h1[:, :], in0=h0[:, :], scalar=st1[:, 6:7], in1=gamma_b[:, :],
                                                op0=ALU.subtract, op1=ALU.mult))
                own.wait()
                own.mark(V.scalar_tensor_tensor(out=h0[:, :], in0=h1[:, :], scalar=st1[:, 10:11], in1=beta_b[:, :],
                                                op0=ALU.mult, op1=ALU.add))
                own.wait()
                own.mark(V.tensor_tensor(xrow, xrow, h0[:, :], ALU.add))
                own.wait()
                norm(st2, xrow, 2 * w + 3)
                if later(w):
                    dve.wait_ge(s_tst, w * 16)
                V.tensor_scalar(tw[:, :], xrow, st2[:, 6:7], st2[:, 10:11], ALU.subtract, ALU.mult).then_inc(s_t, 1)

            def router(w):
                dve.wait_ge(s_tT, w + 1)
                if later(w):
                    dve.wait_ge(s_tk, w)
                V.tensor_copy(flat(tw_t[:, :, :]), ps[:, 3, :]).then_inc(s_tTc, 1)
                dve.wait_ge(s_lg, w + 1)
                own.mark(V.tensor_tensor(lgw[:, :], ps[:, 4, 0:E], rb[:, :], ALU.add))
                own.wait()
                own.mark(V.max(v8w[:, :], lgw[:, :]))
                own.wait()
                own.mark(V.max_index(i8[:, :], v8w[:, :], lgw[:, :]))
                own.mark(V.tensor_scalar(flat(ex6[:, bass.ds(w, 1), :]), v8w[:, 0:TOPK], v8w[:, 0:1], None, ALU.subtract))
                own.mark(V.tensor_scalar(flat(logits[:, bass.ds(w, 1), :]), lgw[:, :], v8w[:, 0:1], None, ALU.subtract))
                own.wait()
                V.tensor_copy(flat(i6_all[:, bass.ds(w, 1), :]), i8[:, 0:TOPK]).then_inc(s_lgc, 1)
                dve.wait_ge(s_lgc, w + 1)

            own.restart()
            with dve.Fori(0, NT) as w:
                tile(w)
                router(w)
                own.restart()

            def choose(w):
                ok, okm = valid[:, bass.ds(w, 1)], vm1[:, bass.ds(w, 1)]
                own.mark(V.tensor_scalar(i6[:, :], flat(i6_all[:, bass.ds(w, 1), :]), ok, okm, ALU.mult, ALU.add))
                own.wait()
                own.mark(V.tensor_tensor(hot_e[:, :, :], iota_e[:, :].rearrange("p (a e) -> p a e", a=1).broadcast_to([P, TOPK, E]),
                                         i6[:, :].rearrange("p (k a) -> p k a", a=1).broadcast_to([P, TOPK, E]), ALU.is_equal))
                own.wait()
                if later(w):
                    dve.wait_ge(s_pre, w)
                    own.mark(V.tensor_tensor(msum[:, :], msum[:, :], mask[:, :], ALU.add))
                    own.wait()
                with nc.allow_low_precision("0 or 1"):
                    V.tensor_reduce(mask[:, :], hot_e[:, :, :].rearrange("p k e -> p e k"), AX.X, ALU.add).then_inc(s_mask, 1)

            def place(w):
                ok = valid[:, bass.ds(w, 1)]
                dve.wait_ge(s_pre, w + 1)
                own.mark(V.tensor_tensor(hot_s[:, :, :], ps[:, 4, 0:E].rearrange("p (a e) -> p a e", a=1).broadcast_to([P, TOPK, E]),
                                         hot_e[:, :, :], ALU.mult))
                own.wait()
                own.mark(V.tensor_reduce(slot[:, :], hot_s[:, :, :], AX.X, ALU.add))
                own.wait()
                own.mark(V.tensor_scalar(keep[:, :], slot[:, :], float(CAP), ok, ALU.is_lt, ALU.mult))
                own.mark(V.tensor_scalar(half[:, :], slot[:, :], float(P), None, ALU.is_ge))
                own.wait()
                own.mark(V.scalar_tensor_tensor(out=lo[:, :], in0=half[:, :], scalar=float(-P), in1=slot[:, :],
                                                op0=ALU.mult, op1=ALU.add))
                own.mark(V.scalar_tensor_tensor(out=hi[:, :], in0=i6[:, :], scalar=2.0, in1=half[:, :],
                                                op0=ALU.mult, op1=ALU.add))
                own.wait()
                own.mark(V.scalar_tensor_tensor(out=hi[:, :], in0=hi[:, :], scalar=1.0, in1=keep[:, :],
                                                op0=ALU.add, op1=ALU.mult))
                own.wait()
                own.mark(V.tensor_scalar(hi[:, :], hi[:, :], -1.0, None, ALU.add))
                own.wait()
                if later(w):
                    dve.wait_ge(s_tab, w)
                for k in range(TOPK):
                    own.mark(V.tensor_scalar(hot_lo[:, k, :], iota_h[:, 0:P], lo[:, k:k + 1], tok1_f[:, bass.ds(w, 1)],
                                             ALU.is_equal, ALU.mult))
                    m = V.tensor_scalar(hot_hi[:, k, :], iota_h[:, 0:P], hi[:, k:k + 1], None, ALU.is_equal)
                    if k < TOPK - 1:
                        own.mark(m)
                own.wait()
                m.then_inc(s_hl, 1)

            def hidden(w):
                dve.wait_ge(s_silu, w + 1)
                dve.wait_ge(s_up, w + 1)
                if later(w):
                    dve.wait_ge(s_hT, w)
                V.tensor_tensor(hsh[:, :], ps[:, 1, :], sg[:, :], ALU.mult).then_inc(s_hm, 1)

            def base_row(w):
                xrow = flat(xs[:, bass.ds(w, 1), :])
                dve.wait_ge(s_dw, w + 1)
                V.scalar_tensor_tensor(out=xrow, in0=ps[:, 3, :], scalar=1.0 / SH, in1=xrow,
                                       op0=ALU.mult, op1=ALU.add).then_inc(s_base, 1)

            dve.wait_ge(s_exp, 2)
            own.mark(V.tensor_reduce(zsum[:, 0, :], gates[:, :, :], AX.X, ALU.add))
            own.mark(V.tensor_reduce(zsum[:, 1, :], ex6[:, :, :], AX.X, ALU.add))
            own.wait()
            own.mark(V.scalar_tensor_tensor(out=rden[:, :], in0=zsum[:, 0, :], scalar=1e-9, in1=zsum[:, 1, :],
                                            op0=ALU.mult, op1=ALU.add))
            own.wait()
            own.mark(V.reciprocal(rden[:, :], rden[:, :]))
            own.wait()
            V.tensor_tensor(gates[:, :, :], gates[:, :, :],
                            rden[:, :].rearrange("p (w a) -> p w a", a=1).broadcast_to([P, NT, E]), ALU.mult).then_inc(s_gate, 1)
            choose(0)
            place(0)
            hidden(0)
            own.restart()
            with dve.Fori(1, NT) as w:
                choose(w)
                place(w)
                hidden(w)
                base_row(w - 1)
                own.restart()
            dve.wait_ge(s_pre, NT)
            own.mark(V.tensor_tensor(msum[:, :], msum[:, :], mask[:, :], ALU.add))
            own.wait()
            dve.sem_inc(s_mask, 1)
            dve.wait_ge(s_tab, NT + 1)
            own.mark(V.tensor_scalar(empty[:, :], ps[:, 5, 0:2 * E], 0.0, dump_f[:, :], ALU.is_equal, ALU.mult))
            own.wait()
            V.scalar_tensor_tensor(out=tokidx[:, :], in0=ps[:, 5, 0:2 * E], scalar=-1.0, in1=empty[:, :],
                                   op0=ALU.add, op1=ALU.add).then_inc(s_tok, 1)
            dve.wait_ge(s_cnt, 1)
            own.mark(V.tensor_scalar(cnt[:, :], ps[0:1, 6, 0:E], float(P), None, ALU.is_gt))
            own.wait()
            own.mark(V.tensor_tensor_scan(rank_f[:, U:U + E], zrow1[:, :], cnt[:, :], 0.0, ALU.add, ALU.add))
            own.wait()
            V.tensor_copy(rank[:, :], rank_f[:, :]).then_inc(s_rank, 1)
            dve.wait_ge(s_rank, 1)
            base_row(NT - 1)
            for q in (e_xl, e_h, e_hl):
                for h in range(2):
                    dve.sem_inc(q[h], 1)

            def w_low(e, s, part):
                dve.wait_ge(e_wh, 3 * e + part + 1)
                cols = slice(part * WPART, (part + 1) * WPART)
                V.tensor_tensor(w_lo[s % 2][:, cols], wbuf[s][:, cols], w_hi[s % 2][:, cols].bitcast(F32), ALU.subtract
                                ).then_inc(e_wl, 1)

            def x_low(h, e, s, n, scaled):
                dve.wait_ge(e_xh[h], n)
                V.tensor_tensor(flat(xt[1][h][s % 2][:, :, :]), ps[:, 4 * h, :], flat(xt[0][h][s % 2][:, :, :]).bitcast(F32),
                                ALU.subtract).then_inc(e_xl[h], 1)
                if scaled is not None:
                    dve.wait_ge(e_yc[h], scaled + 1)
                V.tensor_copy(kept[h][s][:, :], gx[h][s][:, bass.ds(D + e, 1)]).then_inc(e_g[h], 1)

            def hid(h, n):
                dve.wait_ge(e_si[h], n)
                dve.wait_ge(e_hT[h], n)
                V.tensor_tensor(hh[h][:, :], ps[:, 4 * h + 1, F:2 * F], sil[h][:, :], ALU.mult).then_inc(e_h[h], 1)

            def h_low(h, n):
                dve.wait_ge(e_hh[h], n)
                V.tensor_tensor(flat(ht[1][h][:, :, :]), ps[:, 4 * h + 2, 0:F], flat(ht[0][h][:, :, :]).bitcast(F32),
                                ALU.subtract).then_inc(e_hl[h], 1)

            ranks = Ranks(dve, rank, 1, U + 1)

            def expert_body(i, first=False, last=False):
                r = ranks.begin(i, first)
                if first:
                    for part in range(3):
                        w_low(0, 0, part)
                    x_low(0, 0, 0, 1, None)
                    with dve.If(r[U] > r[U - 1]):
                        x_low(1, 0, 0, r[U], None)
                for s in range(U):
                    e = i * U + s
                    s1 = (s + 1) % U
                    if not (last and s == U - 1):
                        some = not (first and s < U - 1)
                        x_low(0, e + 1, s1, e + 2, e + 2 - U if some else None)
                        with dve.If(r[U + s + 1] > r[U + s]):
                            x_low(1, e + 1, s1, r[U + s + 1], r[s + 1] if some else None)
                        w_low(e + 1, s1, 0)
                    ranks.next(s)
                    hid(0, e + 1)
                    with dve.If(r[U + s] > r[U + s - 1]):
                        hid(1, r[U + s])
                    if not (last and s == U - 1):
                        w_low(e + 1, s1, 1)
                    h_low(0, e + 1)
                    with dve.If(r[U + s] > r[U + s - 1]):
                        h_low(1, r[U + s])
                    if not (last and s == U - 1):
                        w_low(e + 1, s1, 2)
                if not last:
                    ranks.hand_over()

            expert_body(0, first=True)
            with dve.Fori(1, E // U - 1) as i:
                expert_body(i)
            expert_body(E // U - 1, last=True)


_OUT = ((ROWS, D), "float32")


def kernel(x, src, dst, L0_gnn_W_self, L0_gnn_W_neigh, L0_gnn_bias, L0_gnn_gamma, L0_gnn_beta, L0_ffn_router_w,
           L0_ffn_bias, L0_ffn_shared_w_gate, L0_ffn_shared_w_up, L0_ffn_shared_w_down, L0_ffn_w_gate, L0_ffn_w_up,
           L0_ffn_w_down):
    import numpy as np
    import concourse.bacc as bacc
    from concourse.bass_utils import run_bass_kernel_spmd

    def chunks(a):
        return a.reshape(a.shape[0] // P, P, a.shape[1]).transpose(1, 0, 2)

    def t(a):
        return np.asarray(a).T

    def rows(a):
        a = np.asarray(a)
        return a.reshape(-1, a.shape[-1]).T

    gu = np.concatenate([np.asarray(L0_ffn_w_gate), np.asarray(L0_ffn_w_up)], axis=1)
    gu = gu.transpose(0, 2, 1).reshape(E, DC, P, 2 * F).transpose(0, 2, 1, 3).reshape(E, P, DC * 2 * F)
    dn = np.asarray(L0_ffn_w_down).transpose(0, 2, 1).reshape(E, FC, P, D).transpose(0, 2, 1, 3).reshape(E, P, FC * D)
    sdn = np.asarray(L0_ffn_shared_w_down).transpose(0, 2, 1).reshape(SH * F, D)
    arrays = {
        "x": x, "src": src, "dst": dst,
        "w_self": chunks(t(L0_gnn_W_self)), "w_neigh": chunks(t(L0_gnn_W_neigh)),
        "bias": L0_gnn_bias, "gamma": L0_gnn_gamma, "beta": L0_gnn_beta,
        "router_w": chunks(t(L0_ffn_router_w)), "router_b": L0_ffn_bias,
        "shared_gu": chunks(np.concatenate([rows(L0_ffn_shared_w_gate), rows(L0_ffn_shared_w_up)], axis=1)),
        "shared_down": chunks(sdn),
        "expert_w": np.concatenate([gu, dn], axis=2),
    }
    nc = bacc.Bacc("TRN2", target_bir_lowering=False, num_devices=1)
    args = []
    for name in arrays:
        arrays[name] = np.ascontiguousarray(arrays[name])
        a = arrays[name]
        args.append(nc.dram_tensor(name, a.shape, mybir.dt.from_np(a.dtype), kind="ExternalInput").ap())
    args.append(nc.dram_tensor("out", _OUT[0], F32, kind="ExternalOutput").ap())
    gnn_moe(nc, *args)
    return run_bass_kernel_spmd(nc, [arrays], core_ids=[0]).results[0]["out"][:N]
```

```python
from contextlib import ExitStack

import concourse.bass as bass
from concourse import mybir

F32 = mybir.dt.float32
F32R = mybir.dt.float32r
BF16 = mybir.dt.bfloat16
F16 = mybir.dt.float16
I32 = mybir.dt.int32
U32 = mybir.dt.uint32
ALU = mybir.AluOpType
ACT = mybir.ActivationFunctionType
AX = mybir.AxisListType

P = 128
N, D, E, F = 1250, 512, 64, 256
TOPK = 6
SH = 2
CAP = N * TOPK * 2 // E
NT = -(-N // P)
NPAD = NT * P
LAST = N - (NT - 1) * P
DC, FC = D // P, F // P
EPS = 1e-5
EDGES, EP = 20000, 125
ET = EDGES // EP
EH = ET // 2
G = 8
NG = ET // G
DEG = NPAD - 1
CW = -(-(N + P) // 4) * 4
NP = NT // 2
assert NG == 2 * NT
TW = D + E
ROWS = N + P
U = 4
WG = DC * 2 * F
WCOL = WG + FC * D
WPART = D * 2
assert WG == 2 * WPART and WCOL == 3 * WPART
EARLY_REST = (G * NPAD + 2 * DC * D + NT * D) - (4 * WCOL + 8 * DC * P + 4 * FC * P + 4 * F)


class Steps:

    def __init__(self, eng, sem):
        self.eng, self.sem, self.n = eng, sem, 0

    def mark(self, ins):
        ins.then_inc(self.sem, 1)
        self.n += 1

    def wait(self):
        self.eng.wait_ge(self.sem, self.n)

    def restart(self):
        if self.n:
            self.wait()
            self.eng.sem_inc(self.sem, -self.n)
            self.n = 0


class Ranks:

    def __init__(self, eng, rank, low, high):
        self.eng, self.rank, self.low, self.high = eng, rank, low, high
        self.kept = [eng.alloc_register(name=f"rank_{j}") for j in range(high - low + 1)]

    def read(self, j):
        at = self.i * U + j
        if not isinstance(at, int) or at < U + E:
            self.r[j] = self.eng.value_load(self.rank[0:1, bass.ds(at, 1)], min_val=0, max_val=E)

    def begin(self, i, first):
        self.i, self.r = i, {}
        for j, reg in zip(range(self.low, self.high + 1), self.kept):
            if first:
                self.read(j)
            else:
                self.r[j] = self.eng.snap(reg, min_val=0, max_val=E)
        return self.r

    def next(self, s):
        self.read(self.high + 1 + s)

    def hand_over(self):
        for j, reg in zip(range(self.low, self.high + 1), self.kept):
            self.eng.reg_mov(reg, self.r[j + U])


def gnn_moe(nc, x, src, dst, w_self, w_neigh, bias, gamma, beta, router_w, router_b,
            shared_gu, shared_down, expert_w, out):
    ctx = ExitStack()
    with ctx:
        def sb(name, shape, dt):
            return ctx.enter_context(nc.sbuf_tensor(name, shape, dt))

        def sem(name):
            return ctx.enter_context(nc.semaphore(name))

        t_dram = nc.dram_tensor("t_rows", [ROWS, TW], F32).ap()

        ps = ctx.enter_context(nc.psum_tensor("ps", [P, 8, 512], F32))
        acc = [ps[:, 3 * b:3 * b + 3, :].rearrange("p b n -> p (b n)") for b in range(2)]

        with ExitStack() as early:
            def sb_early(name, shape, dt):
                return early.enter_context(nc.sbuf_tensor(name, shape, dt))

            hot_all = sb_early("hot_all", [P, 2, G, NPAD], BF16)
            ws = sb_early("ws", [P, DC, D], F32)
            wn = sb_early("wn", [P, DC, D], F32)
            xs = sb_early("xs", [P, NT, D], F32)
        with ExitStack() as middle:
            def sb_middle(name, shape, dt):
                return middle.enter_context(nc.sbuf_tensor(name, shape, dt))

            wsg_lo = sb_middle("wsg_lo", [P, DC, 2 * D], F32R)
            sb_middle("middle_gap", [P, 2 * NPAD + 2 * E], F32)
            hsh_hi = sb_middle("hsh_hi", [P, DC, P], F32R)
            hsh_lo = sb_middle("hsh_lo", [P, DC, P], F32R)
            sb_middle("middle_gap2", [P, G * NPAD - DC * 2 * D - 2 * NPAD - 2 * E - 2 * D], F32)
            wd_lo = sb_middle("wd_lo", [P, DC, D], F32R)
            wd_hi = sb_middle("wd_hi", [P, DC, D], F32R)
        hot_src = [hot_all[0:EP, b, :, :] for b in range(2)]
        w_hi = [sb(f"w_hi{b}", [P, WCOL], F32R) for b in range(2)]
        w_lo = [sb(f"w_lo{b}", [P, WCOL], F32R) for b in range(2)]
        xt = [[[sb(f"xt_{part}{h}_{b}", [P, DC, P], F32R) for b in range(2)] for h in range(2)] for part in ("hi", "lo")]
        ht = [[sb(f"ht_{part}{h}", [P, FC, P], F32R) for h in range(2)] for part in ("hi", "lo")]
        sil = [sb(f"sil{h}", [P, F], F32) for h in range(2)]
        hh = [sb(f"hh{h}", [P, F], F32) for h in range(2)]
        sb("early_rest", [P, EARLY_REST], F32)

        iota_h = sb("iota_h", [P, CW], F16)
        iota_e = sb("iota_e", [P, E], F32)
        ident = sb("ident", [P, P], F32)
        before = sb("before", [P, P], BF16)
        ones = sb("ones", [P, P], BF16)
        zero_h = sb("zero_h", [P, P], F16)
        with nc.sbuf_tensor("zrows", [P, TW], F32) as zrows:
            pass
        xT_lo = sb("xT_lo", [P, DC, P], F32R)
        sb("zrows_rest", [P, TW - D], F32)
        tok_f = sb("tok_f", [P, NT], F32)
        tok1_f = sb("tok1_f", [P, NT], F32)
        dump_f = sb("dump_f", [P, 1], F32)
        valid = sb("valid", [P, NT], F32)
        rw = sb("rw", [P, DC, E], F32)
        rb = sb("rb", [P, E], F32)
        bias_b = sb("bias_b", [P, D], F32)
        gamma_b = sb("gamma_b", [P, D], F32)
        beta_b = sb("beta_b", [P, D], F32)
        with nc.sbuf_tensor("xn", [P, NT, D], F32) as xn:
            pass
        wsg_hi = sb("wsg_hi", [P, DC, 2 * D], F32R)
        tt_lo = [sb(f"tt_lo{b}", [P, DC, P], F32R) for b in range(2)]
        src_i, dst_i = (xn[0:EH, q, 0:2 * EP].bitcast(I32).rearrange("t (h p) -> t h p", h=2) for q in range(2))
        src_f, dst_f = (xn[0:EH, q, 0:2 * EP].rearrange("t (h p) -> t h p", h=2) for q in range(2, 4))
        ends = sb("ends", [EH, 4], F32)
        edge = sb("edge", [EP, 4 * EH], F32)
        wrow = sb("wrow", [1, 2, NG], F32)
        wint = sb("wint", [1, 2, NG], I32)
        wtab_f = sb("wtab_f", [1, 3, NG], F32)
        zrow1 = sb("zrow1", [1, E], F32)
        wtab = sb("wtab", [1, 3, NG], I32)
        hot_dst = [sb(f"hot_dst{b}", [EP, G, P], BF16) for b in range(2)]
        hot_more = sb("hot_more", [EP, G, P], BF16)
        dist = sb("dist", [EP, G, P], BF16)
        counts = sb("counts", [P, NT, CW], F32)
        stat = sb("stat", [P, NT, 6], F32)
        mv = sb("mv", [P, NT, 2], F32)
        ve = sb("ve", [P, NT], F32)
        sd = sb("sd", [P, NT], F32)
        rs = sb("rs", [P, NT], F32)
        rq = sb("rq", [P, NT], F32)
        shift = sb("shift", [P, NT], F32)
        with nc.sbuf_tensor("xw", [P, D], F32) as xw:
            pass
        tt_hi = [sb(f"tt_hi{b}", [P, DC, P], F32R) for b in range(2)]
        xT_hi = tt_hi[1]
        deg = sb("deg", [P, NT], F32)
        rdeg = sb("rdeg", [P, NT], F32)
        over = hot_all[:, :, :, :].rearrange("p b t n -> p (b t n)").bitcast(F32)
        taken = [0]

        def place_over(words):
            taken[0] += words
            assert taken[0] <= G * NPAD
            return over[:, taken[0] - words:taken[0]]

        wsg = place_over(DC * 2 * D).rearrange("p (c n) -> p c n", c=DC)
        ct = place_over(NT * P).rearrange("p (q m) -> p q m", q=NT)
        cw = place_over(NPAD)
        empty = place_over(2 * E)
        nsum_t = place_over(DC * 2 * P).rearrange("p (c m) -> p c m", c=DC)
        h0 = place_over(D)
        h1 = place_over(D)
        tw = place_over(D)
        tw_t = place_over(D).rearrange("p (c m) -> p c m", c=DC)
        st1 = sb("st1", [P, 16], F32)
        st2 = sb("st2", [P, 16], F32)
        t_t = sb("t_t", [P, NT, D], F32)
        logits = sb("logits", [P, NT, E], F32)
        wsd = ws
        sg, hsh = h0, h1
        lgw = sb("lgw", [P, E], F32)
        v8w = sb("v8w", [P, 8], F32)
        i8 = sb("i8", [P, 8], U32)
        i6 = sb("i6", [P, TOPK], F32)
        i6_all = sb("i6_all", [P, NT, TOPK], F32)
        ctf = ct[:, :, :].rearrange("p a n -> p (a n)")
        hot_e = ctf[:, 0:TOPK * E].rearrange("p (k e) -> p k e", k=TOPK)
        hot_s = ctf[:, TOPK * E:2 * TOPK * E].rearrange("p (k e) -> p k e", k=TOPK)
        mask = sb("mask", [P, E], BF16)
        msum = sb("msum", [P, E], BF16)
        slot = sb("slot", [P, TOPK], F32)
        keep = sb("keep", [P, TOPK], F32)
        half = sb("half", [P, TOPK], F32)
        lo = sb("lo", [P, TOPK], F32)
        hi = sb("hi", [P, TOPK], F32)
        vm1 = sb("vm1", [P, NT], F32)
        ex6 = sb("ex6", [P, NT, TOPK], F32)
        zsum = sb("zsum", [P, 2, NT], F32)
        rden = sb("rden", [P, NT], F32)
        gates = sb("gates", [P, NT, E], F32)
        hot_w = TOPK * P // 2
        hot_lo, hot_hi = (cw[:, q * hot_w:(q + 1) * hot_w].bitcast(F16).rearrange("p (k m) -> p k m", k=TOPK)
                          for q in range(2))
        tokidx = sb("tokidx", [P, 2 * E], I32)
        cnt = sb("cnt", [1, E], F32)
        rank_f = sb("rank_f", [1, U + E + U], F32)
        rank = sb("rank", [1, U + E + U], I32)
        cflat = counts[:, :, :].rearrange("p w n -> p (w n)")
        wbuf = [cflat[:, s * WCOL:(s + 1) * WCOL] for s in range(U)]
        idxb = [[sb(f"idx{h}_{s}", [P, 1], I32) for s in range(U)] for h in range(2)]
        idxa = [sb(f"idx_add{h}", [P, 1], I32) for h in range(2)]
        kept = [[sb(f"kept{h}_{s}", [P, 1], F32) for s in range(U)] for h in range(2)]
        xflat = xn[:, :, :].rearrange("p w n -> p (w n)")
        gx = [[xflat[:, (U * h + s) * TW:(U * h + s + 1) * TW] for s in range(U)] for h in range(2)]
        yb = [[t_t[:, 2 * h + b, :] for b in range(2)] for h in range(2)]

        s_src, s_dst, s_x, s_w, s_wn, s_vec, s_rw = (sem(n) for n in (
            "src_in", "dst_in", "x_in", "w_self_in", "w_neigh_in", "vectors_in", "router_in"))
        s_gu, s_dn = sem("shared_gu_in"), sem("shared_down_in")
        s_cst = sem("consts_set")
        s_idt = sem("ident_zeroed")
        s_hot0 = sem("hot_src_set")
        s_xpad = sem("x_pad_zeroed")
        dv = sem("dve_steps")
        s_past = {n: sem(f"past_{n}") for n in ("dve", "pe", "sp", "pool", "act")}
        s_ef = sem("edges_float")
        s_eT = sem("edges_transposed")
        s_win = sem("windows_known")
        s_hs, s_hd = sem("hot_src_ready"), sem("hot_dst_ready")
        s_dist = sem("distances_ready")
        s_cd = sem("group_counted")
        s_cc = sem("counts_current")
        m_hot, m_cnt, m_add = sem("more_hot_ready"), sem("more_counted"), sem("more_added")
        s_ln, s_xn = sem("first_norm_known"), sem("x_normed")
        s_sh, s_sl = sem("w_self_high"), sem("w_self_low")
        s_xw, s_xT, s_xTc, s_xTl = sem("x_staged"), sem("x_T"), sem("x_T_high"), sem("x_T_low")
        s_self, s_selfc = sem("self_projected"), sem("self_copied")
        s_deg, s_rdeg = sem("degrees_turned"), sem("degrees_known")
        s_ns, s_nsc = sem("neigh_summed"), sem("neigh_copied")
        s_nb, s_h = sem("neigh_projected"), sem("neigh_added")
        s_var, s_sqrt = sem("variance_ready"), sem("sqrt_ready")
        s_t, s_tst = sem("t_ready"), sem("t_stored")
        s_tT, s_tTc, s_lg, s_lgc = sem("t_T"), sem("t_T_copied"), sem("logits_done"), sem("logits_copied")
        s_tk = sem("t_T_kept")
        s_tt2, s_ttl = sem("t_T_high"), sem("t_T_low")
        s_gh, s_gl, s_dh, s_dl = (sem(n) for n in ("shared_gu_high", "shared_gu_low", "shared_down_high", "shared_down_low"))
        s_ga, s_up, s_silu, s_hm = sem("gate_done"), sem("up_done"), sem("silu_done"), sem("hidden_done")
        s_hTl = sem("hidden_T_low")
        s_hT, s_hTc, s_dw, s_base = sem("hidden_T"), sem("hidden_T_copied"), sem("down_done"), sem("base_ready")
        s_mask, s_pre = sem("mask_ready"), sem("prefix_done")
        s_exp, s_gate, s_gst = sem("exps_done"), sem("gates_ready"), sem("gates_stored")
        s_z = sem("zrows_set")
        s_rest = sem("spare_rows_zeroed")
        s_bst, s_bst2 = sem("base_stored"), sem("last_base_stored")
        s_hl, s_tab, s_cnt = sem("table_hot"), sem("table_added"), sem("tokens_counted")
        s_rank, s_tok = sem("rank_known"), sem("tokens_listed")
        e_w = [sem(f"expert_w_in{s}") for s in range(U)]
        e_wh = sem("weights_high")
        e_wl, e_wd = sem("gate_up_low"), sem("down_low")
        e_idx = sem("expert_idx_copied")
        e_gx = [sem(f"rows_in{s}") for s in range(U)]
        e_gx2 = sem("second_rows_in")
        e_xT = sem("rows_T"), sem("second_rows_T")
        e_xh = sem("rows_T_high"), sem("second_rows_T_high")
        e_xl = sem("rows_T_low"), sem("second_rows_T_low")
        e_g = sem("gates_kept"), sem("second_gates_kept")
        e_gu = sem("gate_up"), sem("second_gate_up")
        e_si = sem("silu"), sem("second_silu")
        e_h = sem("hidden"), sem("second_hidden")
        e_hT = sem("hid_T"), sem("second_hid_T")
        e_hh = sem("hid_T_high"), sem("second_hid_T_high")
        e_hl = sem("hid_T_low"), sem("second_hid_T_low")
        e_y = sem("y"), sem("second_y")
        e_yc = sem("y_scaled"), sem("second_y_scaled")
        e_sc = sem("y_added")

        block = ctx.enter_context(nc.Block())

        @block.sync
        def _(sp):
            sp.dma_start(dst_i[:, :, :], dst.rearrange("(h t p) -> t h p", h=2, p=EP)).then_inc(s_dst, 16)
            sp.dma_start(src_i[:, :, :], src.rearrange("(h t p) -> t h p", h=2, p=EP)).then_inc(s_src, 16)
            sp.dma_start(xs[:, 0:NT - 1, :], x[0:(NT - 1) * P, :].rearrange("(t p) d -> p t d", p=P)).then_inc(s_x, 16)
            sp.wait_ge(s_xpad, 1)
            sp.dma_start(xs[0:LAST, NT - 1, :], x[(NT - 1) * P:N, :]).then_inc(s_x, 16)
            sp.dma_start(ws[:, :, :], w_self).then_inc(s_w, 16)
            sp.dma_start(rw[:, :, :], router_w).then_inc(s_rw, 16)
            for buf, vec in ((bias_b, bias), (gamma_b, gamma), (beta_b, beta), (rb, router_b)):
                v = vec.rearrange("(a n) -> a n", a=1)
                sp.dma_start(buf[:, :], v.broadcast_to([P, v.shape[1]])).then_inc(s_vec, 16)
            sp.wait_ge(s_z, 1)
            sp.dma_start(t_dram[NPAD:ROWS, :], zrows[0:ROWS - NPAD, :]).then_inc(s_rest, 16)
            sp.dma_start(out[NPAD:ROWS, :], zrows[0:ROWS - NPAD, 0:D]).then_inc(s_rest, 16)
            sp.wait_ge(s_cc, NG + 1)
            sp.dma_start(wsg[:, :, :], shared_gu).then_inc(s_gu, 16)
            sp.wait_ge(s_self, NT)
            sp.dma_start(wn[:, :, :], w_neigh).then_inc(s_wn, 16)
            sp.dma_start(wsd[:, :, :], shared_down).then_inc(s_dn, 16)
            with sp.Fori(0, NT) as w:
                sp.wait_ge(s_t, w + 1)
                sp.dma_start(t_dram[bass.ds(w * P, P), 0:D], tw).then_inc(s_tst, 16)
            sp.wait_ge(s_ns, 2 * NP)
            for s in range(U):
                sp.dma_start(wbuf[s], expert_w[s]).then_inc(e_w[s], 16)

            sp.wait_ge(s_gate, 1)
            sp.dma_start(t_dram[0:NPAD, D:TW].rearrange("(w p) e -> p w e", p=P), gates[:, :, :]).then_inc(s_gst, 16)
            def store_base(w, done):
                sp.wait_ge(s_base, w + 1)
                sp.dma_start(out[bass.ds(w * P, P), :], xs[:, bass.ds(w, 1), :].rearrange("p a n -> p (a n)")).then_inc(done, 16)

            with sp.Fori(0, NT - 2) as w:
                store_base(w, s_bst)
            for w in (NT - 2, NT - 1):
                store_base(w, s_bst2)
            with sp.Fori(0, E // U - 1) as i:
                for s in range(U):
                    sp.wait_ge(e_wl, 2 * (i * U + s) + 2)
                    sp.sem_inc(s_past["sp"], 1)
                    sp.wait_ge(e_wd, i * U + s + 1)
                    sp.dma_start(wbuf[s], expert_w[bass.ds((i + 1) * U + s, 1), :, :].rearrange("a p n -> (a p) n")
                                 ).then_inc(e_w[s], 16)
            second = sp.value_load(rank[0:1, U + E - 1:U + E], min_val=0, max_val=E)
            sp.wait_ge(e_sc, 16 * E + second * 16)
            sp.sem_inc(s_past["sp"], 1)

        @block.gpsimd
        def _(pool):
            g = nc.gpsimd
            g.memset(xs[96:P, NT - 1, :], 0.0).then_inc(s_xpad, 1)
            pool.wait_ge(s_xpad, 1)
            g.memset(ident[:, :], 0.0).then_inc(s_idt, 1)
            g.memset(before[:, :], 1.0).then_inc(s_idt, 1)
            pool.wait_ge(s_idt, 2)
            g.affine_select(out=ident[:, :], in_=ident[:, :], compare_op=ALU.not_equal, fill=1.0, base=0,
                            pattern=[[-1, P]], channel_multiplier=1).then_inc(s_cst, 1)
            g.affine_select(out=before[:, :], in_=before[:, :], compare_op=ALU.is_gt, fill=0.0, base=0,
                            pattern=[[1, P]], channel_multiplier=-1).then_inc(s_cst, 1)
            g.iota(iota_h[:, :], [[1, CW]], base=0, channel_multiplier=0,
                   allow_small_or_imprecise_dtypes=True).then_inc(s_cst, 1)
            for b in range(2):
                g.memset(hot_src[b][:, :, N:NPAD], 0.0).then_inc(s_idt, 1)
            pool.wait_ge(s_idt, 4)
            for b in range(2):
                g.memset(hot_src[b][:, :, DEG:NPAD], 1.0).then_inc(s_hot0, 1)
            g.iota(iota_e[:, :], [[1, E]], base=0, channel_multiplier=0,
                   allow_small_or_imprecise_dtypes=True).then_inc(s_cst, 1)
            g.iota(tok_f[:, :], [[P, NT]], base=0, channel_multiplier=1,
                   allow_small_or_imprecise_dtypes=True).then_inc(s_cst, 1)
            g.iota(tok1_f[:, :], [[P, NT]], base=1, channel_multiplier=1,
                   allow_small_or_imprecise_dtypes=True).then_inc(s_cst, 1)
            g.iota(dump_f[:, :], [[1, 1]], base=N + 1, channel_multiplier=1,
                   allow_small_or_imprecise_dtypes=True).then_inc(s_cst, 1)
            g.memset(ones[:, :], 1.0).then_inc(s_cst, 1)
            g.memset(zero_h[:, :], 0.0).then_inc(s_cst, 1)
            g.memset(msum[:, :], 0.0).then_inc(s_cst, 1)
            g.memset(zrow1[:, :], 0.0).then_inc(s_cst, 1)
            g.memset(rank_f[:, :], 0.0).then_inc(s_cst, 1)
            g.memset(counts[:, :, :], 0.0).then_inc(s_cc, 1)
            g.memset(zrows[:, :], 0.0).then_inc(s_z, 1)

            pool.wait_ge(s_xn, 1)
            g.tensor_copy(xw[:, :], xn[:, 0, :]).then_inc(s_xw, 1)
            for c in range(0, DC, 2):
                pool.wait_ge(s_sh, c // 2 + 1)
                g.tensor_tensor(wd_lo[:, c:c + 2, :], ws[:, c:c + 2, :], wd_hi[:, c:c + 2, :].bitcast(F32), ALU.subtract
                                ).then_inc(s_sl, 1)
            with pool.Fori(1, NT) as w:
                pool.wait_ge(s_xn, w + 1)
                pool.sem_inc(s_past["pool"], 1)
                pool.wait_ge(s_xT, w)
                g.tensor_copy(xw[:, :], xn[:, bass.ds(w, 1), :].rearrange("p a n -> p (a n)")).then_inc(s_xw, 1)
            def keep_t(w):
                pool.wait_ge(s_tTc, w + 1)
                g.tensor_copy(t_t[:, bass.ds(w, 1), :].rearrange("p a n -> p (a n)"),
                              tw_t.rearrange("p c m -> p (c m)")).then_inc(s_tk, 1)

            with pool.Fori(0, NT - 2) as w:
                keep_t(w)
            for c in range(DC):
                pool.wait_ge(s_gh, c + 1)
                g.tensor_tensor(wsg_lo[:, c, :], wsg[:, c, :], wsg_hi[:, c, :].bitcast(F32), ALU.subtract).then_inc(s_gl, 1)
            for w in (NT - 2, NT - 1):
                keep_t(w)
            for c in range(0, DC, 2):
                pool.wait_ge(s_dh, c // 2 + 1)
                g.tensor_tensor(wd_lo[:, c:c + 2, :], wsd[:, c:c + 2, :], wd_hi[:, c:c + 2, :].bitcast(F32), ALU.subtract
                                ).then_inc(s_dl, 1)

            pool.wait_ge(s_tst, 16 * NT)
            pool.wait_ge(s_gst, 16)
            pool.wait_ge(s_rest, 32)
            pool.wait_ge(s_tok, 1)
            pool.wait_ge(s_rank, 1)

            def gather(e, s, h, done):
                g.tensor_copy(idxb[h][s][:, :], tokidx[:, bass.ds(2 * e + h, 1)]).then_inc(e_idx, 1)
                pool.wait_ge(e_idx, 1)
                pool.sem_inc(e_idx, -1)
                g.indirect_dma_start(gx[h][s], None, t_dram, bass.IndirectOffsetOnAxis(ap=idxb[h][s][:, :], axis=0)
                                     ).then_inc(done, 16)

            def gather_both(e, s, r0, r1):
                gather(e, s, 0, e_gx[s])
                with pool.If(r1 > r0):
                    with pool.If(r0 > 0):
                        pool.wait_ge(e_gx2, r0 * 16)
                        pool.sem_inc(s_past["pool"], 1)
                    gather(e, s, 1, e_gx2)

            def add(e, s, h):
                g.tensor_copy(idxa[h][:, :], tokidx[:, bass.ds(2 * e + h, 1)]).then_inc(e_idx, 1)
                pool.wait_ge(e_idx, 1)
                pool.sem_inc(e_idx, -1)
                g.indirect_dma_start(out, bass.IndirectOffsetOnAxis(ap=idxa[h][:, :], axis=0), yb[h][s % 2], None,
                                     compute_op=ALU.add).then_inc(e_sc, 16)

            def y_there(e, r0, r1):
                pool.wait_ge(e_yc[0], e + 2)
                pool.sem_inc(s_past["pool"], 1)
                with pool.If(r1 > r0):
                    pool.wait_ge(e_yc[1], r1 + 1)
                    pool.sem_inc(s_past["pool"], 1)

            def down_low(e, s):
                pool.wait_ge(e_wh, 3 * e + 3)
                g.tensor_tensor(w_lo[s % 2][:, WG:WCOL], wbuf[s][:, WG:WCOL], w_hi[s % 2][:, WG:WCOL].bitcast(F32),
                                ALU.subtract).then_inc(e_wd, 1)

            def add_both(e, s, r0, r1):
                if not (isinstance(e, int) and e == 0):
                    pool.wait_ge(e_sc, (e + r0) * 16)
                pool.sem_inc(s_past["pool"], 1)
                add(e, s, 0)
                with pool.If(r1 > r0):
                    add(e, s, 1)

            for s in range(U):
                r0, r1 = (pool.value_load(rank[0:1, U + s - 1 + j:U + s + j], min_val=0, max_val=E) for j in range(2))
                gather_both(s, s, r0, r1)
            pool.wait_ge(s_bst, 16 * (NT - 2))
            pool.wait_ge(s_bst2, 32)

            def step(e, s, r, i):
                if i is not None:
                    pool.wait_ge(e_xT[0], e + 1 - U)
                    pool.wait_ge(e_g[0], e + 1 - U)
                    pool.sem_inc(s_past["pool"], 1)
                    with pool.If(r[2] > r[1]):
                        pool.wait_ge(e_g[1], r[2])
                        pool.sem_inc(s_past["pool"], 1)
                    gather_both(e, s, r[U + 1], r[U + 2])
                if not (isinstance(e, int) and e == U):
                    y_there(e - U - 1, r[0], r[1])
                    add_both(e - U - 1, (s - 1) % U, r[0], r[1])
                if not isinstance(e, int) or e - U + 1 < E:
                    down_low(e - U + 1, (s + 1) % U)

            ranks = Ranks(pool, rank, -2, U)

            def expert_body(i, first=False):
                r = ranks.begin(i, first)
                for s in range(U):
                    step(i * U + s, s, [r.get(j) for j in range(s - 2, U + s + 1)], i)
                    ranks.next(s)
                ranks.hand_over()

            pool.wait_ge(s_dw, NT)
            down_low(0, 0)
            expert_body(1, first=True)
            with pool.Fori(2, E // U) as i:
                expert_body(i)
            r = [pool.value_load(rank[0:1, E + j:E + j + 1], min_val=0, max_val=E) for j in range(-2, U)]
            for s in range(U + 1):
                step(E + s, s, r[s:s + 2], None)

        @block.tensor
        def _(pe):
            T = nc.tensor
            pe.wait_ge(s_cst, 1)
            pe.wait_ge(s_ef, 2)
            for q, a in enumerate((src_f, src_f, dst_f, dst_f)):
                m = T.transpose(ps[0:EP, 6, q * EH:(q + 1) * EH], a[:, q % 2, :], ident[0:EH, 0:EH])
            m.then_inc(s_eT, 1)
            pe.wait_ge(s_ef, 4)
            for q in range(4):
                m = T.transpose(ps[0:1, 7, q * EH:(q + 1) * EH], ends[:, q:q + 1], ident[0:EH, 0:EH])
            m.then_inc(s_eT, 1)

            def count(par, hot):
                for q in range(NT):
                    for t in range(G):
                        m = T.matmul(acc[par][:, q * P:(q + 1) * P], hot_src[par][:, t, q * P:(q + 1) * P], hot[:, t, :],
                                     start=(t == 0), stop=(t == G - 1))
                return m

            def group(g, par):
                pe.wait_ge(s_hs, (g + 1) * G)
                pe.wait_ge(s_hd, g + 1)
                if not isinstance(g, int) or g >= 2:
                    pe.wait_ge(s_cc, g)
                count(par, hot_dst[par]).then_inc(s_cd, 1)
                more = pe.value_load(wtab[0:1, 1, bass.ds(g, 1)], min_val=0, max_val=NT - 1)
                with pe.If(more > 0):
                    base = pe.value_load(wtab[0:1, 2, bass.ds(g, 1)], min_val=0, max_val=NT * NG)
                    with pe.Fori(0, NT - 1) as j:
                        with pe.If(j < more):
                            pe.wait_ge(s_cc, g + 2)
                            pe.wait_ge(m_hot, (base + j + 1) * G)
                            count(par, hot_more).then_inc(m_cnt, 1)
                            pe.wait_ge(m_add, base + j + 1)
                            pe.sem_inc(s_past["pe"], 1)

            def turn(bank, a, done):
                for c in range(DC):
                    m = T.transpose(ps[:, bank, c * P:(c + 1) * P], a[:, c * P:(c + 1) * P], ident[:, :])
                m.then_inc(done, 1)

            def project(bank, a, wt, done, n=D):
                for c in range(DC):
                    m = T.matmul(ps[:, bank, 0:n], a[:, c, :], wt[:, c, :], start=(c == 0), stop=(c == DC - 1))
                m.then_inc(done, 1)

            def project_parts(bank, a, b, done):
                for c in range(DC):
                    for p, (i, j) in enumerate(((0, 0), (0, 1), (1, 0))):
                        m = T.matmul(ps[:, bank, :], a[i][:, c, :], b[j][:, c, :],
                                     start=(c == 0 and p == 0), stop=(c == DC - 1 and p == 2))
                m.then_inc(done, 1)

            def x_turn(w):
                pe.wait_ge(s_xw, w + 1)
                if not isinstance(w, int) or w:
                    pe.wait_ge(s_xTl, w)
                turn(6, xw, s_xT)

            def self_project(w):
                pe.wait_ge(s_xTl, w + 1)
                if not isinstance(w, int) or w:
                    pe.wait_ge(s_selfc, w)
                pe.wait_ge(s_sl, DC // 2)
                project_parts(7, (xT_hi, xT_lo), (wd_hi, wd_lo), s_self)

            pe.wait_ge(s_hot0, 2)
            pe.wait_ge(s_win, 1)
            for g in range(2):
                group(g, g)
            with pe.Fori(1, NT) as i:
                x_turn(i - 1)
                group(i * 2, 0)
                self_project(i - 1)
                group(i * 2 + 1, 1)
            x_turn(NT - 1)
            self_project(NT - 1)

            pe.wait_ge(s_cc, NG + 1)
            pe.wait_ge(s_selfc, NT)
            for w in range(NT):
                m = T.matmul(ps[:, 3, w:w + 1], counts[:, NT - 1, w * P:(w + 1) * P], ident[:, P - 1:P], start=True, stop=True)
            m.then_inc(s_deg, 1)

            def neigh(k, half):
                if not isinstance(k, int) or k:
                    pe.wait_ge(s_nsc, 2 * k + half - 1)
                for c in (2 * half, 2 * half + 1):
                    for q in range(NT):
                        m = T.matmul(ps[:, 5 + half, (c % 2) * 2 * P:(c % 2 + 1) * 2 * P], xn[:, q, c * P:(c + 1) * P],
                                     counts[:, q, bass.ds(k * 2 * P, 2 * P)], start=(q == 0), stop=(q == NT - 1))
                m.then_inc(s_ns, 1)

            def neigh_project(w, side):
                if side == 0:
                    pe.wait_ge(s_nsc, w + 2)
                if not isinstance(w, int) or w:
                    pe.wait_ge(s_h, w)
                project(7, nsum_t[:, :, side * P:(side + 1) * P], wn, s_nb)

            def t_route(w):
                pe.wait_ge(s_t, w + 1)
                turn(3, tw, s_tT)
                pe.wait_ge(s_tTc, w + 1)
                project(4, tw_t, rw, s_lg, E)

            neigh(0, 0)
            neigh(0, 1)
            pe.wait_ge(s_wn, 16)
            pe.wait_ge(s_rw, 16)
            pe.wait_ge(s_rdeg, 1)
            with pe.Fori(1, NP) as k:
                for side in range(2):
                    neigh_project(2 * k - 2 + side, side)
                    neigh(k, side)
                    t_route(2 * k - 2 + side)
            def gate_(w, par):
                pe.wait_ge(s_ttl, w + 1)
                if not isinstance(w, int) or w:
                    pe.wait_ge(s_silu, w)
                project_parts(0, (tt_hi[par], tt_lo[par]), (wsg_hi[:, :, 0:D], wsg_lo[:, :, 0:D]), s_ga)

            def up_(w, par):
                if not isinstance(w, int) or w:
                    pe.wait_ge(s_hm, w)
                project_parts(1, (tt_hi[par], tt_lo[par]), (wsg_hi[:, :, D:2 * D], wsg_lo[:, :, D:2 * D]), s_up)

            neigh_project(NT - 2, 0)
            t_route(NT - 2)
            neigh_project(NT - 1, 1)
            pe.wait_ge(s_gl, DC)
            gate_(0, 0)
            up_(0, 0)
            t_route(NT - 1)

            def down(w):
                pe.wait_ge(s_hTl, w + 1)
                if isinstance(w, int) and w == 0:
                    pe.wait_ge(s_dl, DC // 2)
                if not isinstance(w, int) or w:
                    pe.wait_ge(s_base, w)
                project_parts(3, (hsh_hi, hsh_lo), (wd_hi, wd_lo), s_dw)

            def hidden_T(w):
                pe.wait_ge(s_hm, w + 1)
                turn(2, hsh, s_hT)

            def prefix(w):
                pe.wait_ge(s_mask, w + 1)
                T.matmul(ps[:, 4, 0:E], before[:, :], mask[:, :], start=True, stop=False)
                T.matmul(ps[:, 4, 0:E], ones[:, :], msum[:, :], start=False, stop=True).then_inc(s_pre, 1)

            def table(w):
                pe.wait_ge(s_hl, w + 1)
                for k in range(TOPK):
                    m = T.matmul(ps[:, 5, 0:P], hot_lo[:, k, :], hot_hi[:, k, :], start=False, stop=False,
                                 skip_group_check=True)
                m.then_inc(s_tab, 1)

            pe.wait_ge(s_cst, 12)
            pe.wait_ge(s_lgc, NT)
            T.matmul(ps[:, 5, 0:P], zero_h[:, :], zero_h[:, :], start=True, stop=False, skip_group_check=True)

            def shared(w, par, first=False):
                if not first:
                    gate_(w, par)
                    hidden_T(w - 1)
                    up_(w, par)
                prefix(w)
                if not first:
                    down(w - 1)
                    table(w - 1)

            shared(0, 0, True)
            shared(1, 1)
            with pe.Fori(1, NT // 2) as i:
                shared(i * 2, 0)
                shared(i * 2 + 1, 1)
            hidden_T(NT - 1)
            down(NT - 1)
            table(NT - 1)
            T.matmul(ps[:, 5, 0:P], zero_h[:, :], zero_h[:, :], start=False, stop=True,
                     skip_group_check=True).then_inc(s_tab, 1)
            pe.wait_ge(s_mask, NT + 1)
            T.matmul(ps[0:1, 6, 0:E], ones[:, 0:1], msum[:, :], start=True, stop=True).then_inc(s_cnt, 1)

            pe.wait_ge(s_tok, 1)
            pe.wait_ge(s_rank, 1)
            for h in range(2):
                for q in (e_gu, e_hT, e_y):
                    pe.sem_inc(q[h], 1)

            def rows_T(h, s, n):
                pe.wait_ge(e_xl[h], n)
                for c in range(DC):
                    m = T.transpose(ps[:, 4 * h, c * P:(c + 1) * P], gx[h][s][:, c * P:(c + 1) * P], ident[:, :])
                m.then_inc(e_xT[h], 1)

            def three_passes(bank, a, b, chunks, column):
                for c in range(chunks):
                    for p, (i, j) in enumerate(((0, 0), (0, 1), (1, 0))):
                        m = T.matmul(ps[:, bank, :], a[i][:, c, :], b[j][:, column + c * D:column + (c + 1) * D],
                                     start=(c == 0 and p == 0), stop=(c == chunks - 1 and p == 2))
                return m

            def gate_up(h, s, n):
                pe.wait_ge(e_xl[h], n + 1)
                pe.wait_ge(e_h[h], n)
                three_passes(4 * h + 1, [x[h][s % 2] for x in xt], [w_hi[s % 2], w_lo[s % 2]], DC, 0).then_inc(e_gu[h], 1)

            def hid_T(h, n):
                pe.wait_ge(e_h[h], n + 1)
                pe.wait_ge(e_hl[h], n)
                for c in range(FC):
                    m = T.transpose(ps[:, 4 * h + 2, c * P:(c + 1) * P], hh[h][:, c * P:(c + 1) * P], ident[:, :])
                m.then_inc(e_hT[h], 1)

            def down_y(h, s, n):
                pe.wait_ge(e_hl[h], n + 1)
                pe.wait_ge(e_yc[h], n)
                three_passes(4 * h + 3, [x[h] for x in ht], [w_hi[s % 2], w_lo[s % 2]], FC, WG).then_inc(e_y[h], 1)

            def rows_T_both(e, s, turn_no, r0, r1):
                pe.wait_ge(e_gx[s], turn_no * 16)
                rows_T(0, s, e + 1)
                with pe.If(r1 > r0):
                    pe.wait_ge(e_gx2, r1 * 16)
                    rows_T(1, s, r1)

            def down_both(e, s, r0, r1):
                if isinstance(e, int) and e == 0:
                    pe.wait_ge(s_base, NT)
                pe.wait_ge(e_wd, e + 1)
                down_y(0, s, e + 1)
                with pe.If(r1 > r0):
                    down_y(1, s, r1)

            ranks = Ranks(pe, rank, U - 2, U + 1)

            def expert_body(i, first=False, last=False):
                r = ranks.begin(i, first)
                if first:
                    rows_T_both(0, 0, 1, r[U - 1], r[U])
                    rows_T_both(1, 1, 1, r[U], r[U + 1])
                for s in range(U):
                    e = i * U + s
                    pe.wait_ge(e_wl, 2 * e + 2)
                    gate_up(0, s, e + 1)
                    ranks.next(s)
                    with pe.If(r[U + s] > r[U + s - 1]):
                        gate_up(1, s, r[U + s])
                    if not (first and s == 0):
                        down_both(e - 1, (s - 1) % U, r[U + s - 2], r[U + s - 1])
                    if not (last and s >= U - 2):
                        rows_T_both(e + 2, (s + 2) % U, i + 1 + (s + 2) // U, r[U + s + 1], r[U + s + 2])
                    hid_T(0, e + 1)
                    with pe.If(r[U + s] > r[U + s - 1]):
                        hid_T(1, r[U + s])
                if last:
                    down_both(E - 1, U - 1, r[2 * U - 2], r[2 * U - 1])
                else:
                    ranks.hand_over()

            expert_body(0, first=True)
            with pe.Fori(1, E // U - 1) as i:
                expert_body(i)
            expert_body(E // U - 1, last=True)

        @block.scalar
        def _(act):
            A = nc.scalar

            def later(w):
                return not isinstance(w, int) or w > 0

            def flat(a):
                return a.rearrange("p a n -> p (a n)")

            def hot_window(g, par):
                w = act.value_load(wtab[0:1, 0, bass.ds(g, 1)], min_val=0, max_val=N - 1)
                if not isinstance(g, int) or g >= 1:
                    act.wait_ge(s_hd, g)
                for t in range(G):
                    m = A.activation(dist[:, t, :], iota_h[0:EP, bass.ds(w, P)], ACT.Abs, scale=-1.0,
                                     bias=edge[:, bass.ds(ET + g * G + t, 1)])
                m.then_inc(s_dist, 1)
                act.wait_ge(s_dist, g + 1)
                if not isinstance(g, int) or g >= 2:
                    act.wait_ge(s_cd, g - 1)
                A.activation(hot_dst[par][:, :, :], dist[:, :, :], ACT.Relu, scale=-1.0, bias=1.0).then_inc(s_hd, 1)

            def x_T(w):
                act.wait_ge(s_xT, w + 1)
                if later(w):
                    act.wait_ge(s_self, w)
                A.activation(flat(xT_hi[:, :, :]), ps[:, 6, :], ACT.Copy).then_inc(s_xTc, 1)

            def normalise(w):
                A.activation(flat(xn[:, bass.ds(w, 1), :]), flat(xs[:, bass.ds(w, 1), :]), ACT.Identity,
                             scale=rs[:, bass.ds(w, 1)], bias=shift[:, bass.ds(w, 1)]).then_inc(s_xn, 1)

            act.wait_ge(s_win, 1)
            act.wait_ge(s_cst, 3)
            hot_window(0, 0)
            hot_window(1, 1)
            act.wait_ge(s_var, 1)
            A.activation(sd[:, :], ve[:, :], ACT.Sqrt).then_inc(s_sqrt, 1)
            act.wait_ge(s_ln, 1)
            normalise(0)
            act.wait_ge(s_w, 16)
            for c in range(0, DC, 2):
                A.activation(flat(wd_hi[:, c:c + 2, :]), flat(ws[:, c:c + 2, :]), ACT.Copy).then_inc(s_sh, 1)
            with act.Fori(1, NT) as i:
                hot_window(2 * i, 0)
                normalise(i)
                x_T(i - 1)
                hot_window(2 * i + 1, 1)
            x_T(NT - 1)

            def neigh(k, half):
                act.wait_ge(s_ns, 2 * k + half + 1)
                if later(k):
                    act.wait_ge(s_nb, 2 * k)
                A.activation(nsum_t[:, 2 * half:2 * half + 2, :].rearrange("p c m -> p (c m)"), ps[:, 5 + half, :], ACT.Copy
                             ).then_inc(s_nsc, 1)

            def roots(w):
                for j, st in enumerate((st1, st2)):
                    act.wait_ge(s_var, 2 * w + j + 2)
                    A.activation(st[:, 9:10], st[:, 8:9], ACT.Sqrt).then_inc(s_sqrt, 1)

            neigh(0, 0)
            neigh(0, 1)
            with act.Fori(1, NP) as k:
                roots(2 * k - 2)
                roots(2 * k - 1)
                neigh(k, 0)
                neigh(k, 1)

            def stage(w, par):
                act.wait_ge(s_tk, w + 1)
                if not isinstance(w, int) or w >= 2:
                    act.wait_ge(s_up, w - 1)
                A.activation(flat(tt_hi[par][:, :, :]), flat(t_t[:, bass.ds(w, 1), :]), ACT.Copy).then_inc(s_tt2, 1)

            act.wait_ge(s_self, NT)
            stage(0, 0)
            act.wait_ge(s_gu, 16)
            act.wait_ge(s_ns, 2 * NP)
            for c in range(DC):
                A.activation(wsg_hi[:, c, :], wsg[:, c, :], ACT.Copy).then_inc(s_gh, 1)
            roots(NT - 2)
            roots(NT - 1)
            act.wait_ge(s_lgc, NT)
            A.activation(flat(gates[:, :, :]), flat(logits[:, :, :]), ACT.Exp).then_inc(s_exp, 1)
            A.activation(flat(ex6[:, :, :]), flat(ex6[:, :, :]), ACT.Exp).then_inc(s_exp, 1)

            def silu(w):
                act.wait_ge(s_ga, w + 1)
                if later(w):
                    act.wait_ge(s_hm, w)
                A.activation(sg[:, :], ps[:, 0, :], ACT.Silu).then_inc(s_silu, 1)

            def hidden_T(w):
                act.wait_ge(s_hT, w + 1)
                if later(w):
                    act.wait_ge(s_dw, w)
                A.activation(flat(hsh_hi[:, :, :]), ps[:, 2, :], ACT.Copy).then_inc(s_hTc, 1)

            stage(1, 1)
            act.wait_ge(s_t, NT)
            silu(0)
            act.wait_ge(s_dn, 16)
            act.wait_ge(s_nb, NT)
            for c in range(0, DC, 2):
                A.activation(flat(wd_hi[:, c:c + 2, :]), flat(wsd[:, c:c + 2, :]), ACT.Copy).then_inc(s_dh, 1)
            silu(1)
            hidden_T(0)
            with act.Fori(1, NT // 2) as i:
                for par in range(2):
                    stage(2 * i + par, par)
                    silu(2 * i + par)
                    hidden_T(2 * i + par - 1)
            hidden_T(NT - 1)
            for h in range(2):
                act.sem_inc(e_yc[h], 1)

            def w_high(e, s, n, part, r):
                if part == 0:
                    act.wait_ge(e_w[s], n * 16)
                if r is not None:
                    used = e_y if part == 2 else e_gu
                    act.wait_ge(used[0], e)
                    act.wait_ge(used[1], r + 1)
                cols = slice(part * WPART, (part + 1) * WPART)
                A.activation(w_hi[s % 2][:, cols], wbuf[s][:, cols], ACT.Copy).then_inc(e_wh, 1)

            def x_high(h, s, n, gu):
                act.wait_ge(e_xT[h], n)
                act.wait_ge(e_gu[h], gu)
                A.activation(flat(xt[0][h][s % 2][:, :, :]), ps[:, 4 * h, :], ACT.Copy).then_inc(e_xh[h], 1)

            def e_silu(h, n):
                act.wait_ge(e_gu[h], n + 1)
                act.wait_ge(e_h[h], n)
                A.activation(sil[h][:, :], ps[:, 4 * h + 1, 0:F], ACT.Silu).then_inc(e_si[h], 1)

            def h_high(h, n):
                act.wait_ge(e_hT[h], n + 1)
                act.wait_ge(e_y[h], n)
                A.activation(flat(ht[0][h][:, :, :]), ps[:, 4 * h + 2, 0:F], ACT.Copy).then_inc(e_hh[h], 1)

            def y_scaled(h, e, s, n):
                act.wait_ge(e_g[h], n)
                act.wait_ge(e_y[h], n + 1)
                A.activation(yb[h][s % 2], ps[:, 4 * h + 3, :], ACT.Copy, scale=kept[h][s][:, :]
                             ).then_inc(e_yc[h], 1)

            def y_both(e, s, added, r0, r1):
                if added is not None:
                    act.wait_ge(e_sc, (e - 1 + added) * 16)
                y_scaled(0, e, s, e + 1)
                with act.If(r1 > r0):
                    y_scaled(1, e, s, r1)

            ranks = Ranks(act, rank, U - 3, U + 1)

            def expert_body(i, first=False, last=False):
                if first:
                    act.wait_ge(s_up, NT)
                    for part in range(3):
                        w_high(0, 0, 1, part, None)
                    act.wait_ge(s_dw, NT)
                    act.wait_ge(s_tab, NT + 1)
                    act.wait_ge(s_bst, 16 * (NT - 2))
                    act.wait_ge(s_rank, 1)
                r = ranks.begin(i, first)
                if first:
                    for s in range(2):
                        x_high(0, s, s + 1, 1)
                        with act.If(r[U + s] > r[U + s - 1]):
                            x_high(1, s, r[U + s], 1)
                for s in range(U):
                    e = i * U + s
                    s1 = (s + 1) % U
                    before = None if first and s == 0 else r[U + s - 1]
                    if not (last and s == U - 1):
                        for part in range(2):
                            w_high(e + 1, s1, i + 1 + (s + 1) // U, part, before)
                    ranks.next(s)
                    e_silu(0, e + 1)
                    with act.If(r[U + s] > r[U + s - 1]):
                        e_silu(1, r[U + s])
                    if not (first and s == 0):
                        y_both(e - 1, (s - 1) % U, None if first and s <= 2 else r[U + s - 3],
                               r[U + s - 2], r[U + s - 1])
                    if not (last and s >= U - 2):
                        s2 = (s + 2) % U
                        x_high(0, s2, e + 3, e + 2)
                        with act.If(r[U + s + 2] > r[U + s + 1]):
                            x_high(1, s2, r[U + s + 2], r[U + s] + 1)
                    h_high(0, e + 1)
                    with act.If(r[U + s] > r[U + s - 1]):
                        h_high(1, r[U + s])
                    if not (last and s == U - 1):
                        w_high(e + 1, s1, i + 1 + (s + 1) // U, 2, before)
                if last:
                    y_both(E - 1, U - 1, r[2 * U - 3], r[2 * U - 2], r[2 * U - 1])
                else:
                    ranks.hand_over()

            expert_body(0, first=True)
            with act.Fori(1, E // U - 1) as i:
                expert_body(i)
            expert_body(E // U - 1, last=True)

        @block.vector
        def _(dve):
            V = nc.vector
            own = Steps(dve, dv)

            def later(w):
                return not isinstance(w, int) or w > 0

            def flat(a):
                return a.rearrange("p a n -> p (a n)")

            dve.wait_ge(s_dst, 16)
            V.tensor_copy(dst_f[:, :, :], dst_i[:, :, :]).then_inc(s_ef, 1)
            dve.wait_ge(s_src, 16)
            V.tensor_copy(src_f[:, :, :], src_i[:, :, :]).then_inc(s_ef, 1)
            dve.wait_ge(s_ef, 2)
            V.tensor_reduce(ends[:, 0:2], dst_f[:, :, :], AX.X, ALU.min).then_inc(s_ef, 1)
            V.tensor_reduce(ends[:, 2:4], dst_f[:, :, :], AX.X, ALU.max).then_inc(s_ef, 1)
            dve.wait_ge(s_eT, 1)
            own.mark(V.tensor_copy(edge[:, :], ps[0:EP, 6, 0:4 * EH]))
            dve.wait_ge(s_eT, 2)
            for j, op in enumerate((ALU.min, ALU.max)):
                own.mark(V.tensor_reduce(wrow[0:1, j, :], ps[0:1, 7, j * ET:(j + 1) * ET].rearrange("p (g t) -> p g t", t=G),
                                         AX.X, op))
            own.wait()
            own.mark(V.tensor_copy(wtab_f[:, 0, :], wrow[:, 0, :]))
            own.mark(V.tensor_tensor(wrow[:, 1, :], wrow[:, 1, :], wrow[:, 0, :], ALU.subtract))
            own.wait()
            own.mark(V.tensor_copy(wint[:, 0, :], wrow[:, 1, :]))
            own.wait()
            own.mark(V.tensor_single_scalar(wint[:, 0, :], wint[:, 0, :], 7, ALU.arith_shift_right))
            own.wait()
            own.mark(V.tensor_copy(wtab_f[:, 1, :], wint[:, 0, :]))
            own.wait()
            dve.wait_ge(s_cst, 12)
            own.mark(V.tensor_tensor_scan(wtab_f[:, 2, :], zrow1[:, 0:NG], wtab_f[:, 1, :], 0.0, ALU.add, ALU.add))
            own.wait()
            own.mark(V.tensor_tensor(wtab_f[:, 2, :], wtab_f[:, 2, :], wtab_f[:, 1, :], ALU.subtract))
            own.wait()
            V.tensor_copy(wtab[:, :, :], wtab_f[:, :, :]).then_inc(s_win, 1)
            dve.wait_ge(s_win, 1)
            dve.wait_ge(s_hot0, 2)

            def hot_rows(g, par):
                if not isinstance(g, int) or g >= 2:
                    dve.wait_ge(s_cd, g - 1)
                for t in range(G):
                    V.tensor_scalar(hot_src[par][:, t, 0:N], iota_h[0:EP, 0:N],
                                    edge[:, bass.ds(g * G + t, 1)], None, ALU.is_equal).then_inc(s_hs, 1)

            def add_counts(w, par):
                cells = counts[:, :, bass.ds(w, P)]
                return V.tensor_tensor(cells, acc[par][:, 0:NPAD].rearrange("p (q m) -> p q m", q=NT), cells, ALU.add)

            def add_group(g, par):
                w = dve.value_load(wtab[0:1, 0, bass.ds(g, 1)], min_val=0, max_val=N - 1)
                more = dve.value_load(wtab[0:1, 1, bass.ds(g, 1)], min_val=0, max_val=NT - 1)
                dve.wait_ge(s_cd, g + 1)
                dve.wait_ge(s_cc, g + 1)
                add_counts(w, par).then_inc(s_cc, 1)
                with dve.If(more > 0):
                    base = dve.value_load(wtab[0:1, 2, bass.ds(g, 1)], min_val=0, max_val=NT * NG)
                    with dve.Fori(0, NT - 1) as j:
                        with dve.If(j < more):
                            dve.wait_ge(s_cc, g + 2)
                            v = nc.s_assert_within(w + (j + 1) * P, 0, N - 1, skip_runtime_bounds_check_because="the last window of a group starts at its last node or before it")
                            for t in range(G):
                                m = V.tensor_scalar(hot_more[:, t, :], iota_h[0:EP, bass.ds(v, P)],
                                                    edge[:, bass.ds(ET + g * G + t, 1)], None, ALU.is_equal)
                                m.then_inc(m_hot, 1)
                            dve.wait_ge(m_cnt, base + j + 1)
                            add_counts(v, par).then_inc(m_add, 1)
                            dve.wait_ge(m_add, base + j + 1)
                            dve.sem_inc(s_past["dve"], 1)

            def keep_self(w):
                dve.wait_ge(s_self, w + 1)
                V.tensor_tensor(flat(t_t[:, bass.ds(w, 1), :]), ps[:, 7, :], bias_b[:, :], ALU.add).then_inc(s_selfc, 1)

            def x_low(w):
                dve.wait_ge(s_xTc, w + 1)
                V.tensor_tensor(flat(xT_lo[:, :, :]), ps[:, 6, :], flat(xT_hi[:, :, :]).bitcast(F32), ALU.subtract
                                ).then_inc(s_xTl, 1)

            hot_rows(0, 0)
            hot_rows(1, 1)

            dve.wait_ge(s_x, 32)
            for w in range(NT):
                own.mark(V.bn_stats(stat[:, w, :], xs[:, w, :]))
            own.wait()
            for w in range(NT):
                own.mark(V.bn_aggr(mv[:, w, :], stat[:, w, :]))
            own.wait()
            V.tensor_scalar(ve[:, :], mv[:, :, 1], EPS, None, ALU.add).then_inc(s_var, 1)
            dve.wait_ge(s_sqrt, 1)

            def inv_sqrt(r, q, root, v):
                own.mark(V.reciprocal(r, root))
                own.wait()
                own.mark(V.tensor_tensor(q, r, r, ALU.mult))
                own.wait()
                own.mark(V.tensor_tensor(q, q, v, ALU.mult))
                own.wait()
                own.mark(V.tensor_scalar(q, q, -0.5, 1.5, ALU.mult, ALU.add))
                own.wait()
                own.mark(V.tensor_tensor(r, r, q, ALU.mult))
                own.wait()

            inv_sqrt(rs[:, :], rq[:, :], sd[:, :], ve[:, :])
            V.scalar_tensor_tensor(out=shift[:, :], in0=mv[:, :, 0], scalar=-1.0, in1=rs[:, :], op0=ALU.mult, op1=ALU.mult
                                   ).then_inc(s_ln, 1)
            own.mark(V.tensor_scalar(valid[:, :], tok_f[:, :], float(N), None, ALU.is_lt))
            own.wait()
            own.mark(V.tensor_scalar(vm1[:, :], valid[:, :], 1.0, None, ALU.subtract))

            dve.wait_ge(s_vec, 64)
            add_group(0, 0)
            dve.wait_ge(s_rest, 32)
            own.restart()
            with dve.Fori(1, NT) as i:
                hot_rows(2 * i, 0)
                add_group(2 * i - 1, 1)
                x_low(i - 1)
                hot_rows(2 * i + 1, 1)
                add_group(2 * i, 0)
                keep_self(i - 1)
                own.restart()
            add_group(NG - 1, 1)
            x_low(NT - 1)
            keep_self(NT - 1)
            dve.wait_ge(s_cc, NG + 1)

            dve.wait_ge(s_deg, 1)
            own.mark(V.tensor_scalar(deg[:, :], ps[:, 3, 0:NT], 1.0, None, ALU.max))
            own.wait()
            V.reciprocal(rdeg[:, :], deg[:, :]).then_inc(s_rdeg, 1)
            dve.wait_ge(s_rdeg, 1)

            def norm(st, a, at):
                own.mark(V.bn_stats(st[:, 0:6], a))
                own.wait()
                own.mark(V.bn_aggr(st[:, 6:8], st[:, 0:6]))
                own.wait()
                V.tensor_scalar(st[:, 8:9], st[:, 7:8], EPS, None, ALU.add).then_inc(s_var, 1)
                dve.wait_ge(s_sqrt, at)
                inv_sqrt(st[:, 10:11], st[:, 11:12], st[:, 9:10], st[:, 8:9])

            def tile(w):
                xrow = flat(xs[:, bass.ds(w, 1), :])
                dve.wait_ge(s_nb, w + 1)
                V.scalar_tensor_tensor(out=h0[:, :], in0=ps[:, 7, :], scalar=rdeg[:, bass.ds(w, 1)],
                                       in1=flat(t_t[:, bass.ds(w, 1), :]), op0=ALU.mult, op1=ALU.add).then_inc(s_h, 1)
                dve.wait_ge(s_h, w + 1)
                norm(st1, h0[:, :], 2 * w + 2)
                own.mark(V.scalar_tensor_tensor(out=h1[:, :], in0=h0[:, :], scalar=st1[:, 6:7], in1=gamma_b[:, :],
                                                op0=ALU.subtract, op1=ALU.mult))
                own.wait()
                own.mark(V.scalar_tensor_tensor(out=h0[:, :], in0=h1[:, :], scalar=st1[:, 10:11], in1=beta_b[:, :],
                                                op0=ALU.mult, op1=ALU.add))
                own.wait()
                own.mark(V.tensor_tensor(xrow, xrow, h0[:, :], ALU.add))
                own.wait()
                norm(st2, xrow, 2 * w + 3)
                if later(w):
                    dve.wait_ge(s_tst, w * 16)
                V.tensor_scalar(tw[:, :], xrow, st2[:, 6:7], st2[:, 10:11], ALU.subtract, ALU.mult).then_inc(s_t, 1)

            def router(w):
                dve.wait_ge(s_tT, w + 1)
                if later(w):
                    dve.wait_ge(s_tk, w)
                V.tensor_copy(flat(tw_t[:, :, :]), ps[:, 3, :]).then_inc(s_tTc, 1)
                dve.wait_ge(s_lg, w + 1)
                own.mark(V.tensor_tensor(lgw[:, :], ps[:, 4, 0:E], rb[:, :], ALU.add))
                own.wait()
                own.mark(V.max(v8w[:, :], lgw[:, :]))
                own.wait()
                own.mark(V.max_index(i8[:, :], v8w[:, :], lgw[:, :]))
                own.mark(V.tensor_scalar(flat(ex6[:, bass.ds(w, 1), :]), v8w[:, 0:TOPK], v8w[:, 0:1], None, ALU.subtract))
                own.mark(V.tensor_scalar(flat(logits[:, bass.ds(w, 1), :]), lgw[:, :], v8w[:, 0:1], None, ALU.subtract))
                own.wait()
                V.tensor_copy(flat(i6_all[:, bass.ds(w, 1), :]), i8[:, 0:TOPK]).then_inc(s_lgc, 1)
                dve.wait_ge(s_lgc, w + 1)

            own.restart()
            def stage_low(w, par):
                dve.wait_ge(s_tt2, w + 1)
                if not isinstance(w, int) or w >= 2:
                    dve.wait_ge(s_up, w - 1)
                V.tensor_tensor(flat(tt_lo[par][:, :, :]), flat(t_t[:, bass.ds(w, 1), :]),
                                flat(tt_hi[par][:, :, :]).bitcast(F32), ALU.subtract).then_inc(s_ttl, 1)

            with dve.Fori(0, NT - 2) as w:
                tile(w)
                router(w)
                own.restart()
            dve.wait_ge(s_ns, 2 * NP)
            stage_low(0, 0)
            for w in (NT - 2, NT - 1):
                tile(w)
                router(w)
            own.restart()

            def choose(w):
                ok, okm = valid[:, bass.ds(w, 1)], vm1[:, bass.ds(w, 1)]
                own.mark(V.tensor_scalar(i6[:, :], flat(i6_all[:, bass.ds(w, 1), :]), ok, okm, ALU.mult, ALU.add))
                own.wait()
                own.mark(V.tensor_tensor(hot_e[:, :, :], iota_e[:, :].rearrange("p (a e) -> p a e", a=1).broadcast_to([P, TOPK, E]),
                                         i6[:, :].rearrange("p (k a) -> p k a", a=1).broadcast_to([P, TOPK, E]), ALU.is_equal))
                own.wait()
                if later(w):
                    dve.wait_ge(s_pre, w)
                    own.mark(V.tensor_tensor(msum[:, :], msum[:, :], mask[:, :], ALU.add))
                    own.wait()
                with nc.allow_low_precision("0 or 1"):
                    V.tensor_reduce(mask[:, :], hot_e[:, :, :].rearrange("p k e -> p e k"), AX.X, ALU.add).then_inc(s_mask, 1)

            def place(w):
                ok = valid[:, bass.ds(w, 1)]
                dve.wait_ge(s_pre, w + 1)
                own.mark(V.tensor_tensor(hot_s[:, :, :], ps[:, 4, 0:E].rearrange("p (a e) -> p a e", a=1).broadcast_to([P, TOPK, E]),
                                         hot_e[:, :, :], ALU.mult))
                own.wait()
                own.mark(V.tensor_reduce(slot[:, :], hot_s[:, :, :], AX.X, ALU.add))
                own.wait()
                own.mark(V.tensor_scalar(keep[:, :], slot[:, :], float(CAP), ok, ALU.is_lt, ALU.mult))
                own.mark(V.tensor_scalar(half[:, :], slot[:, :], float(P), None, ALU.is_ge))
                own.wait()
                own.mark(V.scalar_tensor_tensor(out=lo[:, :], in0=half[:, :], scalar=float(-P), in1=slot[:, :],
                                                op0=ALU.mult, op1=ALU.add))
                own.mark(V.scalar_tensor_tensor(out=hi[:, :], in0=i6[:, :], scalar=2.0, in1=half[:, :],
                                                op0=ALU.mult, op1=ALU.add))
                own.wait()
                own.mark(V.scalar_tensor_tensor(out=hi[:, :], in0=hi[:, :], scalar=1.0, in1=keep[:, :],
                                                op0=ALU.add, op1=ALU.mult))
                own.wait()
                own.mark(V.tensor_scalar(hi[:, :], hi[:, :], -1.0, None, ALU.add))
                own.wait()

            def table_rows(w):
                if later(w):
                    dve.wait_ge(s_tab, w)
                for k in range(TOPK):
                    own.mark(V.tensor_scalar(hot_lo[:, k, :], iota_h[:, 0:P], lo[:, k:k + 1], tok1_f[:, bass.ds(w, 1)],
                                             ALU.is_equal, ALU.mult))
                    m = V.tensor_scalar(hot_hi[:, k, :], iota_h[:, 0:P], hi[:, k:k + 1], None, ALU.is_equal)
                    if k < TOPK - 1:
                        own.mark(m)
                own.wait()
                m.then_inc(s_hl, 1)

            def hidden(w):
                dve.wait_ge(s_silu, w + 1)
                dve.wait_ge(s_up, w + 1)
                if later(w):
                    dve.wait_ge(s_hT, w)
                V.tensor_tensor(hsh[:, :], ps[:, 1, :], sg[:, :], ALU.mult).then_inc(s_hm, 1)

            def base_row(w):
                xrow = flat(xs[:, bass.ds(w, 1), :])
                dve.wait_ge(s_dw, w + 1)
                V.scalar_tensor_tensor(out=xrow, in0=ps[:, 3, :], scalar=1.0 / SH, in1=xrow,
                                       op0=ALU.mult, op1=ALU.add).then_inc(s_base, 1)

            choose(0)
            stage_low(1, 1)
            dve.wait_ge(s_exp, 2)
            own.mark(V.tensor_reduce(zsum[:, 0, :], gates[:, :, :], AX.X, ALU.add))
            own.mark(V.tensor_reduce(zsum[:, 1, :], ex6[:, :, :], AX.X, ALU.add))
            own.wait()
            own.mark(V.scalar_tensor_tensor(out=rden[:, :], in0=zsum[:, 0, :], scalar=1e-9, in1=zsum[:, 1, :],
                                            op0=ALU.mult, op1=ALU.add))
            own.wait()
            own.mark(V.reciprocal(rden[:, :], rden[:, :]))
            own.wait()
            V.tensor_tensor(gates[:, :, :], gates[:, :, :],
                            rden[:, :].rearrange("p (w a) -> p w a", a=1).broadcast_to([P, NT, E]), ALU.mult).then_inc(s_gate, 1)
            place(0)
            hidden(0)
            table_rows(0)
            own.restart()

            def hidden_low(w):
                dve.wait_ge(s_hTc, w + 1)
                V.tensor_tensor(flat(hsh_lo[:, :, :]), ps[:, 2, :], flat(hsh_hi[:, :, :]).bitcast(F32), ALU.subtract
                                ).then_inc(s_hTl, 1)

            def shared_step(w, par, last=False):
                choose(w)
                hidden_low(w - 1)
                if not last:
                    stage_low(w + 1, 1 - par)
                place(w)
                hidden(w)
                base_row(w - 1)
                table_rows(w)
                own.restart()

            with dve.Fori(0, NT // 2 - 1) as i:
                shared_step(2 * i + 1, 1)
                shared_step(2 * i + 2, 0)
            shared_step(NT - 1, 1, last=True)
            hidden_low(NT - 1)
            dve.wait_ge(s_pre, NT)
            own.mark(V.tensor_tensor(msum[:, :], msum[:, :], mask[:, :], ALU.add))
            own.wait()
            dve.sem_inc(s_mask, 1)
            dve.wait_ge(s_tab, NT + 1)
            own.mark(V.tensor_scalar(empty[:, :], ps[:, 5, 0:2 * E], 0.0, dump_f[:, :], ALU.is_equal, ALU.mult))
            own.wait()
            V.scalar_tensor_tensor(out=tokidx[:, :], in0=ps[:, 5, 0:2 * E], scalar=-1.0, in1=empty[:, :],
                                   op0=ALU.add, op1=ALU.add).then_inc(s_tok, 1)
            dve.wait_ge(s_cnt, 1)
            own.mark(V.tensor_scalar(cnt[:, :], ps[0:1, 6, 0:E], float(P), None, ALU.is_gt))
            own.wait()
            own.mark(V.tensor_tensor_scan(rank_f[:, U:U + E], zrow1[:, :], cnt[:, :], 0.0, ALU.add, ALU.add))
            own.wait()
            V.tensor_copy(rank[:, :], rank_f[:, :]).then_inc(s_rank, 1)
            dve.wait_ge(s_rank, 1)
            base_row(NT - 1)
            for q in (e_xl, e_h, e_hl):
                for h in range(2):
                    dve.sem_inc(q[h], 1)

            def w_low(e, s, part):
                dve.wait_ge(e_wh, 3 * e + part + 1)
                cols = slice(part * WPART, (part + 1) * WPART)
                V.tensor_tensor(w_lo[s % 2][:, cols], wbuf[s][:, cols], w_hi[s % 2][:, cols].bitcast(F32), ALU.subtract
                                ).then_inc(e_wl, 1)

            def x_low(h, e, s, n, scaled):
                dve.wait_ge(e_xh[h], n)
                V.tensor_tensor(flat(xt[1][h][s % 2][:, :, :]), ps[:, 4 * h, :], flat(xt[0][h][s % 2][:, :, :]).bitcast(F32),
                                ALU.subtract).then_inc(e_xl[h], 1)
                if scaled is not None:
                    dve.wait_ge(e_yc[h], scaled + 1)
                V.tensor_copy(kept[h][s][:, :], gx[h][s][:, bass.ds(D + e, 1)]).then_inc(e_g[h], 1)

            def hid(h, n):
                dve.wait_ge(e_si[h], n)
                dve.wait_ge(e_hT[h], n)
                V.tensor_tensor(hh[h][:, :], ps[:, 4 * h + 1, F:2 * F], sil[h][:, :], ALU.mult).then_inc(e_h[h], 1)

            def h_low(h, n):
                dve.wait_ge(e_hh[h], n)
                V.tensor_tensor(flat(ht[1][h][:, :, :]), ps[:, 4 * h + 2, 0:F], flat(ht[0][h][:, :, :]).bitcast(F32),
                                ALU.subtract).then_inc(e_hl[h], 1)

            ranks = Ranks(dve, rank, 1, U + 1)

            def expert_body(i, first=False, last=False):
                r = ranks.begin(i, first)
                if first:
                    for part in range(2):
                        w_low(0, 0, part)
                    for s in range(2):
                        x_low(0, s, s, s + 1, None)
                        with dve.If(r[U + s] > r[U + s - 1]):
                            x_low(1, s, s, r[U + s], None)
                for s in range(U):
                    e = i * U + s
                    s1 = (s + 1) % U
                    if not (last and s == U - 1):
                        w_low(e + 1, s1, 0)
                    ranks.next(s)
                    hid(0, e + 1)
                    with dve.If(r[U + s] > r[U + s - 1]):
                        hid(1, r[U + s])
                    if not (last and s == U - 1):
                        w_low(e + 1, s1, 1)
                    if not (last and s >= U - 2):
                        s2 = (s + 2) % U
                        some = not (first and s < U - 2)
                        x_low(0, e + 2, s2, e + 3, e + 3 - U if some else None)
                        with dve.If(r[U + s + 2] > r[U + s + 1]):
                            x_low(1, e + 2, s2, r[U + s + 2], r[s + 2] if some else None)
                    h_low(0, e + 1)
                    with dve.If(r[U + s] > r[U + s - 1]):
                        h_low(1, r[U + s])
                if not last:
                    ranks.hand_over()

            expert_body(0, first=True)
            with dve.Fori(1, E // U - 1) as i:
                expert_body(i)
            expert_body(E // U - 1, last=True)


_OUT = ((ROWS, D), "float32")


def kernel(x, src, dst, L0_gnn_W_self, L0_gnn_W_neigh, L0_gnn_bias, L0_gnn_gamma, L0_gnn_beta, L0_ffn_router_w,
           L0_ffn_bias, L0_ffn_shared_w_gate, L0_ffn_shared_w_up, L0_ffn_shared_w_down, L0_ffn_w_gate, L0_ffn_w_up,
           L0_ffn_w_down):
    import numpy as np
    import concourse.bacc as bacc
    from concourse.bass_utils import run_bass_kernel_spmd

    def chunks(a):
        return a.reshape(a.shape[0] // P, P, a.shape[1]).transpose(1, 0, 2)

    def t(a):
        return np.asarray(a).T

    def rows(a):
        a = np.asarray(a)
        return a.reshape(-1, a.shape[-1]).T

    gu = np.concatenate([np.asarray(L0_ffn_w_gate), np.asarray(L0_ffn_w_up)], axis=1)
    gu = gu.transpose(0, 2, 1).reshape(E, DC, P, 2 * F).transpose(0, 2, 1, 3).reshape(E, P, DC * 2 * F)
    dn = np.asarray(L0_ffn_w_down).transpose(0, 2, 1).reshape(E, FC, P, D).transpose(0, 2, 1, 3).reshape(E, P, FC * D)
    sdn = np.asarray(L0_ffn_shared_w_down).transpose(0, 2, 1).reshape(SH * F, D)
    arrays = {
        "x": x, "src": src, "dst": dst,
        "w_self": chunks(t(L0_gnn_W_self)), "w_neigh": chunks(t(L0_gnn_W_neigh)),
        "bias": L0_gnn_bias, "gamma": L0_gnn_gamma, "beta": L0_gnn_beta,
        "router_w": chunks(t(L0_ffn_router_w)), "router_b": L0_ffn_bias,
        "shared_gu": chunks(np.concatenate([rows(L0_ffn_shared_w_gate), rows(L0_ffn_shared_w_up)], axis=1)),
        "shared_down": chunks(sdn),
        "expert_w": np.concatenate([gu, dn], axis=2),
    }
    nc = bacc.Bacc("TRN2", target_bir_lowering=False, num_devices=1)
    args = []
    for name in arrays:
        arrays[name] = np.ascontiguousarray(arrays[name])
        a = arrays[name]
        args.append(nc.dram_tensor(name, a.shape, mybir.dt.from_np(a.dtype), kind="ExternalInput").ap())
    args.append(nc.dram_tensor("out", _OUT[0], F32, kind="ExternalOutput").ap())
    gnn_moe(nc, *args)
    return run_bass_kernel_spmd(nc, [arrays], core_ids=[0]).results[0]["out"][:N]
```
